# Optimizing a Trainium2 kernel written in Bass

```python
import numpy as np
import jax
import jax.numpy as jnp

def _softmax(x, axis=-1):
    return jax.nn.softmax(x, axis=axis)

def _gelu(x):
    return jax.nn.gelu(x, approximate=True)

def _silu(x):
    return jax.nn.silu(x)

def _sigmoid(x):
    return jax.nn.sigmoid(x)

def _layernorm(x, axis=-1, eps=1e-05):
    m = jnp.mean(x, axis=axis, keepdims=True)
    v = jnp.var(x, axis=axis, keepdims=True)
    return (x - m) / jnp.sqrt(v + eps)

def _scatter_add(tgt, idx, src, axis=0):
    return tgt.at[idx].add(src)

def _segment_sum(src, seg, n):
    return jax.ops.segment_sum(src, seg, n)
kernel_name = 'mk_early_fusion_embed_d1_tok_img256_r4_931b13'

def setup_inputs(seed: int=0):
    np.random.seed(seed)
    _w = jnp.asarray

    def _rec_inputs():
        import jax
        import jax.numpy as jnp
        _rk = jax.random.key(seed)
        x = -0.0003702 + 0.999946 * jax.random.normal(jax.random.fold_in(_rk, 1), (64, 1, 84, 84), jnp.float32)
        x_txt = jax.random.randint(jax.random.fold_in(_rk, 51), (64, 128), 0, 2048, jnp.int32)
        return (x, x_txt)
    x, x_txt = _rec_inputs()

    def _L0_tok_setup():
        import jax, jax.numpy as jnp
        import numpy as np
        PH, PW = (64, 25)
        SH, SW = (64, 12)

        def _unfold(x, ph, pw, sh, sw):
            B, C, H, W = x.shape
            nh = (H - ph) // sh + 1
            nw = (W - pw) // sw + 1
            rows = jnp.arange(nh)[:, None] * sh + jnp.arange(ph)[None, :]
            cols = jnp.arange(nw)[:, None] * sw + jnp.arange(pw)[None, :]
            p = x[:, :, rows, :]
            p = p[:, :, :, :, cols]
            p = jnp.transpose(p, (0, 2, 4, 1, 3, 5))
            return p.reshape(B, nh * nw, C * ph * pw)
        key = jax.random.key(seed)
        kx, kw = jax.random.split(key, 2)
        x = jax.random.normal(kx, (64, 1, 64, 1000), dtype=jnp.float32)
        in_dim = 1 * PH * PW
        weight = jax.random.normal(kw, (in_dim, 64), dtype=jnp.float32) / np.sqrt(in_dim).astype(np.float32)
        bias = jnp.zeros((64,), dtype=jnp.float32)
        return {'x': x, 'weight': weight, 'bias': bias}
    _L0_tok_all = _L0_tok_setup()
    _L0_tok_in = {k: v for k, v in _L0_tok_all.items() if k in ('weight', 'bias')}
    del _L0_tok_all

    def _L0_txt_setup():
        import jax, jax.numpy as jnp
        import numpy as np
        D = 64
        NLEAF = 8
        N_INTERNAL = 7
        N_STRUCT = 2048
        COMP_V = 256
        OP_V = 64
        EPS = 1e-05

        def _layer_norm(x, gamma, beta):
            mu = jnp.mean(x, axis=-1, keepdims=True)
            var = jnp.mean(jnp.square(x - mu), axis=-1, keepdims=True)
            return (x - mu) * jax.lax.rsqrt(var + EPS) * gamma + beta
        key = jax.random.key(seed)
        ks = jax.random.split(key, 8)
        struct_indices = jax.random.randint(ks[0], (32, 512), 0, N_STRUCT)
        leaf_ids = jax.random.randint(ks[1], (N_STRUCT, NLEAF), 0, COMP_V).astype(jnp.int32)
        op_ids = jax.random.randint(ks[2], (N_STRUCT, N_INTERNAL), 0, OP_V).astype(jnp.int32)
        comp_emb = jax.random.normal(ks[3], (COMP_V, D), dtype=jnp.float32)
        op_emb = jax.random.normal(ks[4], (OP_V, D), dtype=jnp.float32)
        W_bin = jax.random.normal(ks[5], (3 * D, D), dtype=jnp.float32) / np.sqrt(3 * D)
        b_bin = jnp.zeros((D,), dtype=jnp.float32)
        gamma = jnp.ones((D,), dtype=jnp.float32)
        beta = jnp.zeros((D,), dtype=jnp.float32)
        return {'struct_indices': struct_indices, 'leaf_ids': leaf_ids, 'op_ids': op_ids, 'comp_emb': comp_emb, 'op_emb': op_emb, 'W_bin': W_bin, 'b_bin': b_bin, 'gamma': gamma, 'beta': beta}
    _L0_txt_all = _L0_txt_setup()
    _L0_txt_in = {k: v for k, v in _L0_txt_all.items() if k in ('leaf_ids', 'op_ids', 'comp_emb', 'op_emb', 'W_bin', 'b_bin', 'gamma', 'beta')}
    del _L0_txt_all

    def _L0_attn_setup():
        import jax, jax.numpy as jnp
        import numpy as np
        B, N, C, H = (4, 256, 64, 8)
        HD = C // H
        BN_EPS = 1e-05
        key = jax.random.key(seed)
        ks = jax.random.split(key, 6)

        def w(k, shape, sc=0.02):
            return jax.random.normal(k, shape, jnp.float32) * sc
        return {'x': jax.random.normal(ks[0], (B, N, C), jnp.float32), 'w_qkv': w(ks[1], (3 * C, C)), 'b_qkv': jnp.zeros((3 * C,), jnp.float32), 'w_proj': w(ks[2], (C, C)), 'b_proj': jnp.zeros((C,), jnp.float32), 'scale': jnp.float32(HD ** (-0.5)), 'riem_scale': jnp.float32(HD ** (-0.5)), 'grassman_scale': jnp.float32(HD ** (-0.5)), 'bn_gamma': jnp.ones((3 * H,), jnp.float32), 'bn_beta': jnp.zeros((3 * H,), jnp.float32), 'bn_mean': jnp.zeros((3 * H,), jnp.float32), 'bn_var': jnp.ones((3 * H,), jnp.float32), 'conv_w': w(ks[3], (H, 3 * H)), 'conv_b': jnp.zeros((H,), jnp.float32)}
    _L0_attn_all = _L0_attn_setup()
    _L0_attn_in = {k: v for k, v in _L0_attn_all.items() if k in ('w_qkv', 'b_qkv', 'w_proj', 'b_proj', 'scale', 'riem_scale', 'grassman_scale', 'bn_gamma', 'bn_beta', 'bn_mean', 'bn_var', 'conv_w', 'conv_b')}
    del _L0_attn_all

    def _L0_ffn_setup():
        import jax, jax.numpy as jnp
        import numpy as np
        B, S, D, F, E, K = (8, 512, 64, 256, 8, 2)
        key = jax.random.key(seed)
        ks = jax.random.split(key, 10)
        s = 0.02
        return {'x': jax.random.normal(ks[0], (B, S, D), dtype=jnp.float32), 'Wr': jax.random.normal(ks[1], (D, E), dtype=jnp.float32) * s, 'W1s': jax.random.normal(ks[2], (D, F), dtype=jnp.float32) * s, 'b1s': jnp.zeros((F,), dtype=jnp.float32), 'W2s': jax.random.normal(ks[3], (F, D), dtype=jnp.float32) * s, 'b2s': jnp.zeros((D,), dtype=jnp.float32), 'W1p': jax.random.normal(ks[4], (E, D, F), dtype=jnp.float32) * s, 'b1p': jnp.zeros((E, F), dtype=jnp.float32), 'W2p': jax.random.normal(ks[5], (E, F, D), dtype=jnp.float32) * s, 'b2p': jnp.zeros((E, D), dtype=jnp.float32)}
    _L0_ffn_all = _L0_ffn_setup()
    _L0_ffn_in = {k: v for k, v in _L0_ffn_all.items() if k in ('Wr', 'W1s', 'b1s', 'W2s', 'b2s', 'W1p', 'b1p', 'W2p', 'b2p')}
    del _L0_ffn_all
    return {'x': x, 'x_txt': x_txt, 'L0_tok_weight': _L0_tok_in['weight'], 'L0_tok_bias': _L0_tok_in['bias'], 'L0_txt_leaf_ids': _L0_txt_in['leaf_ids'], 'L0_txt_op_ids': _L0_txt_in['op_ids'], 'L0_txt_comp_emb': _L0_txt_in['comp_emb'], 'L0_txt_op_emb': _L0_txt_in['op_emb'], 'L0_txt_W_bin': _L0_txt_in['W_bin'], 'L0_txt_b_bin': _L0_txt_in['b_bin'], 'L0_txt_gamma': _L0_txt_in['gamma'], 'L0_txt_beta': _L0_txt_in['beta'], 'L0_attn_w_qkv': _L0_attn_in['w_qkv'], 'L0_attn_b_qkv': _L0_attn_in['b_qkv'], 'L0_attn_w_proj': _L0_attn_in['w_proj'], 'L0_attn_b_proj': _L0_attn_in['b_proj'], 'L0_attn_scale': _L0_attn_in['scale'], 'L0_attn_riem_scale': _L0_attn_in['riem_scale'], 'L0_attn_grassman_scale': _L0_attn_in['grassman_scale'], 'L0_attn_bn_gamma': _L0_attn_in['bn_gamma'], 'L0_attn_bn_beta': _L0_attn_in['bn_beta'], 'L0_attn_bn_mean': _L0_attn_in['bn_mean'], 'L0_attn_bn_var': _L0_attn_in['bn_var'], 'L0_attn_conv_w': _L0_attn_in['conv_w'], 'L0_attn_conv_b': _L0_attn_in['conv_b'], 'L0_ffn_Wr': _L0_ffn_in['Wr'], 'L0_ffn_W1s': _L0_ffn_in['W1s'], 'L0_ffn_b1s': _L0_ffn_in['b1s'], 'L0_ffn_W2s': _L0_ffn_in['W2s'], 'L0_ffn_b2s': _L0_ffn_in['b2s'], 'L0_ffn_W1p': _L0_ffn_in['W1p'], 'L0_ffn_b1p': _L0_ffn_in['b1p'], 'L0_ffn_W2p': _L0_ffn_in['W2p'], 'L0_ffn_b2p': _L0_ffn_in['b2p']}

def reference(x, x_txt, L0_tok_weight, L0_tok_bias, L0_txt_leaf_ids, L0_txt_op_ids, L0_txt_comp_emb, L0_txt_op_emb, L0_txt_W_bin, L0_txt_b_bin, L0_txt_gamma, L0_txt_beta, L0_attn_w_qkv, L0_attn_b_qkv, L0_attn_w_proj, L0_attn_b_proj, L0_attn_scale, L0_attn_riem_scale, L0_attn_grassman_scale, L0_attn_bn_gamma, L0_attn_bn_beta, L0_attn_bn_mean, L0_attn_bn_var, L0_attn_conv_w, L0_attn_conv_b, L0_ffn_Wr, L0_ffn_W1s, L0_ffn_b1s, L0_ffn_W2s, L0_ffn_b2s, L0_ffn_W1p, L0_ffn_b1p, L0_ffn_W2p, L0_ffn_b2p):
    import jax
    import jax.numpy as jnp

    def _L0_tok_ref(x, weight, bias):
        import jax, jax.numpy as jnp
        import numpy as np
        PH, PW = (64, 25)
        SH, SW = (64, 12)

        def _unfold(x, ph, pw, sh, sw):
            B, C, H, W = x.shape
            nh = (H - ph) // sh + 1
            nw = (W - pw) // sw + 1
            rows = jnp.arange(nh)[:, None] * sh + jnp.arange(ph)[None, :]
            cols = jnp.arange(nw)[:, None] * sw + jnp.arange(pw)[None, :]
            p = x[:, :, rows, :]
            p = p[:, :, :, :, cols]
            p = jnp.transpose(p, (0, 2, 4, 1, 3, 5))
            return p.reshape(B, nh * nw, C * ph * pw)
        p = _unfold(x, PH, PW, SH, SW)
        return jax.nn.gelu(jnp.einsum('bnk,kd->bnd', p, weight) + bias, approximate=False)

    def _L0_txt_ref(struct_indices, leaf_ids, op_ids, comp_emb, op_emb, W_bin, b_bin, gamma, beta):
        import jax, jax.numpy as jnp
        import numpy as np
        D = 64
        NLEAF = 8
        N_INTERNAL = 7
        N_STRUCT = 2048
        COMP_V = 256
        OP_V = 64
        EPS = 1e-05

        def _layer_norm(x, gamma, beta):
            mu = jnp.mean(x, axis=-1, keepdims=True)
            var = jnp.mean(jnp.square(x - mu), axis=-1, keepdims=True)
            return (x - mu) * jax.lax.rsqrt(var + EPS) * gamma + beta
        h = _layer_norm(comp_emb[leaf_ids], gamma, beta)
        off = 0
        while h.shape[1] > 1:
            n = h.shape[1] // 2
            ops = op_emb[op_ids[:, off:off + n]]
            cat = jnp.concatenate([ops, h[:, 0::2], h[:, 1::2]], axis=-1)
            h = _layer_norm(jnp.einsum('nkc,cd->nkd', cat, W_bin) + b_bin, gamma, beta)
            off += n
        root = h[:, 0]
        out = root[struct_indices]
        mask = (struct_indices > 1)[..., None]
        return jnp.where(mask, out, jnp.zeros((), dtype=out.dtype))

    def _L0_attn_ref(x, w_qkv, b_qkv, w_proj, b_proj, scale, riem_scale, grassman_scale, bn_gamma, bn_beta, bn_mean, bn_var, conv_w, conv_b):
        import jax, jax.numpy as jnp
        import numpy as np
        B, N, C, H = (4, 256, 64, 8)
        HD = C // H
        BN_EPS = 1e-05
        b, n, c = x.shape
        h, hd = (H, c // H)
        qkv = (x @ w_qkv.T + b_qkv).reshape(b, n, 3, h, hd).transpose(2, 0, 3, 1, 4)
        q, k, v = (qkv[0], qkv[1], qkv[2])
        qgr, _ = jnp.linalg.qr(q)
        kgr, _ = jnp.linalg.qr(k)
        attn_grass = jnp.einsum('bhnd,bhmd->bhnm', qgr, kgr) ** 2 * grassman_scale
        dots = jnp.einsum('bhnd,bhmd->bhnm', q, k)
        attn_eucl = dots * scale
        attn_riem = dots ** 2 * riem_scale
        a = jnp.concatenate([attn_eucl, attn_riem, attn_grass], axis=1)
        inv = (bn_gamma * jax.lax.rsqrt(bn_var + BN_EPS))[:, None, None]
        a = (a - bn_mean[:, None, None]) * inv + bn_beta[:, None, None]
        a = jnp.einsum('oc,bcnm->bonm', conv_w, a) + conv_b[None, :, None, None]
        a = jax.nn.softmax(a, axis=-1)
        out = jnp.einsum('bhnm,bhmd->bhnd', a, v)
        out = out.transpose(0, 2, 1, 3).reshape(b, n, c)
        return out @ w_proj.T + b_proj

    def _L0_ffn_ref(x, Wr, W1s, b1s, W2s, b2s, W1p, b1p, W2p, b2p):
        import jax, jax.numpy as jnp
        import numpy as np
        B, S, D, F, E, K = (8, 512, 64, 256, 8, 2)
        gelu = lambda t: jax.nn.gelu(t, approximate=False)
        shared = gelu(x @ W1s + b1s) @ W2s + b2s
        rw = jax.nn.softmax(x @ Wr, axis=-1)
        topw, topi = jax.lax.top_k(rw, K)
        topw = topw / jnp.sum(topw, axis=-1, keepdims=True)
        mask = jnp.sum(jax.nn.one_hot(topi, E, dtype=topw.dtype) * topw[..., None], axis=-2)
        h = gelu(jnp.einsum('bsd,edf->bsef', x, W1p) + b1p)
        priv = jnp.einsum('bsef,efd->bsed', h, W2p) + b2p
        routed = jnp.einsum('bsed,bse->bsd', priv, mask)
        return shared + routed
    h = _L0_tok_ref(x, L0_tok_weight, L0_tok_bias)
    h = jnp.concatenate([h, _L0_txt_ref(x_txt, L0_txt_leaf_ids, L0_txt_op_ids, L0_txt_comp_emb, L0_txt_op_emb, L0_txt_W_bin, L0_txt_b_bin, L0_txt_gamma, L0_txt_beta)], axis=1)
    h = h + _L0_attn_ref(_layernorm(h, axis=-1), L0_attn_w_qkv, L0_attn_b_qkv, L0_attn_w_proj, L0_attn_b_proj, L0_attn_scale, L0_attn_riem_scale, L0_attn_grassman_scale, L0_attn_bn_gamma, L0_attn_bn_beta, L0_attn_bn_mean, L0_attn_bn_var, L0_attn_conv_w, L0_attn_conv_b)
    h = h + _L0_ffn_ref(_layernorm(h, axis=-1), L0_ffn_Wr, L0_ffn_W1s, L0_ffn_b1s, L0_ffn_W2s, L0_ffn_b2s, L0_ffn_W1p, L0_ffn_b1p, L0_ffn_W2p, L0_ffn_b2p)
    return h

_drawn_inputs = setup_inputs


def setup_inputs(seed=0):
    import zlib

    import numpy as np

    out = dict(_drawn_inputs(seed))
    spreads = {'L0_tok_bias': (0.0, 0.576),
     'L0_txt_b_bin': (0.0, 0.1),
     'L0_txt_gamma': (1.0, 0.2),
     'L0_txt_beta': (0.0, 0.1),
     'L0_attn_b_qkv': (0.0, 0.367),
     'L0_attn_b_proj': (0.0, 0.1),
     'L0_attn_bn_gamma': (1.0, 0.6),
     'L0_attn_bn_beta': (0.0, 0.8),
     'L0_attn_bn_mean': (0.0, 0.8),
     'L0_attn_bn_var': (1.0, 0.6),
     'L0_attn_conv_b': (0.0, 0.8),
     'L0_ffn_b1s': (0.0, 0.479),
     'L0_ffn_b2s': (0.0, 0.1),
     'L0_ffn_b1p': (0.0, 0.676),
     'L0_ffn_b2p': (0.0, 0.1)}
    factors = {'L0_attn_w_qkv': 8.0, 'L0_attn_conv_w': 8.0, 'L0_ffn_W1p': 3.076}
    for name, (base, spread) in spreads.items():
        noise = np.random.default_rng([zlib.crc32(name.encode()), seed]).standard_normal(out[name].shape)
        drawn = base * np.exp(spread * noise) if base else spread * noise
        out[name] = jnp.asarray(drawn.astype(out[name].dtype))
    for name, factor in factors.items():
        out[name] = (out[name] * factor).astype(out[name].dtype)
    return out
```

```python
from contextlib import ExitStack

import concourse.bass as bass
from concourse import mybir

F32 = mybir.dt.float32
BF16 = mybir.dt.bfloat16
I32 = mybir.dt.int32
ACT = mybir.ActivationFunctionType
ALU = mybir.AluOpType
AX = mybir.AxisListType

P = 128
D = 64
B = 64
PAIRS = B // 2
TXT, TOK = 128, 5
N = TXT + TOK
NP = 136
H, HD = 8, 8
QB = HD
G = 2 * H
TILES = NP // 8
GROUPS = [range(j, min(j + 3, TILES)) for j in range(0, TILES, 3)]
NG = len(GROUPS)
PH, PW, SW, PX = 64, 25, 12, 84
STRUCTS, LEAVES, INNER = 2048, 8, 7
OPS, VOCAB = 64, 256
ST = STRUCTS // P
TS = ST // 2
LEAFC, OPC = LEAVES * P, INNER * P
EXPERTS, FF = 8, 256
CH = (EXPERTS + 1) * FF // P
EPS = 1e-5
MASKED = -1.0e30
HG = 4


def need(eng, sem, value):
    if isinstance(value, int) and value <= 0:
        return
    eng.wait_ge(sem, value)


def within(t, lo, hi):
    return not isinstance(t, int) or lo <= t < hi


def slots(eng, first, lo, hi, last, step, body):
    for t in range(first, lo):
        body(t, t % step)
    assert (hi - lo) % step == 0
    with eng.Fori(0, (hi - lo) // step) as i:
        for u in range(step):
            body(step * i + (lo + u), (lo + u) % step)
    for t in range(hi, last):
        body(t, t % step)


class Chain:

    def __init__(self, eng, sem):
        self.eng, self.sem, self.count = eng, sem, 0

    def step(self, ins):
        ins.then_inc(self.sem, 1)
        self.count += 1
        self.eng.wait_ge(self.sem, self.count)


def build(nc, a, out):
    ctx = ExitStack()
    with ctx:
        ctx.enter_context(nc.allow_non_contiguous_dma(reason="strided loads of weights and indices"))

        def sb(name, shape, dt=F32):
            return ctx.enter_context(nc.sbuf_tensor(name, shape, dt))

        def sem(name):
            return ctx.enter_context(nc.semaphore(name))

        bank = [ctx.enter_context(nc.psum_tensor(f"bank{i}", [P, 512], F32)) for i in range(8)]
        root_dram = nc.dram_tensor("root_table", [STRUCTS, D], F32, kind="Internal").ap()

        ident = sb("ident", [P, P])
        ident2 = sb("ident2", [P, D])
        group_of = sb("group_of", [P, G])
        head_of = sb("head_of", [P, H])
        lane_of = sb("lane_of", [P, 8])
        group_ones = sb("group_ones", [P, P])
        ones_row = sb("ones_row", [1, P])
        ones_col = sb("ones_col", [P, 1])
        ones16 = sb("ones16", [ST, P], BF16)
        iota_col = sb("iota_col", [P, 2])
        eps_col = sb("eps_col", [P, 1])
        minus_half = sb("minus_half", [P, 4])

        h_txt = sb("h_txt", [P, B, D])
        h_tok = sb("h_tok", [2 * TOK, PAIRS, D])
        hn_t = sb("hn_t", [P, PAIRS, N])

        wn = sb("wn", [D, 4, 2, D])
        wq_dup = sb("wq_dup", [P, 2, P])
        wk_dup = sb("wk_dup", [P, 2, P])
        wv_pair = sb("wv_pair", [P, P])
        wqk_pair = sb("wqk_pair", [P, 2, P])
        wqk_top = sb("wqk_top", [P, 2, D])
        wp_pair = sb("wp_pair", [P, P])
        wp_both = sb("wp_both", [P, D])
        wr_both = sb("wr_both", [P, EXPERTS])
        wr_pair = sb("wr_pair", [P, 2, EXPERTS])
        b_qkv = sb("b_qkv", [P, 3])
        b_qk_rows = sb("b_qk_rows", [P, P])
        b_top = sb("b_top", [P, D])
        bp_row = sb("bp_row", [1, 2, D])
        w1_split = sb("w1_split", [P, 3, EXPERTS + 1, FF], BF16)
        w2_s = sb("w2_s", [P, EXPERTS + 1, 2, D])
        b1_col = sb("b1_col", [P, EXPERTS + 1, 2])
        b2_rows = sb("b2_rows", [D, D])
        b2_split = sb("b2_split", [D, 3, D], BF16)
        b2s_col = sb("b2s_col", [P, 1])
        sel_e = sb("sel_e", [D, EXPERTS, P], BF16)
        conv_t = sb("conv_t", [3 * H, H])
        bn = sb("bn", [3 * H, 4])
        score_scale = sb("score_scale", [3 * H, 1])
        bn_inv = sb("bn_inv", [3 * H, 4])
        conv_a = sb("conv_a", [3 * H, H])
        pick_sq = sb("pick_sq", [3 * H, P])
        pick_lin = sb("pick_lin", [3 * H, D])
        conv_x = sb("conv_x", [3 * H, P])
        cb_row = sb("cb_row", [1, H])
        cb_x = sb("cb_x", [1, P])
        mix = sb("mix", [P, D])
        lin_a = sb("lin_a", [D, H])
        score_c = sb("score_c", [P, 2])
        bases = sb("bases", [P, PAIRS, 2, HD])
        router = sb("router", [P, B, EXPERTS])
        router_tok = sb("router_tok", [2 * TOK, PAIRS, EXPERTS])
        earlier = sb("earlier", [P, EXPERTS, EXPERTS])

        ARENA = 31500
        arena = sb("arena", [P, ARENA])

        def carver():
            at = [0]

            def carve(shape, dt=F32, parts=P):
                n = 1
                for s in shape:
                    n *= s
                words = n if dt != BF16 else (n + 1) // 2
                v = arena[0:parts, at[0]:at[0] + words]
                at[0] += words
                assert at[0] <= ARENA, at[0]
                if dt != F32:
                    v = v.bitcast(dt)
                names = "abcde"[:len(shape)]
                if len(shape) > 1:
                    v = v.rearrange(f"p ({' '.join(names)}) -> p {' '.join(names)}",
                                    **dict(zip(names, shape)))
                return v
            carve.used = at
            return carve

        one = carver()
        ids_raw = one([LEAFC + OPC], I32, ST)
        ids_all = one([LEAFC + OPC], BF16, ST)
        ids_one = one([LEAFC + OPC], BF16, ST)
        ids_bc = one([LEAFC + OPC], BF16)
        leaf_hot = one([2, 2, LEAFC], BF16)
        op_hot = one([2, 4 * P], BF16, OPS)
        up_hot = one([8, 3 * P], BF16)
        comp = one([2, D])
        comp_sq = one([2, D])
        comp_d = one([2, 2, D])
        comp_st = one([4, 2])
        comp_t = one([2, P])
        gamma_bc = one([D])
        beta_bc = one([D])
        op_raw = one([D], F32, OPS)
        op_t = one([OPS], F32, D)
        w_op = one([D], F32, D)
        w_lr = one([D])
        w_mean = one([4])
        bc_row = one([D], F32, 1)
        tab = one([2, 2, 3, D], BF16)
        tab_op = one([3, D], BF16)
        tab_f = one([5, D])
        tab_r = one([5, D])
        lv_sq = [one([8, D]), one([4, D]), one([2, D])]
        lv_var = [one([8]), one([4]), one([2])]
        lv_std = [one([8]), one([4]), one([2])]
        lv_inv = [one([8]), one([4]), one([2])]
        lv_h = [one([8, D]), one([4, D]), one([2, D])]
        lv_g = [one([8, D]), one([4, D]), one([2, D])]
        kids1 = one([4, P])
        kids2 = one([2, P])
        one.at_txt = one.used[0]
        txt_idx = one([B], I32)
        xs = one([B, PX])
        wt = one([(PW + 1) // 2, D])
        btok = one([1])
        tok_t = one([PAIRS, TOK])
        tok_m = one([PAIRS, 2, TOK])
        ln_s = one([B])
        ln_m = one([B])
        ln_v = one([B])
        ln_d = one([B])
        ln_r = one([B])
        hn_txt = one([B, D])
        hn_tok = one([PAIRS, D], F32, 2 * TOK)
        ln_sq = xs.rearrange("p a b -> p (a b)")[:, 0:B * D].rearrange("p (a b) -> p a b", a=B)
        st_txt = [one([2, D]) for _ in range(2)]
        st_tok = [one([2, D], F32, 2 * TOK) for _ in range(2)]
        hs = [one([NP]) for _ in range(2)]
        qkn = [one([2, P]) for _ in range(2)]
        qkt = [one([2, P], F32, TOK) for _ in range(2)]
        gm = [one([2, G, HD]) for _ in range(2)]
        b2_r = one([D], F32, D)
        w1_f = hn_txt.rearrange("p a b -> p (a b)")[:, 0:(EXPERTS + 1) * FF].rearrange("p (e f) -> p e f", f=FF)
        w1_r = carver()([EXPERTS + 1, FF])

        qr = carver()
        gall = qr([HD, 2, 2, PAIRS])
        top = qr([2, HD, 2, 2, PAIRS])
        ym = qr([H, 3 * HD, HD])
        yt = qr([H * 3 * HD * (HD - 1)])
        qsd = qr([H])
        qri = qr([H])
        um = qr([H, HD, HD])
        sg = qr([H, HD])
        piv = qr([H])
        pinv = qr([H])
        ucol = qr([H, HD])
        mx = qr([HD, 2, H, HD])
        assert qr.used[0] < one.at_txt

        two = carver()
        kbd = [two([2, G, NP]) for _ in range(2)]
        vbt = two([G, NP])
        vbd = [two([TILES, P]) for _ in range(2)]
        linb = [two([2, H, NP]) for _ in range(2)]
        qq = [two([2, N]) for _ in range(2)]
        kk = [two([2, NP]) for _ in range(2)]
        vv = [two([NP]) for _ in range(2)]
        pm = [two([2, D]) for _ in range(2)]
        mqx = [two([2, 2, H, HD]) for _ in range(2)]
        mkx = [two([H, HD]) for _ in range(2)]
        sq = [[two([3 * N]) for _ in range(2)] for _ in range(2)]
        ll = [two([TILES, N]) for _ in range(2)]
        mxv = two([N])
        mn = two([G])
        mn5 = two([G], F32, TOK)
        mnx = two([G, 8])
        mnx5 = two([G, 8], F32, TOK)
        es = two([N])
        rec = two([N])
        ot = two([N])
        ot5 = two([2, TOK])
        gate = two([2])
        st6 = two([3, 6])
        mv = two([3, 2])
        ve = two([3])
        rs = two([3])
        hn2 = two([2, D])
        hn2k = two([2, D], F32, 2 * TOK)
        hs2 = [two([N]) for _ in range(2)]
        tk10 = [two([2, TOK]) for _ in range(2)]

        three = carver()
        rt_m = three([B])
        rt_w = three([B, EXPERTS])
        rt_gt = three([B, EXPERTS, EXPERTS])
        rt_eq = three([B, EXPERTS, EXPERTS])
        rt_rank = three([B, EXPERTS])
        rt_16 = three([B, EXPERTS], BF16)
        wsp = three([B, 4, EXPERTS])
        wsp_tok = three([PAIRS, 4, EXPERTS], F32, 2 * TOK)
        st_w = [three([2, D]) for _ in range(2)]
        st_wk = [three([2, 4 * EXPERTS], F32, 2 * TOK) for _ in range(2)]
        mt = [three([2, N], BF16, D) for _ in range(2)]
        dup = three([2, P])
        x12 = [three([2 * N], BF16) for _ in range(2)]
        x13 = [three([2 * N], BF16) for _ in range(2)]
        x_r = three([2 * N])
        hg = [three([2, 2 * N]) for _ in range(HG)]
        yt_sb = three([N])
        yk = three([2, TOK])
        yo = [three([D]) for _ in range(3)]

        E = {}

        def ev(name):
            if name not in E:
                E[name] = sem(name)
            return E[name]

        LV = [bank[4][:, :].rearrange("p (n d) -> p n d", d=D),
              bank[6][:, 0:256].rearrange("p (n d) -> p n d", d=D),
              bank[7][:, 0:P].rearrange("p (n d) -> p n d", d=D)]

        def ln_slice(g):
            if g == 0:
                r, c, h, hn = slice(0, 2 * TOK), slice(0, PAIRS), h_tok[:, :, :], hn_tok
            else:
                r, c = slice(0, P), slice(16 * (g - 1), 16 * g)
                h, hn = h_txt[:, c, :], hn_txt[:, c, :]
            parts, n = r.stop, c.stop - c.start
            return dict(parts=parts, shape=[parts, n, D], h=h, hn=hn, sq=ln_sq[r, c, :],
                        **{k: v[r, c] for k, v in dict(s=ln_s, m=ln_m, v=ln_v, d=ln_d, r=ln_r).items()})

        def ROUTES():
            return [(router[:, :, :], rt_w), (router_tok[:, :, :], rt_w[0:2 * TOK, 0:PAIRS])]

        def weights(dve, ch):
            nc.vector.tensor_reduce(lane_of[:, :], ident[:, :].rearrange("p (g k) -> p k g", g=G), AX.X, ALU.add)
            ch.step(nc.vector.tensor_reduce(group_of[:, :], ident[:, :].rearrange("p (g k) -> p g k", g=G), AX.X, ALU.add))
            nc.vector.tensor_tensor(head_of[:, :], group_of[:, 0:H], group_of[:, H:G], ALU.add)
            nc.vector.tensor_copy(group_ones[:, :].rearrange("p (g k) -> p g k", g=G),
                                  group_of[:, :].unsqueeze(2).to_broadcast([P, G, 8]))
            dve.wait_ge(ev("w_turned"), 1)
            turned = [bank[5][:, i * D:i * D + D] for i in range(4)]
            for b in range(2):
                half, cols = slice(b * D, b * D + D), slice(b * D, b * D + D)
                for c in range(2):
                    nc.vector.tensor_copy(wq_dup[half, b, c * D:c * D + D], turned[0][half])
                    nc.vector.tensor_copy(wk_dup[half, b, c * D:c * D + D], turned[1][half])
                    nc.vector.tensor_copy(wqk_pair[half, b, c * D:c * D + D], turned[c][half])
                nc.vector.tensor_copy(wv_pair[half, cols], turned[2][half])
                nc.vector.tensor_copy(wp_pair[half, cols], turned[3][half])
                nc.vector.tensor_copy(wqk_top[:, b, :], turned[b])
                nc.vector.tensor_copy(wr_pair[half, b, :], wr_both[half, :])
            nc.vector.tensor_copy(wp_both[:, :], turned[3])
            nc.vector.tensor_copy(conv_x[:, :].rearrange("c (b o k) -> c b o k", b=2, o=H),
                                  conv_t[:, :].unsqueeze(1).unsqueeze(3).to_broadcast([3 * H, 2, H, 8]))
            nc.vector.tensor_copy(cb_x[:, :].rearrange("c (b o k) -> c b o k", b=2, o=H),
                                  cb_row[:, :].unsqueeze(1).unsqueeze(3).to_broadcast([1, 2, H, 8]))
            ch.step(nc.vector.tensor_copy(w1_split[:, 0], w1_f))
            ch.step(nc.vector.tensor_tensor(w1_r, w1_f, w1_split[:, 0], ALU.subtract))
            ch.step(nc.vector.tensor_copy(w1_split[:, 1], w1_r))
            nc.vector.tensor_tensor(w1_split[0:D, 2], w1_r[0:D], w1_split[0:D, 1], ALU.subtract)
            nc.vector.tensor_copy(w1_split[D:P, 2], w1_split[D:P, 0])
            ch.step(nc.vector.tensor_copy(b2_split[:, 0], b2_rows[:, :]))
            ch.step(nc.vector.tensor_tensor(b2_r, b2_rows[:, :], b2_split[:, 0], ALU.subtract))
            ch.step(nc.vector.tensor_copy(b2_split[:, 1], b2_r))
            nc.vector.tensor_tensor(b2_split[:, 2], b2_r, b2_split[:, 1], ALU.subtract)
            nc.vector.tensor_copy(sel_e[:, :, :], lane_of[0:D, :].unsqueeze(2).to_broadcast([D, EXPERTS, P]))
            dve.wait_ge(ev("bn_std"), 1)
            ch.step(nc.vector.reciprocal(bn_inv[:, 1:2], bn_inv[:, 0:1]))
            ch.step(nc.vector.tensor_tensor(bn_inv[:, 2:3], bn_inv[:, 1:2], bn[:, 0:1], ALU.mult))
            nc.vector.tensor_scalar(conv_a[:, :], conv_t[:, :], bn_inv[:, 2:3], score_scale[:, :], ALU.mult, ALU.mult)
            ch.step(nc.vector.tensor_tensor(bn_inv[:, 3:4], bn[:, 2:3], bn_inv[:, 2:3], ALU.mult))
            nc.vector.tensor_tensor(bn_inv[:, 3:4], bn[:, 1:2], bn_inv[:, 3:4], ALU.subtract).then_inc(ev("conv_ready"), 1)
            dve.wait_ge(ev("conv_mm"), 1)
            nc.vector.tensor_copy(lin_a[:, :], bank[6][0:D, 8:16])
            ch.step(nc.vector.tensor_copy(score_c[:, 0:1], bank[6][:, 16:17]))
            nc.vector.tensor_tensor(mix[:, :].rearrange("p (o k) -> p o k", o=H),
                                    bank[6][:, 0:H].unsqueeze(2).to_broadcast([P, H, 8]),
                                    lane_of[:, :].unsqueeze(1).to_broadcast([P, H, 8]), ALU.mult)
            nc.vector.scalar_tensor_tensor(score_c[:, 1:2], lane_of[:, 7:8], MASKED, score_c[:, 0:1], ALU.mult,
                                           ALU.add).then_inc(ev("weights_ready"), 1)

        def factorise(dve):
            cs = ev("qr_chain")
            n = [0]

            def step(ins):
                ins.then_inc(cs, 1)
                n[0] += 1
                dve.wait_ge(cs, n[0])
            nc.vector.memset(ym[:, :, 2 * HD:3 * HD, :], 0.0).then_inc(cs, 1)
            n[0] += 1
            dve.wait_ge(cs, 1)
            nc.vector.memset(ym.rearrange("p h r c -> p h (r c)")[:, :, 2 * HD * HD::HD + 1], 1.0)
            dve.wait_ge(ev("qr_mm"), 1)
            nc.vector.tensor_copy(ym[:, :, 0:HD, :], bank[0][:, :].rearrange("p (c h r) -> p h r c", c=HD, h=H))
            last = nc.vector.tensor_tensor(
                ym[:, :, HD:2 * HD, :], bank[1][:, :].rearrange("p (t h c) -> p h t c", t=QB, h=H),
                b_top[:, :].rearrange("p (h c) -> p h c", h=H).unsqueeze(2).to_broadcast([P, H, QB, HD]), ALU.add)
            for c in range(QB):
                last.then_inc(ev("pivot"), 1)
                dve.wait_ge(ev("pivot"), c + 1)
                dve.wait_ge(ev("pivot_root"), c + 1)
                step(nc.vector.reciprocal(qri, qsd))
                step(nc.vector.tensor_tensor(ym[:, :, :, c], ym[:, :, :, c],
                                             qri.unsqueeze(2).to_broadcast([P, H, 3 * HD]), ALU.mult))
                rest = HD - 1 - c
                if not rest:
                    break
                tmp = yt[:, 0:H * 3 * HD * rest].rearrange("p (h r k) -> p h r k", h=H, r=3 * HD)
                shape = [P, H, 3 * HD, rest]
                step(nc.vector.tensor_tensor(tmp, ym[:, :, :, c].unsqueeze(3).to_broadcast(shape),
                                             ym[:, :, c + 1:HD, c].unsqueeze(2).to_broadcast(shape), ALU.mult))
                last = nc.vector.tensor_tensor(ym[:, :, :, c + 1:], ym[:, :, :, c + 1:], tmp, ALU.subtract)
            step(nc.vector.tensor_copy(um, ym[:, :, HD:2 * HD, :]))
            for c in range(QB):
                step(nc.vector.tensor_scalar(sg[:, :, c], um[:, :, c, c], 0.0, 0.5, ALU.is_ge, ALU.subtract))
                rest = HD - 1 - c
                if not rest:
                    break
                step(nc.vector.scalar_tensor_tensor(piv, sg[:, :, c], 2.0, um[:, :, c, c], ALU.mult, ALU.add))
                step(nc.vector.reciprocal(pinv, piv))
                step(nc.vector.tensor_tensor(ucol[:, :, 0:rest], um[:, :, c + 1:, c],
                                             pinv.unsqueeze(2).to_broadcast([P, H, rest]), ALU.mult))
                tmp = yt[:, 0:H * rest * rest].rearrange("p (h r k) -> p h r k", h=H, r=rest)
                shape = [P, H, rest, rest]
                step(nc.vector.tensor_tensor(tmp, ucol[:, :, 0:rest].unsqueeze(3).to_broadcast(shape),
                                             um[:, :, c, c + 1:].unsqueeze(2).to_broadcast(shape), ALU.mult))
                step(nc.vector.tensor_tensor(um[:, :, c + 1:, c + 1:], um[:, :, c + 1:, c + 1:], tmp, ALU.subtract))
            step(nc.vector.tensor_scalar(sg, sg, -2.0, None, ALU.mult))
            for c in range(2):
                ins = nc.vector.tensor_tensor(mx[:, :, c].rearrange("p i h j -> p h i j"), ym[:, :, 2 * HD:, :],
                                              sg.unsqueeze(2).to_broadcast([P, H, HD, HD]), ALU.mult)
            ins.then_inc(ev("mx_done"), 1)
            dve.wait_ge(ev("bases_mm"), 1)
            for q in range(2):
                v = bank[2 + q][:, :].rearrange("p (i x b t) -> p b t x i", i=4, x=2, b=2)
                for b in range(2):
                    half = slice(b * D, b * D + D)
                    nc.vector.tensor_copy(bases[half, :, :, 4 * q:4 * q + 4], v[half, b]).then_inc(ev("bases_ready"), 1)

        def attention_dve(dve, s, u):
            p1 = 1 - u
            a, b1, b2 = within(s, 0, PAIRS), within(s - 1, 0, PAIRS), within(s - 2, 0, PAIRS)
            prep = within(s + 1, 0, PAIRS)

            def scores(j):
                if not a:
                    return
                dve.wait_ge(ev("lg_done"), NG * s + j + 1)
                need(dve, ev("av_done"), s - 1)
                masked = N - (8 - 1) * TILES
                parts = [[i for i in GROUPS[j] if i < masked], [i for i in GROUPS[j] if i >= masked]]
                for c, tiles in enumerate(parts):
                    if tiles:
                        lo, k = tiles[0] - GROUPS[j].start, len(tiles)
                        ins = nc.vector.tensor_scalar(
                            ll[u][:, tiles[0]:tiles[0] + k, :],
                            bank[2 + j % 2][:, lo * N:(lo + k) * N].rearrange("p (a b) -> p a b", a=k),
                            score_c[:, c:c + 1], None, ALU.add)
                ins.then_inc(ev("scores_out"), 1)
            if b1:
                need(dve, ev("t1_done"), s - 1)
                dve.wait_ge(ev("scores_out"), NG * s)
                nc.vector.tensor_reduce(mxv, ll[p1].rearrange("p t n -> p n t"), AX.X, ALU.max).then_inc(ev("mx_ready"), 1)
            if b2:
                t = s - 2
                dve.wait_ge(ev("pr_done"), t + 1)
                hp = h_txt[:, bass.ds(2 * t, 2), :]
                nc.vector.tensor_tensor(hp, hp, bank[7][:, 0:P].rearrange("p (a b) -> p a b", a=2), ALU.add)
                ht = h_tok[:, bass.ds(t, 1), :]
                nc.vector.tensor_tensor(ht, ht, bank[7][0:2 * TOK, P:P + D].unsqueeze(1), ALU.add).then_inc(ev("h_added"), 1)
            if b2:
                t = s - 2
                dve.wait_ge(ev("h_added"), t + 1)
                nc.vector.tensor_copy(gate[:, 0:1], minus_half[:, 0:1])
                for b in range(2):
                    nc.vector.bn_stats(st6[:, b, :], h_txt[:, bass.ds(2 * t + b, 1), :].rearrange("p a b -> p (a b)"))
                nc.vector.bn_stats(st6[0:2 * TOK, 2, :], h_tok[:, bass.ds(t, 1), :].rearrange("p a b -> p (a b)")).then_inc(
                    ev("stats"), 1)
                dve.wait_ge(ev("stats"), t + 1)
                nc.vector.tensor_copy(gate[:, 1:2], minus_half[:, 1:2])
                for b in range(2):
                    nc.vector.bn_aggr(mv[:, b, :], st6[:, b, :])
                nc.vector.bn_aggr(mv[0:2 * TOK, 2, :], st6[0:2 * TOK, 2, :]).then_inc(ev("moments"), 1)
                dve.wait_ge(ev("moments"), t + 1)
                need(dve, ev("rs_ready"), t)
                nc.vector.tensor_scalar(ve, mv[:, :, 1], EPS, None, ALU.add).then_inc(ev("ve_ready"), 1)
            if prep:
                t = s + 1
                dve.wait_ge(ev("k_mm"), t + 1)
                need(dve, ev("k_diag"), 16 * G * (t - 1))
                need(dve, ev("lin_ready"), t - 1)
                nc.vector.tensor_scalar(kk[p1][:, :, 0:N], bank[5][:, 0:2 * N].rearrange("p (a b) -> p a b", a=2),
                                        b_qkv[:, 1:2], None, ALU.add).then_inc(ev("k_copied"), 1)
            scores(0)
            if b2:
                t = s - 2
                dve.wait_ge(ev("rs_ready"), t + 1)
                need(dve, ev("t4a_done"), t)
                for b in range(2):
                    nc.vector.tensor_scalar(hn2[:, b, :], h_txt[:, bass.ds(2 * t + b, 1), :].rearrange("p a b -> p (a b)"),
                                            mv[:, b, 0:1], rs[:, b:b + 1], ALU.subtract, ALU.mult)
                for c in range(2):
                    ins = nc.vector.tensor_scalar(hn2k[:, c, :], h_tok[:, bass.ds(t, 1), :].rearrange("p a b -> p (a b)"),
                                                  mv[0:2 * TOK, 2, 0:1], rs[0:2 * TOK, 2:3], ALU.subtract, ALU.mult)
                ins.then_inc(ev("hn2_rows"), 1)
            if b1:
                dve.wait_ge(ev("t1_done"), s)
                nc.vector.tensor_reduce(mn, bank[7][:, 0:P].rearrange("p (g k) -> p g k", g=G), AX.X, ALU.max)
                nc.vector.tensor_reduce(mn5, bank[7][0:TOK, P:2 * P].rearrange("p (g k) -> p g k", g=G), AX.X,
                                        ALU.max).then_inc(ev("mn_done"), 1)
                dve.wait_ge(ev("mn_done"), s)
                nc.vector.tensor_copy(mnx, mn.unsqueeze(2).to_broadcast([P, G, 8]))
                nc.vector.tensor_copy(mnx5, mn5.unsqueeze(2).to_broadcast([TOK, G, 8])).then_inc(ev("mn_ready"), 1)
            scores(1)
            if b1:
                dve.wait_ge(ev("t2_done"), s)
                nc.vector.tensor_tensor(ll[p1], ll[p1], bank[7][:, 0:N].unsqueeze(1).to_broadcast([P, TILES, N]),
                                        ALU.subtract).then_inc(ev("sub_done"), 1)
            scores(2)
            if b2:
                t = s - 2
                dve.wait_ge(ev("t4a_done"), t + 1)
                need(dve, ev("hn2_ready"), t - 1)
                need(dve, ev("t4b_done"), t - 1)
                nc.vector.tensor_copy(hs2[u][:, 0:TXT], bank[7][:, 0:TXT])
                for b in range(2):
                    half, src = slice(b * D, b * D + D), slice(TXT + b * TOK, TXT + b * TOK + TOK)
                    nc.vector.tensor_copy(tk10[u][half, b, :], bank[7][half, src])
                    ins = nc.vector.tensor_copy(hs2[u][half, TXT:N], bank[7][half, src])
                ins.then_inc(ev("hs2_ready"), 1)
            scores(3)
            if b2:
                t = s - 2
                dve.wait_ge(ev("t4b_done"), t + 1)
                nc.vector.tensor_copy(router[:, bass.ds(2 * t, 2), :], bank[7][:, 0:2 * EXPERTS].rearrange("p (a b) -> p a b", a=2))
                nc.vector.tensor_copy(router_tok[:, bass.ds(t, 1), :],
                                      bank[7][0:2 * TOK, 2 * EXPERTS:3 * EXPERTS].unsqueeze(1)).then_inc(ev("router_out"), 1)
            scores(4)
            if b1:
                dve.wait_ge(ev("exp_done"), s)
                need(dve, ev("av_done"), s - 1)
                nc.vector.tensor_reduce(es, ll[p1].rearrange("p t n -> p n t"), AX.X, ALU.add).then_inc(ev("es_ready"), 1)
            scores(5)
            if b1:
                dve.wait_ge(ev("av_done"), s)
                need(dve, ev("pr_done"), s - 1)
                nc.vector.reciprocal(rec, bank[4][:, N:2 * N]).then_inc(ev("rec_ready"), 1)
                dve.wait_ge(ev("rec_ready"), s)
                nc.vector.tensor_tensor(ot, bank[4][:, 0:N], rec, ALU.mult)
                for b in range(2):
                    half = slice(b * D, b * D + D)
                    ins = nc.vector.tensor_tensor(ot5[half, b, :], bank[4][half, TXT:N], rec[half, TXT:N], ALU.mult)
                ins.then_inc(ev("ot_ready"), 1)

        def route(dve):
            dve.wait_ge(ev("hn2_ready"), PAIRS)
            dve.wait_ge(ev("router_out"), PAIRS)
            ch = Chain(dve, ev("route_chain"))
            for i, (r, x) in enumerate(ROUTES()):
                parts, n = r.shape[0], r.shape[1]
                full = [parts, n, EXPERTS]
                m, gt, eq, rank = rt_m[0:parts, 0:n], rt_gt[0:parts, 0:n], rt_eq[0:parts, 0:n], rt_rank[0:parts, 0:n]
                ch.step(nc.vector.tensor_reduce(m, r, AX.X, ALU.max))
                nc.vector.tensor_tensor(x, r, m.unsqueeze(2).to_broadcast(full), ALU.subtract).then_inc(ev("rt_shifted"), 1)
                dve.wait_ge(ev("rt_exp"), i + 1)

                def normalise(dst):
                    ch.step(nc.vector.tensor_reduce(m, x, AX.X, ALU.add))
                    ch.step(nc.vector.reciprocal(m, m))
                    ch.step(nc.vector.tensor_tensor(dst, x, m.unsqueeze(2).to_broadcast(full), ALU.mult))
                normalise(x)
                square = [parts, n, EXPERTS, EXPERTS]
                other, own = x.unsqueeze(2).to_broadcast(square), x.unsqueeze(3).to_broadcast(square)
                nc.vector.tensor_tensor(gt, other, own, ALU.is_gt)
                ch.step(nc.vector.tensor_tensor(eq, other, own, ALU.is_equal))
                ch.step(nc.vector.tensor_tensor(eq, eq, earlier[0:parts].unsqueeze(1).to_broadcast(square), ALU.mult))
                ch.step(nc.vector.tensor_tensor(gt, gt, eq, ALU.add))
                ch.step(nc.vector.tensor_reduce(rank, gt, AX.X, ALU.add))
                ch.step(nc.vector.tensor_scalar(rank, rank, 2.0, None, ALU.is_lt))
                ch.step(nc.vector.tensor_tensor(x, x, rank, ALU.mult))
                normalise(r)
                pieces, h = (wsp, wsp_tok)[i], rt_16[0:parts, 0:n]
                ch.step(nc.vector.memset(pieces[:, :, 3, :], 0.0))
                for k in range(2):
                    ch.step(nc.vector.tensor_copy(h, r))
                    ch.step(nc.vector.tensor_copy(pieces[:, :, k, :], h))
                    ch.step(nc.vector.tensor_tensor(r, r, pieces[:, :, k, :], ALU.subtract))
                ch.step(nc.vector.tensor_copy(pieces[:, :, 2, :], r))
            for v in (*mt, yk, dup):
                nc.vector.memset(v, 0.0)
            nc.vector.memset(x_r, 0.0)
            ch.step(nc.vector.memset(yt_sb, 0.0))
            for b in range(2):
                for c in range(2):
                    half = slice(b * D, b * D + D)
                    ins = nc.vector.tensor_copy(dup[half, b, c * D:c * D + D], ident[half, half])
            ins.then_inc(ev("weights_split"), 1)
            dve.wait_ge(ev("weights_split"), 1)

        def combine(dve, s, u):
            t1, p1 = s + 1, 1 - u
            if within(s - 1, 0, PAIRS):
                dve.wait_ge(ev("y_mm"), s)
                need(dve, ev("y_turned"), s - 1)
                nc.vector.tensor_scalar(yt_sb, bank[5][:, 0:N], b2s_col[:, :], None, ALU.add)
                for b in range(2):
                    half = slice(b * D, b * D + D)
                    ins = nc.vector.tensor_scalar(yk[half, b, :], bank[5][half, TXT:N], b2s_col[half, :], None, ALU.add)
                ins.then_inc(ev("y_copied"), 1)
            for e in range(EXPERTS):
                if within(s, 0, PAIRS):
                    dve.wait_ge(ev("mask_mm"), EXPERTS * s + e + 1)
                    dve.wait_ge(ev("gelu_done"), CH * s + 2 * e + 2)
                    nc.vector.tensor_tensor(hg[e % HG], hg[e % HG],
                                            bank[4 + 2 * (e % 2)][:, 0:2 * N].unsqueeze(1).to_broadcast([P, 2, 2 * N]),
                                            ALU.mult).then_inc(ev("weighted"), 1)
                if e == 1 and within(s - 1, 0, PAIRS):
                    dve.wait_ge(ev("y_turned"), s)
                    need(dve, ev("out_stored"), 64 * (s - 1))
                    nc.vector.tensor_copy(yo[2][0:2 * TOK], bank[7][0:2 * TOK, P:P + D])
                    for b in range(2):
                        ins = nc.vector.tensor_tensor(
                            yo[b], bank[7][:, b * D:b * D + D],
                            h_txt[:, bass.ds(2 * (s - 1) + b, 1), :].rearrange("p a d -> p (a d)"), ALU.add)
                    ins.then_inc(ev("y_added"), 1)
                    dve.wait_ge(ev("y_added"), s)
                    nc.vector.tensor_tensor(yo[2][0:2 * TOK], yo[2][0:2 * TOK],
                                            h_tok[:, bass.ds(s - 1, 1), :].rearrange("p a d -> p (a d)"),
                                            ALU.add).then_inc(ev("y_out"), 1)
                if e == 3 and within(t1, 0, PAIRS):
                    dve.wait_ge(ev("w_turned2"), t1 + 1)
                    need(dve, ev("mask_mm"), EXPERTS * (t1 - 1))
                    need(dve, ev("y_mm"), t1 - 1)
                    for b in range(2):
                        rows = slice(32 * b, 32 * b + 32)
                        nc.vector.tensor_copy(mt[p1][rows, b, 0:TXT], bank[7][rows, 0:TXT])
                        ins = nc.vector.tensor_copy(mt[p1][rows, b, TXT:N],
                                                    bank[7][rows, TXT + b * TOK:TXT + b * TOK + TOK])
                    ins.then_inc(ev("mt_ready"), 1)
                if e == 4 and within(t1, 0, PAIRS):
                    dve.wait_ge(ev("x_mm"), t1 + 1)
                    need(dve, ev("w1_done"), CH * (t1 - 1))
                    xd = bank[3][:, 0:2 * N]
                    nc.vector.tensor_copy(x12[p1], xd).then_inc(ev("x_piece"), 1)
                    dve.wait_ge(ev("x_piece"), 4 * t1 + 1)
                    nc.vector.tensor_copy(x13[p1][0:D], x12[p1][0:D])
                    nc.vector.tensor_tensor(x_r, xd, x12[p1], ALU.subtract).then_inc(ev("x_piece"), 1)
                    dve.wait_ge(ev("x_piece"), 4 * t1 + 2)
                if e == 5 and within(t1, 0, PAIRS):
                    nc.vector.tensor_copy(x12[p1][D:P], x_r[D:P]).then_inc(ev("x_piece"), 1)
                    dve.wait_ge(ev("x_piece"), 4 * t1 + 3)
                    nc.vector.tensor_tensor(x13[p1][D:P], x_r[D:P], x12[p1][D:P], ALU.subtract).then_inc(ev("x_piece"), 1)
                    dve.wait_ge(ev("x_piece"), 4 * t1 + 4)

        block = ctx.enter_context(nc.Block())

        @block.sync
        def _(sp):
            tl = ev("tree_loaded")
            loads = [
                (ids_raw[:, 0:LEAFC], a["leaf_ids"].rearrange("(t s) l -> t (s l)", t=ST)),
                (ids_raw[:, LEAFC:], a["op_ids"].rearrange("(t s) l -> t (s l)", t=ST)),
                (comp, a["comp_emb"].rearrange("(v p) d -> p v d", v=2)),
                (op_raw, a["op_emb"]),
                (w_op, a["W_bin"][0:D, :]),
                (w_lr, a["W_bin"][D:3 * D, :]),
                (bc_row, a["b_bin"].rearrange("(o d) -> o d", o=1)),
                (gamma_bc, a["gamma"].partition_broadcast(P)),
                (beta_bc, a["beta"].partition_broadcast(P)),
                (txt_idx, a["x_txt"].rearrange("b n -> n b")),
            ]
            for dst, src in loads:
                sp.dma_start(dst, src).then_inc(tl, 16)

            kl = ev("tok_loaded")
            x = a["x"].rearrange("b c h w -> (b c) h w")
            sp.dma_start(xs[0:PH], x[:, 0:PH, :].rearrange("b h w -> h b w")).then_inc(kl, 16)
            sp.dma_start(xs[PH:P, :, 0:PX - 1], x[:, 0:PH, 1:PX].rearrange("b h w -> h b w")).then_inc(kl, 16)
            w = a["tok_weight"].rearrange("(h w) d -> h w d", h=PH)
            sp.dma_start(wt[0:PH], w[:, 0:PW:2, :]).then_inc(kl, 16)
            sp.dma_start(wt[PH:P, 0:PW // 2, :], w[:, 1:PW:2, :]).then_inc(kl, 16)
            for b in range(2):
                sp.dma_start(btok[b * D:b * D + D], a["tok_bias"].rearrange("(d o) -> d o", o=1)).then_inc(kl, 16)

            wl = ev("weights_loaded")
            n = [0]

            def load(dst, src):
                sp.dma_start(dst, src).then_inc(wl, 16)
                n[0] += 1
            for b in range(2):
                load(wn[:, 0:3, b, :], a["w_qkv"].rearrange("(s c) d -> c s d", s=3))
                load(wn[:, 3, b, :], a["w_proj"])
                half = slice(b * D, b * D + D)
                for s in range(3):
                    load(b_qkv[half, s:s + 1], a["b_qkv"][s * D:s * D + D].rearrange("(d o) -> d o", o=1))
                load(b_top[half, :], a["b_qkv"][b * D:b * D + D].partition_broadcast(D))
                load(bp_row[:, b, :], a["b_proj"].rearrange("(o d) -> o d", o=1))
                load(wr_both[half, :], a["Wr"])
                load(w1_f[half, 0:EXPERTS, :], a["W1p"].rearrange("e d f -> d e f"))
                load(w1_f[half, EXPERTS, :], a["W1s"])
                load(b2s_col[half, :], a["b2s"].rearrange("(d o) -> d o", o=1))
            load(b_qk_rows[:, :], a["b_qkv"][0:P].partition_broadcast(P))
            for c in range(2):
                load(w2_s[:, 0:EXPERTS, c, :], a["W2p"][:, c * P:c * P + P, :].rearrange("e f d -> f e d"))
                load(w2_s[:, EXPERTS, c, :], a["W2s"][c * P:c * P + P, :])
                load(b1_col[:, 0:EXPERTS, c], a["b1p"][:, c * P:c * P + P].rearrange("e f -> f e"))
                load(b1_col[:, EXPERTS, c:c + 1], a["b1s"][c * P:c * P + P].rearrange("(f o) -> f o", o=1))
            for i in range(D // EXPERTS):
                load(b2_rows[i * EXPERTS:(i + 1) * EXPERTS, :], a["b2p"])
            load(conv_t[:, :], a["conv_w"].rearrange("o c -> c o"))
            for i, name in enumerate(["bn_gamma", "bn_beta", "bn_mean", "bn_var"]):
                load(bn[:, i:i + 1], a[name].rearrange("(c o) -> c o", o=1))
            for i, name in enumerate(["scale", "riem_scale", "grassman_scale"]):
                load(score_scale[i * H:i * H + H, :], a[name].partition_broadcast(H))
            load(cb_row[:, :], a["conv_b"].rearrange("(o c) -> o c", o=1))
            assert n[0] == WLOADS, n[0]

            def store_roots(s, _):
                if within(s - 2, 0, TS):
                    need(sp, ev("roots_ready"), s - 1)
                    sp.dma_start(root_dram.rearrange("(i u s) d -> i s u d", u=2, s=P)[s - 2], lv_g[2]).then_inc(
                        ev("roots_stored"), 16)
            slots(sp, 0, 2, TS, TS + 2, 1, store_roots)


            def diag(s, u):
                t, par = s + 1, 1 - u
                if within(t, 0, PAIRS):
                    sp.wait_ge(ev("k_copied"), t + 1)
                    if isinstance(t, int) and t < 2:
                        sp.wait_ge(ev("blocks_zero"), 2)
                    for g in range(G):
                        r = slice(8 * g, 8 * g + 8)
                        sp.dma_start(kbd[par][r, :, g, :], kk[par][r, :, :]).then_inc(ev("k_diag"), 16)
                    if isinstance(t, int) and t == 0:
                        sp.wait_ge(ev("v_copied"), 1)
                    else:
                        sp.wait_ge(ev("vt_done"), NVT * t)
                    for g in range(G):
                        r = slice(8 * g, 8 * g + 8)
                        sp.dma_start(vbt[r, g, :], vv[par][r, :]).then_inc(ev("v_diag"), 16)
            slots(sp, -1, 5, PAIRS - 1, PAIRS + 2, 2, diag)

            pairs_out = out.rearrange("(t b) n d -> t b n d", b=2)

            def store(t, u):
                sp.wait_ge(ev("y_out"), t + 1)
                for b in range(2):
                    sp.dma_start(pairs_out[t, b, TOK:N, :], yo[b]).then_inc(ev("out_stored"), 16)
                sp.dma_start(pairs_out[t, 0, 0:TOK, :], yo[2][0:TOK, :]).then_inc(ev("out_stored"), 16)
                sp.dma_start(pairs_out[t, 1, 0:TOK, :], yo[2][TOK:2 * TOK, :]).then_inc(ev("out_stored"), 16)
            slots(sp, 0, 2, PAIRS, PAIRS, 2, store)
            sp.wait_ge(ev("out_stored"), 64 * PAIRS)

        @block.gpsimd
        def _(pool):
            ch = Chain(pool, ev("pool_chain"))
            nc.gpsimd.memset(ones_row[:, :], 1.0)
            nc.gpsimd.memset(ones_col[:, :], 1.0)
            nc.gpsimd.memset(ones16[:, :], 1.0)
            nc.gpsimd.memset(eps_col[:, :], EPS)
            nc.gpsimd.memset(minus_half[:, :], -0.5)
            nc.gpsimd.memset(pick_sq[:, :], 0.0)
            nc.gpsimd.memset(pick_lin[:, :], 0.0)
            nc.gpsimd.memset(ident2[:, :], 0.0)
            nc.gpsimd.iota(iota_col[:, :], pattern=[[P, 2]], base=0, channel_multiplier=1,
                           allow_small_or_imprecise_dtypes=True)
            ch.step(nc.gpsimd.memset(ident[:, :], 0.0))

            def diagonal(v, pattern, base=0):
                return nc.gpsimd.affine_select(out=v, in_=v, compare_op=ALU.not_equal, fill=1.0, base=base,
                                               pattern=pattern, channel_multiplier=1)
            diagonal(ident[:, :], [[-1, P]]).then_inc(ev("ident_ready"), 1)
            diagonal(ident2[:, :], [[-1, D]])
            diagonal(pick_lin[:, :].rearrange("c (h d) -> c h d", h=H), [[-1, H], [0, HD]])
            diagonal(pick_sq[:, :].rearrange("c (g m) -> c g m", g=G), [[-1, G], [0, 8]], base=-H)
            ch.step(nc.gpsimd.memset(wq_dup[:, :, :], 0.0))
            diagonal(ident2[:, :], [[-1, D]], base=-D)
            nc.gpsimd.memset(earlier[:, :, :], 1.0).then_inc(ev("earlier_ones"), 1)
            pool.wait_ge(ev("earlier_ones"), 1)
            nc.gpsimd.affine_select(out=earlier[:, :, :], in_=earlier[:, :, :], compare_op=ALU.is_gt, fill=0.0,
                                    base=0, pattern=[[1, EXPERTS], [-1, EXPERTS]], channel_multiplier=0)
            for z in (wk_dup, wqk_pair, wr_pair):
                nc.gpsimd.memset(z[:, :, :], 0.0)
            nc.gpsimd.memset(wv_pair[:, :], 0.0)
            nc.gpsimd.memset(tok_m, 0.0)
            nc.gpsimd.memset(wp_pair[:, :], 0.0).then_inc(ev("zeros_ready"), 1)

            def affine(level, s):
                shape = [P, 8 >> level, D]
                first = isinstance(s, int) and s == 0
                pool.wait_ge(ev(f"normed{level}"), s + 1)
                if level < 2:
                    need(pool, ev(f"kids{level}"), s)
                else:
                    need(pool, ev("roots_stored"), 16 * s)
                nc.gpsimd.tensor_tensor(lv_g[level], lv_h[level], gamma_bc.unsqueeze(1).to_broadcast(shape),
                                        ALU.mult).then_inc(ev(f"gained{level}"), 1)
                pool.wait_ge(ev(f"gained{level}"), s + 1)
                nc.gpsimd.tensor_tensor(lv_g[level], lv_g[level], beta_bc.unsqueeze(1).to_broadcast(shape),
                                        ALU.add).then_inc(ev(f"leveled{level}" if level < 2 else "roots_raw" if first else "roots_ready"), 1)

            def tree(s, _):
                if within(s, 0, TS):
                    affine(0, s)
                if within(s - 1, 0, TS):
                    affine(1, s - 1)
                if within(s - 2, 0, TS):
                    affine(2, s - 2)
                    if isinstance(s, int) and s == 2:
                        pool.wait_ge(ev("roots_raw"), 1)
                        nc.gpsimd.memset(lv_g[2][0:2, 0, :], 0.0).then_inc(ev("roots_ready"), 1)
            pool.wait_ge(ev("tree_loaded"), 160)
            slots(pool, 0, 3, TS, TS + 2, 1, tree)

            pool.wait_ge(ev("roots_stored"), 16 * TS)
            for b in range(B):
                nc.gpsimd.indirect_dma_start(
                    out=h_txt[:, b, :], out_offset=None, in_=root_dram,
                    in_offset=bass.IndirectOffsetOnAxis(ap=txt_idx[:, b:b + 1], axis=0)).then_inc(
                        ev(f"gathered{b // 16}"), 16)

            pool.wait_ge(ev("bases_ready"), 4)
            for par in range(2):
                nc.gpsimd.memset(kbd[par], 0.0)
            nc.gpsimd.memset(mv, 1.0)
            nc.gpsimd.memset(ot5, 0.0).then_inc(ev("blocks_zero"), 1)
            pool.wait_ge(ev("blocks_zero"), 2)

            def attention(s, u):
                t, par = s + 1, 1 - u
                if within(t, 0, PAIRS):
                    need(pool, ev("p_mm"), t - 1)
                    shape = [P, 2, H, HD]
                    for b in range(2):
                        nc.gpsimd.tensor_tensor(
                            mqx[par][:, b], bases[:, bass.ds(t, 1), 0, :].unsqueeze(2).to_broadcast(shape),
                            group_of[:, b * H:b * H + H].unsqueeze(1).unsqueeze(3).to_broadcast(shape), ALU.mult)
                    nc.gpsimd.tensor_tensor(mkx[par], bases[:, bass.ds(t, 1), 1, :].to_broadcast([P, H, HD]),
                                            head_of[:, :].unsqueeze(2).to_broadcast([P, H, HD]),
                                            ALU.mult).then_inc(ev("mq_ready"), 1)
                if within(s - 2, 0, PAIRS):
                    pool.wait_ge(ev("ve_ready"), s - 1)
                    nc.gpsimd.tensor_tensor(rs, ve, minus_half[:, 0:3], ALU.pow).then_inc(ev("rs_ready"), 1)
                if within(t, 0, PAIRS):
                    pool.wait_ge(ev("k_copied"), t + 1)
                    need(pool, ev("lg_done"), NG * (t - 1))
                    shape = [D, 2, H, NP]
                    nc.gpsimd.tensor_tensor(linb[par][0:D], kk[par][0:D].unsqueeze(2).to_broadcast(shape),
                                            lin_a[:, :].unsqueeze(1).unsqueeze(3).to_broadcast(shape),
                                            ALU.mult).then_inc(ev("lin_ready"), 1)
            slots(pool, -1, 5, PAIRS - 1, PAIRS + 2, 2, attention)

        @block.scalar
        def _(act):
            act.wait_ge(ev("ident_ready"), 1)
            act.wait_ge(ev("comp_centred"), 1)
            nc.scalar.activation(comp_sq, comp, ACT.Square).then_inc(ev("comp_sq"), 1)
            act.wait_ge(ev("comp_var"), 1)
            nc.scalar.activation(comp_st[:, 2, :], comp_st[:, 1, :], ACT.Sqrt, bias=eps_col[:, :],
                                 scale=1.0 / D).then_inc(ev("comp_std"), 1)

            def copy_ids(s, u):
                act.wait_ge(ev("ids_bc"), 2 * s + u + 1)
                if not isinstance(s, int) or 2 * s + u > 0:
                    act.wait_ge(ev("hot"), 2 * s + u)
                for i, (lo, hi) in enumerate(ID_PARTS):
                    ins = nc.scalar.activation(ids_bc[:, lo:hi], bank[i][:, 0:hi - lo], ACT.Identity)
                ins.then_inc(ev("ids_copied"), 1)

            def deviation(level, s):
                n = 8 >> level
                act.wait_ge(ev(f"level{level}"), s + 1)
                need(act, ev(f"var{level}"), s)
                nc.scalar.activation(lv_sq[level], LV[level], ACT.Square).then_inc(ev(f"sq{level}"), 1)

            def root(level, s):
                act.wait_ge(ev(f"var{level}"), s + 1)
                need(act, ev(f"inv{level}"), s)
                nc.scalar.activation(lv_std[level], lv_var[level], ACT.Sqrt, bias=eps_col[:, :],
                                     scale=1.0 / D).then_inc(ev(f"std{level}"), 1)

            def tree(s, _):
                if within(s - 1, 0, TS):
                    act.wait_ge(ev("kids0"), s)
                    need(act, ev("level1"), s - 1)
                    nc.scalar.activation(kids1, bank[5][:, :].rearrange("p (a b) -> p a b", a=4),
                                         ACT.Identity).then_inc(ev("kids0_copied"), 1)
                if within(s - 2, 0, TS):
                    act.wait_ge(ev("kids1"), s - 1)
                    need(act, ev("level2"), s - 2)
                    nc.scalar.activation(kids2, bank[5][:, 0:256].rearrange("p (a b) -> p a b", a=2),
                                         ACT.Identity).then_inc(ev("kids1_copied"), 1)
                for level in range(3):
                    if within(s - level, 0, TS):
                        deviation(level, s - level)
                for level in range(3):
                    if within(s - level, 0, TS):
                        root(level, s - level)
                if within(s + 1, 0, TS):
                    copy_ids(s + 1, 0)
                    copy_ids(s + 1, 1)
            copy_ids(0, 0)
            copy_ids(0, 1)
            slots(act, 0, 3, TS - 1, TS + 2, 1, tree)

            act.wait_ge(ev("tok_mm"), 1)
            act.wait_ge(ev("tok_loaded"), 96)
            nc.scalar.activation(tok_t.rearrange("p a b -> p (a b)"), bank[0][:, 0:PAIRS * TOK], ACT.Gelu,
                                 bias=btok).then_inc(ev("tok_gelu"), 1)
            act.wait_ge(ev("weights_loaded"), 16 * WLOADS)
            nc.scalar.activation(bn_inv[:, 0:1], bn[:, 3:4], ACT.Sqrt, bias=eps_col[0:3 * H, :]).then_inc(ev("bn_std"), 1)
            for g in range(5):
                act.wait_ge(ev("ln_centred"), g + 1)
                w = ln_slice(g)
                nc.scalar.activation(w["sq"], w["hn"], ACT.Square).then_inc(ev("ln_sq"), 1)
                act.wait_ge(ev("ln_var"), g + 1)
                nc.scalar.activation(w["d"], w["v"], ACT.Sqrt, bias=eps_col[0:w["parts"], :],
                                     scale=1.0 / D).then_inc(ev("ln_std"), 1)

            def first(s, u):
                if within(s, 0, PAIRS):
                    need(act, ev("hs_mm"), s - 1)
                    if isinstance(s, int) and s == 0:
                        act.wait_ge(ev("hn_ready"), 5)
                    nc.scalar.activation(st_txt[u], hn_txt[:, bass.ds(2 * s, 2), :], ACT.Identity)
                    nc.scalar.activation(st_tok[u], hn_tok[:, bass.ds(s, 1), :].to_broadcast([2 * TOK, 2, D]),
                                         ACT.Identity).then_inc(ev("staged"), 1)
                if within(s - 1, 0, PAIRS):
                    act.wait_ge(ev("hs_ready"), s)
                    nc.scalar.activation(hn_t[:, bass.ds(s - 1, 1), :], hs[1 - u][:, 0:N].unsqueeze(1),
                                         ACT.Identity).then_inc(ev("hn_t_ready"), 1)
            slots(act, 0, 3, PAIRS - 1, PAIRS + 1, 2, first)

            for c in range(QB):
                act.wait_ge(ev("pivot"), c + 1)
                nc.scalar.activation(qsd, ym[:, :, c, c], ACT.Sqrt).then_inc(ev("pivot_root"), 1)

            def attention(s, u):
                t1, p1 = s + 1, 1 - u

                def squares(j, b):
                    act.wait_ge(ev("dg_done"), 2 * NG * s + 2 * j + b + 1)
                    need(act, ev("lg_done"), NG * s + j - 1)
                    n = len(GROUPS[j]) * N
                    nc.scalar.activation(sq[b][j % 2][:, 0:n], bank[b][:, 0:n], ACT.Square).then_inc(ev("sq_done"), 1)

                def turned(r):
                    act.wait_ge(ev("vt_done"), NVT * s + r + 1)
                    need(act, ev("av_done"), s - 1)
                    n = len(VTS[r])
                    nc.scalar.activation(vbd[u][:, VTS[r].start:VTS[r].stop, :],
                                         bank[5 + r % 2][:, 0:n * P].rearrange("p (a b) -> p a b", a=n),
                                         ACT.Identity).then_inc(ev("vt_copied"), 1)
                for j in range(NG):
                    if within(s, 0, PAIRS):
                        squares(j, 0)
                        squares(j, 1)
                    if within(t1, 0, PAIRS):
                        if j == 0:
                            act.wait_ge(ev("q_mm"), t1 + 1)
                            need(act, ev("lg_done"), NG * (t1 - 1))
                            nc.scalar.activation(qq[p1].rearrange("p a b -> p (a b)"), bank[6][:, 0:2 * N], ACT.Identity,
                                                 bias=b_qkv[:, 0:1]).then_inc(ev("q_copied"), 1)
                        if j == 1:
                            act.wait_ge(ev("v_mm"), t1 + 1)
                            need(act, ev("v_diag"), 16 * G * (t1 - 1))
                            nc.scalar.activation(vv[p1][:, 0:N], bank[6][:, 0:N], ACT.Identity,
                                                 bias=b_qkv[:, 2:3]).then_inc(ev("v_copied"), 1)
                            act.wait_ge(ev("p_mm"), t1 + 1)
                            need(act, ev("q2_mm"), t1 - 1)
                            nc.scalar.activation(pm[p1][D:P].rearrange("p a b -> p (a b)"), bank[5][D:P, 0:P],
                                                 ACT.Identity).then_inc(ev("p_copied"), 1)
                        if j == 2:
                            act.wait_ge(ev("q2_mm"), t1 + 1)
                            nc.scalar.activation(qq[p1][D:P].rearrange("p a b -> p (a b)"), bank[6][D:P, 0:2 * N],
                                                 ACT.Identity).then_inc(ev("q2_ready"), 1)
                    if j == 3 and within(s, 0, PAIRS):
                        turned(0)
                        turned(1)
                    if j == 4 and within(s - 1, 0, PAIRS):
                        act.wait_ge(ev("sub_done"), s)
                        nc.scalar.activation(ll[p1], ll[p1], ACT.Exp).then_inc(ev("exp_done"), 1)
                    if j == 4 and within(s, 0, PAIRS):
                        turned(2)
                        turned(3)
                    if j == 5 and within(s, 0, PAIRS):
                        turned(4)
                if within(s - 2, 0, PAIRS):
                    act.wait_ge(ev("hs2_ready"), s - 1)
                    nc.scalar.activation(hn_t[:, bass.ds(s - 2, 1), :], hs2[u].unsqueeze(1),
                                         ACT.Identity).then_inc(ev("hn2_ready"), 1)
            act.wait_ge(ev("blocks_zero"), 2)
            slots(act, -1, 5, PAIRS - 1, PAIRS + 2, 2, attention)

            for i, (r, x) in enumerate(ROUTES()):
                act.wait_ge(ev("rt_shifted"), i + 1)
                nc.scalar.activation(x, x, ACT.Exp).then_inc(ev("rt_exp"), 1)

            def experts(s, u):
                t1, p1 = s + 1, 1 - u
                for c in range(CH):
                    if within(s, 0, PAIRS):
                        act.wait_ge(ev("w1_done"), CH * s + c + 1)
                        if c % 2 == 0:
                            need(act, ev("w2_done"), (EXPERTS + 1) * s + c // 2 + 1 - HG)
                        nc.scalar.activation(hg[c // 2 % HG][:, c % 2], bank[c % 3][:, 0:2 * N], ACT.Gelu,
                                             bias=b1_col[:, c // 2, c % 2:c % 2 + 1]).then_inc(ev("gelu_done"), 1)
                    if c == 1 and within(t1, 0, PAIRS):
                        need(act, ev("w_turned2"), t1 - 1)
                        if isinstance(t1, int) and t1 == 0:
                            act.wait_ge(ev("weights_split"), 1)
                        nc.scalar.activation(st_w[p1], wsp[:, bass.ds(2 * t1, 2)].rearrange(
                            "p a b c -> p (a b c)").unsqueeze(1).to_broadcast([P, 2, D]), ACT.Identity)
                        nc.scalar.activation(st_wk[p1],
                                             wsp_tok[:, bass.ds(t1, 1)].rearrange("p a b c -> p a (b c)").to_broadcast(
                                                 [2 * TOK, 2, 4 * EXPERTS]), ACT.Identity).then_inc(ev("w_staged"), 1)
            slots(act, -1, 3, PAIRS - 1, PAIRS + 1, 2, experts)

        @block.vector
        def _(dve):
            ch = Chain(dve, ev("dve_chain"))
            dve.wait_ge(ev("tree_loaded"), 160)
            dve.wait_ge(ev("ident_ready"), 1)
            nc.vector.tensor_copy(ids_all[:, 0:LEAFC].rearrange("t (l s) -> t l s", l=LEAVES),
                                  ids_raw[:, 0:LEAFC].rearrange("t (s l) -> t l s", l=LEAVES))
            nc.vector.tensor_copy(ids_all[:, LEAFC:].rearrange("t (l s) -> t l s", l=INNER),
                                  ids_raw[:, LEAFC:].rearrange("t (s l) -> t l s", l=INNER))
            nc.vector.memset(tab_op[OPS:P], 0.0)
            nc.vector.tensor_reduce(w_mean[:, 0:1], w_lr, AX.X, ALU.add)
            nc.vector.tensor_reduce(w_mean[0:D, 1:2], w_op, AX.X, ALU.add)
            nc.vector.tensor_reduce(w_mean[0:1, 2:3], bc_row, AX.X, ALU.add)
            ch.step(nc.vector.tensor_reduce(comp_st[:, 0, :], comp, AX.X, ALU.add))
            nc.vector.tensor_scalar(w_mean[:, 0:1], w_mean[:, 0:1], 1.0 / D, None, ALU.mult)
            nc.vector.tensor_scalar(w_mean[0:D, 1:2], w_mean[0:D, 1:2], 1.0 / D, None, ALU.mult)
            nc.vector.tensor_scalar(w_mean[0:1, 2:3], w_mean[0:1, 2:3], 1.0 / D, None, ALU.mult)
            ch.step(nc.vector.tensor_scalar(comp_st[:, 0, :], comp_st[:, 0, :], 1.0 / D, None, ALU.mult))
            nc.vector.tensor_scalar(w_lr, w_lr, w_mean[:, 0:1], None, ALU.subtract)
            nc.vector.tensor_scalar(w_op, w_op, w_mean[0:D, 1:2], None, ALU.subtract)
            nc.vector.tensor_scalar(bc_row, bc_row, w_mean[0:1, 2:3], None, ALU.subtract)
            nc.vector.tensor_tensor(comp, comp, comp_st[:, 0, :].unsqueeze(2).to_broadcast([P, 2, D]),
                                    ALU.subtract).then_inc(ev("comp_centred"), 1)
            dve.wait_ge(ev("comp_sq"), 1)
            nc.vector.tensor_reduce(comp_st[:, 1, :], comp_sq, AX.X, ALU.add).then_inc(ev("comp_var"), 1)
            dve.wait_ge(ev("comp_std"), 1)
            ch.step(nc.vector.reciprocal(comp_st[:, 3, :], comp_st[:, 2, :]))
            ch.step(nc.vector.tensor_tensor(comp, comp, comp_st[:, 3, :].unsqueeze(2).to_broadcast([P, 2, D]), ALU.mult))
            ch.step(nc.vector.tensor_tensor(comp, comp, gamma_bc.unsqueeze(1).to_broadcast([P, 2, D]), ALU.mult))
            for c in range(2):
                ins = nc.vector.tensor_tensor(comp_d[:, :, c, :], comp, beta_bc.unsqueeze(1).to_broadcast([P, 2, D]),
                                              ALU.add)
            ins.then_inc(ev("comp_ready"), 1)
            dve.wait_ge(ev("comp_turned"), 1)
            nc.vector.tensor_copy(comp_t, bank[0][:, 0:256].rearrange("p (a b) -> p a b", a=2))
            nc.vector.tensor_copy(op_t, bank[0][0:D, 256:256 + OPS]).then_inc(ev("comp_copied"), 1)
            dve.wait_ge(ev("tables"), 1)
            for side in range(2):
                nc.vector.tensor_copy(tab_f[:, 2 * side:2 * side + 2, :],
                                      bank[1 + 2 * side][:, 0:P].rearrange("p (a b) -> p a b", a=2))
            ch.step(nc.vector.tensor_copy(tab_f[0:OPS, 4, :], bank[2][0:OPS, 0:D]))
            for piece in range(3):
                nc.vector.tensor_copy(tab[:, :, :, piece, :], tab_f[:, 0:4, :].rearrange("p (a v) d -> p a v d", a=2))
                ins = nc.vector.tensor_copy(tab_op[0:OPS, piece, :], tab_f[0:OPS, 4, :])
                if piece == 2:
                    ins.then_inc(ev("tables_split"), 1)
                    break
                ch.step(ins)
                nc.vector.tensor_copy(tab_r[:, 0:4, :].rearrange("p (a v) d -> p a v d", a=2), tab[:, :, :, piece, :])
                ch.step(nc.vector.tensor_copy(tab_r[0:OPS, 4, :], tab_op[0:OPS, piece, :]))
                nc.vector.tensor_tensor(tab_f[:, 0:4, :], tab_f[:, 0:4, :], tab_r[:, 0:4, :], ALU.subtract)
                ch.step(nc.vector.tensor_tensor(tab_f[0:OPS, 4, :], tab_f[0:OPS, 4, :], tab_r[0:OPS, 4, :], ALU.subtract))

            def pick_ids(s, u):
                if not isinstance(s, int) or 2 * s + u > 0:
                    dve.wait_ge(ev("ids_bc"), 2 * s + u)
                nc.vector.tensor_scalar(ids_one, ids_all, ident[0:ST, bass.ds(2 * s + u, 1)], None,
                                        ALU.mult).then_inc(ev("ids_picked"), 1)

            def hots(s, u):
                dve.wait_ge(ev("ids_copied"), 2 * s + u + 1)
                if u == 0:
                    need(dve, ev("level0"), s)
                    need(dve, ev("level2"), s - 3)
                for v in range(2):
                    nc.vector.tensor_scalar(leaf_hot[:, u, v, :], ids_bc[:, 0:LEAFC], iota_col[:, v:v + 1], None,
                                            ALU.is_equal)
                nc.vector.tensor_scalar(op_hot[:, u, :], ids_bc[0:OPS, LEAFC:LEAFC + 4 * P], iota_col[0:OPS, 0:1],
                                        None, ALU.is_equal)
                nc.vector.tensor_scalar(up_hot[:, bass.ds(2 * (s % 4) + u, 1), :].rearrange("p a b -> p (a b)"),
                                        ids_bc[:, LEAFC + 4 * P:], iota_col[:, 0:1],
                                        None, ALU.is_equal).then_inc(ev("hot"), 1)

            def variance(level, s):
                dve.wait_ge(ev(f"sq{level}"), s + 1)
                need(dve, ev(f"std{level}"), s)
                nc.vector.tensor_reduce(lv_var[level], lv_sq[level], AX.X, ALU.add).then_inc(ev(f"var{level}"), 1)

            def norm(level, s):
                shape = [P, 8 >> level, D]
                dve.wait_ge(ev(f"std{level}"), s + 1)
                nc.vector.reciprocal(lv_inv[level], lv_std[level]).then_inc(ev(f"inv{level}"), 1)
                dve.wait_ge(ev(f"inv{level}"), s + 1)
                need(dve, ev(f"gained{level}"), s)
                nc.vector.tensor_tensor(lv_h[level], LV[level], lv_inv[level].unsqueeze(2).to_broadcast(shape),
                                        ALU.mult).then_inc(ev(f"normed{level}"), 1)

            def tree(s, _):
                for level in range(3):
                    if within(s - level, 0, TS):
                        variance(level, s - level)
                for level in range(3):
                    if within(s - level, 0, TS):
                        norm(level, s - level)
                if within(s + 1, 0, TS):
                    for u in range(2):
                        pick_ids(s + 1, u)
                        hots(s + 1, u)
            for u in range(2):
                pick_ids(0, u)
                hots(0, u)
            slots(dve, 0, 3, TS - 1, TS + 2, 1, tree)

            dve.wait_ge(ev("tok_gelu"), 1)
            dve.wait_ge(ev("zeros_ready"), 1)
            nc.vector.tensor_copy(tok_m[0:D, :, 0, :], tok_t[0:D])
            nc.vector.tensor_copy(tok_m[D:P, :, 1, :], tok_t[D:P]).then_inc(ev("tok_split"), 1)
            for q in range(4):
                dve.wait_ge(ev("tok_rows"), q + 1)
                ins = nc.vector.tensor_copy(h_tok[:, 8 * q:8 * q + 8, :],
                                            bank[1 + q][0:2 * TOK, :].rearrange("p (a b) -> p a b", a=8))
            ins.then_inc(ev("tok_ready"), 1)
            dve.wait_ge(ev("tok_ready"), 1)

            weights(dve, ch)

            for g in range(5):
                w = ln_slice(g)
                if g:
                    dve.wait_ge(ev(f"gathered{g - 1}"), 256)
                ch.step(nc.vector.tensor_reduce(w["s"], w["h"], AX.X, ALU.add))
                ch.step(nc.vector.tensor_scalar(w["m"], w["s"], 1.0 / D, None, ALU.mult))
                nc.vector.tensor_tensor(w["hn"], w["h"], w["m"].unsqueeze(2).to_broadcast(w["shape"]),
                                        ALU.subtract).then_inc(ev("ln_centred"), 1)
                dve.wait_ge(ev("ln_sq"), g + 1)
                nc.vector.tensor_reduce(w["v"], w["sq"], AX.X, ALU.add).then_inc(ev("ln_var"), 1)
                dve.wait_ge(ev("ln_std"), g + 1)
                ch.step(nc.vector.reciprocal(w["r"], w["d"]))
                nc.vector.tensor_tensor(w["hn"], w["hn"], w["r"].unsqueeze(2).to_broadcast(w["shape"]),
                                        ALU.mult).then_inc(ev("hn_ready"), 1)
                if g == 4:
                    nc.vector.memset(gall, 0.0)
                    nc.vector.memset(top, 0.0)

            def first(s, u):
                p1 = 1 - u
                if within(s, 0, PAIRS):
                    dve.wait_ge(ev("hs_mm"), s + 1)
                    need(dve, ev("qk_mm"), s - 1)
                    need(dve, ev("hn_t_ready"), s - 1)
                    nc.vector.tensor_copy(hs[u][:, 0:TXT], bank[u][:, 0:TXT])
                    for b in range(2):
                        ins = nc.vector.tensor_copy(hs[u][b * D:b * D + D, TXT:N],
                                                    bank[u][b * D:b * D + D, TXT + b * TOK:TXT + b * TOK + TOK])
                    ins.then_inc(ev("hs_ready"), 1)
                if within(s - 1, 0, PAIRS):
                    dve.wait_ge(ev("qk_mm"), s)
                    need(dve, ev("gram_mm"), s - 2)
                    nc.vector.tensor_tensor(qkn[p1], bank[2 + p1][:, 0:2 * P].rearrange("p (a b) -> p a b", a=2),
                                            b_qk_rows[:, :].unsqueeze(1).to_broadcast([P, 2, P]), ALU.add)
                    nc.vector.tensor_tensor(qkt[p1], bank[4 + p1][0:TOK, 0:2 * P].rearrange("p (a b) -> p a b", a=2),
                                            b_qk_rows[0:TOK, :].unsqueeze(1).to_broadcast([TOK, 2, P]),
                                            ALU.add).then_inc(ev("qk_ready"), 1)
                if within(s - 2, 0, PAIRS):
                    dve.wait_ge(ev("gram_mm"), s - 1)
                    shape = [P, 2, G, HD]
                    nc.vector.tensor_tensor(gm[u], bank[6 + u][:, 0:2 * P].rearrange("p (a g b) -> p a g b", a=2, g=G),
                                            group_of[:, :].unsqueeze(1).unsqueeze(3).to_broadcast(shape),
                                            ALU.mult).then_inc(ev("gm_ready"), 1)
                    dve.wait_ge(ev("gm_ready"), s - 1)
                    for x in range(2):
                        half = slice(x * D, x * D + D)
                        ins = nc.vector.tensor_reduce(
                            gall[half, :, x, :, bass.ds(s - 2, 1)].rearrange("p a b c -> p b (a c)"),
                            gm[u][half].rearrange("p a g b -> p a b g"), AX.X, ALU.add)
                    ins.then_inc(ev("gall_ready"), 1)
            slots(dve, 0, 4, PAIRS, PAIRS + 2, 2, first)

            dve.wait_ge(ev("hn_t_ready"), PAIRS)
            for x in range(2):
                for b in range(2):
                    half = slice(b * D, b * D + D)
                    nc.vector.tensor_copy(top[half, x, 0:TOK, x, b, :], hn_t[half, :, TXT:N].rearrange("p t n -> p n t"))
                    ins = nc.vector.tensor_copy(top[half, x, TOK:QB, x, b, :],
                                                hn_t[half, :, 0:QB - TOK].rearrange("p t n -> p n t"))
            ins.then_inc(ev("top_ready"), 1)
            factorise(dve)

            for par in range(2):
                nc.vector.memset(linb[par], 0.0)
                nc.vector.memset(kk[par], 0.0)
                nc.vector.memset(vv[par], 0.0)
                nc.vector.memset(tk10[par], 0.0)
                nc.vector.memset(qq[par], 0.0)
                nc.vector.memset(pm[par], 0.0)
            nc.vector.memset(vbt, 0.0).then_inc(ev("blocks_zero"), 1)
            dve.wait_ge(ev("blocks_zero"), 2)
            slots(dve, -1, 5, PAIRS - 1, PAIRS + 2, 2, lambda s, u: attention_dve(dve, s, u))
            route(dve)
            slots(dve, -1, 3, PAIRS - 1, PAIRS + 1, 2, lambda s, u: combine(dve, s, u))

        @block.tensor
        def _(pe):
            mm = nc.tensor.matmul
            pe.wait_ge(ev("ident_ready"), 1)
            pe.wait_ge(ev("comp_ready"), 1)
            for v in range(2):
                pe.transpose(bank[0][:, v * P:v * P + P], comp_d[:, v, :, :].rearrange("p c d -> p (c d)"), ident[:, :])
            pe.transpose(bank[0][0:D, 256:256 + OPS], op_raw, ident[0:OPS, 0:OPS]).then_inc(ev("comp_turned"), 1)
            pe.wait_ge(ev("comp_copied"), 1)
            for side in range(2):
                half = slice(side * D, side * D + D)
                for v in range(2):
                    mm(bank[1 + 2 * side][:, v * D:v * D + D], comp_t[half, v, :], w_lr[half, :], start=True, stop=True)
            mm(bank[2][0:OPS, 0:D], op_t, w_op, start=True, stop=False)
            mm(bank[2][0:OPS, 0:D], ones_row[:, 0:OPS], bc_row, start=False, stop=True).then_inc(ev("tables"), 1)
            pe.wait_ge(ev("tables_split"), 1)

            def spread(s, u):
                pe.wait_ge(ev("ids_picked"), 2 * s + u + 1)
                if not isinstance(s, int) or 2 * s + u > 0:
                    pe.wait_ge(ev("ids_copied"), 2 * s + u)
                for i, (lo, hi) in enumerate(ID_PARTS):
                    ins = mm(bank[i][:, 0:hi - lo], ones16[:, :], ids_one[:, lo:hi], start=True, stop=True)
                ins.then_inc(ev("ids_bc"), 1)

            def op_terms(o, hot, rows):
                for piece in range(3):
                    mm(o, hot, tab_op[0:rows, piece, :], start=piece == 0, stop=False)

            def level0(s):
                pe.wait_ge(ev("hot"), 2 * s + 2)
                need(pe, ev("normed0"), s)
                for u in range(2):
                    for k in range(4):
                        o = LV[0][:, 4 * u + k, :]
                        op_terms(o, op_hot[:, u, k * P:k * P + P], OPS)
                        for side in range(2):
                            for v in range(2):
                                for piece in range(3):
                                    leaf = 2 * k + side
                                    ins = mm(o, leaf_hot[:, u, v, leaf * P:leaf * P + P], tab[:, side, v, piece, :],
                                             start=False, stop=side == v == 1 and piece == 2)
                ins.then_inc(ev("level0"), 1)

            def turn(level, s, dst):
                pe.wait_ge(ev(f"leveled{level}"), s + 1)
                if level == 0:
                    need(pe, ev("kids1_copied"), s - 1)
                else:
                    pe.wait_ge(ev("kids0_copied"), min(s + 2, TS) if isinstance(s, int) else s + 2)
                n = 4 >> level
                src = lv_g[level].rearrange("p (a b) d -> p a (b d)", b=2)
                for i in range(n):
                    ins = pe.transpose(dst[:, i * P:i * P + P], src[:, i, :], ident[:, :])
                ins.then_inc(ev(f"kids{level}"), 1)

            def upper(level, s, kids):
                pe.wait_ge(ev(f"kids{level - 1}_copied"), s + 1)
                need(pe, ev(f"normed{level}"), s)
                nodes = 4 >> level
                for u in range(2):
                    for k in range(nodes):
                        o = LV[level][:, nodes * u + k, :]
                        k3 = (0 if level == 1 else 2) + k
                        op_terms(o, up_hot[:, bass.ds(2 * (s % 4) + u, 1), k3 * P:k3 * P + P].rearrange(
                            "p a b -> p (a b)"), P)
                        ins = mm(o, kids[:, nodes * u + k, :], w_lr, start=False, stop=True)
                ins.then_inc(ev(f"level{level}"), 1)

            def tree(s, _):
                if within(s - 1, 0, TS):
                    turn(0, s - 1, bank[5][:, :])
                if within(s - 2, 0, TS):
                    turn(1, s - 2, bank[5][:, 0:256])
                if within(s, 0, TS):
                    level0(s)
                if within(s - 1, 0, TS):
                    upper(1, s - 1, kids1)
                if within(s - 2, 0, TS):
                    upper(2, s - 2, kids2)
                if within(s + 1, 0, TS):
                    spread(s + 1, 0)
                    spread(s + 1, 1)
            spread(0, 0)
            spread(0, 1)
            slots(pe, 0, 3, TS - 1, TS + 2, 1, tree)

            pe.wait_ge(ev("tok_loaded"), 96)
            pe.wait_ge(ev("zeros_ready"), 1)
            steps = (PW + 1) // 2
            for b in range(2):
                for c in range(steps):
                    last = c == steps - 1
                    rows = slice(0, PH if last else P)
                    ins = mm(bank[0][b * D:b * D + D, 0:PAIRS * TOK], wt[rows, c, :],
                             xs[rows, b:B:2, 2 * c:2 * c + SW * (TOK - 1) + 1:SW], start=c == 0, stop=last)
            ins.then_inc(ev("tok_mm"), 1)
            pe.wait_ge(ev("tok_split"), 1)
            for t in range(PAIRS):
                ins = mm(bank[1 + t // 8][0:2 * TOK, (t % 8) * D:(t % 8) * D + D],
                         tok_m[:, t, :, :].rearrange("p a b -> p (a b)"), ident2[:, :], start=True, stop=True)
                if t % 8 == 7:
                    ins.then_inc(ev("tok_rows"), 1)

            pe.wait_ge(ev("weights_loaded"), 16 * WLOADS)
            for i in range(4):
                ins = pe.transpose(bank[5][:, i * D:i * D + D], wn[:, i, :, :].rearrange("p a b -> p (a b)"), ident[0:D, 0:D])
            ins.then_inc(ev("w_turned"), 1)
            pe.wait_ge(ev("conv_ready"), 1)
            mm(bank[6][:, 0:H], pick_sq[:, :], conv_a[:, :], start=True, stop=True)
            mm(bank[6][0:D, H:2 * H], pick_lin[:, :], conv_a[:, :], start=True, stop=True)
            mm(bank[6][:, 16:17], conv_x[:, :], bn_inv[:, 3:4], start=True, stop=False)
            mm(bank[6][:, 16:17], cb_x[:, :], ones_col[0:1, :], start=False, stop=True).then_inc(ev("conv_mm"), 1)
            pe.wait_ge(ev("weights_ready"), 1)

            def first(s, u):
                p1 = 1 - u
                if within(s, 0, PAIRS):
                    pe.wait_ge(ev("staged"), s + 1)
                    need(pe, ev("hs_ready"), s - 1)
                    pe.transpose(bank[u][:, 0:TXT], st_txt[u].rearrange("p a b -> p (a b)"), ident[:, :])
                    pe.transpose(bank[u][:, TXT:TXT + 2 * TOK], st_tok[u].rearrange("p a b -> p (a b)"),
                                 ident[0:2 * TOK, 0:2 * TOK]).then_inc(ev("hs_mm"), 1)
                if within(s - 1, 0, PAIRS):
                    pe.wait_ge(ev("hs_ready"), s)
                    need(pe, ev("qk_ready"), s - 2)
                    w = wqk_pair[:, :, :].rearrange("p a b -> p (a b)")
                    mm(bank[2 + p1][:, 0:2 * P], hs[p1][:, 0:TXT], w, start=True, stop=True)
                    mm(bank[4 + p1][0:TOK, 0:2 * P], hs[p1][:, TXT:N], w, start=True, stop=True).then_inc(ev("qk_mm"), 1)
                if within(s - 2, 0, PAIRS):
                    pe.wait_ge(ev("qk_ready"), s - 1)
                    need(pe, ev("gm_ready"), s - 3)
                    for b in range(2):
                        o = bank[6 + u][:, b * P:b * P + P]
                        mm(o, qkn[u][:, b, :], qkn[u][:, b, :], start=True, stop=False)
                        ins = mm(o, qkt[u][:, b, :], qkt[u][:, b, :], start=False, stop=True)
                    ins.then_inc(ev("gram_mm"), 1)
            slots(pe, 0, 5, PAIRS - 1, PAIRS + 2, 2, first)

            pe.wait_ge(ev("gall_ready"), PAIRS)
            pe.wait_ge(ev("top_ready"), 1)
            for c in range(HD):
                mm(bank[0][:, c * D:c * D + D], gall[:, c].rearrange("p a b c -> p (a b c)"), ident2[:, :],
                   start=True, stop=True)
            for r in range(QB):
                for x in range(2):
                    ins = mm(bank[1][:, r * D:r * D + D], top[:, x, r].rearrange("p a b c -> p (a b c)"),
                             wqk_top[:, x, :], start=x == 0, stop=x == 1)
            ins.then_inc(ev("qr_mm"), 1)
            pe.wait_ge(ev("mx_done"), 1)
            for i in range(HD):
                ins = pe.transpose(bank[2 + i // 4][:, (i % 4) * P:(i % 4) * P + P],
                                   mx[:, i].rearrange("p a b c -> p (a b c)"), ident[:, :])
            ins.then_inc(ev("bases_mm"), 1)
            pe.wait_ge(ev("bases_ready"), 4)

            def attention(s, u):
                t1, p1 = s + 1, 1 - u
                prep = within(t1, 0, PAIRS)
                a, b1, b2 = within(s, 0, PAIRS), within(s - 1, 0, PAIRS), within(s - 2, 0, PAIRS)

                def dots(j):
                    if j == 0:
                        pe.wait_ge(ev("k_diag"), 16 * G * (s + 1))
                        pe.wait_ge(ev("q2_ready"), s + 1)
                    for b in range(2):
                        need(pe, ev("sq_done"), 2 * NG * s + 2 * j + b - 1)
                        keys = kbd[u][:, b].rearrange("p g m -> p (g m)")
                        for i, tile in enumerate(GROUPS[j]):
                            ins = mm(bank[b][:, i * N:i * N + N], keys[:, tile:tile + TILES * (P - 1) + 1:TILES],
                                     qq[u][:, b, :], start=True, stop=True)
                        ins.then_inc(ev("dg_done"), 1)

                def mixed(j):
                    pe.wait_ge(ev("sq_done"), 2 * NG * s + 2 * j + 2)
                    need(pe, ev("scores_out"), NG * s + j - 1)
                    if j == 0:
                        pe.wait_ge(ev("lin_ready"), s + 1)
                    for i, tile in enumerate(GROUPS[j]):
                        cols = slice(i * N, i * N + N)
                        for b in range(2):
                            mm(bank[2 + j % 2][b * D:b * D + D, cols], mix[:, :], sq[b][j % 2][:, cols],
                               start=True, stop=False)
                        for b in range(2):
                            keys = linb[u][:, b].rearrange("p o m -> p (o m)")
                            ins = mm(bank[2 + j % 2][b * D:b * D + D, cols],
                                     keys[:, tile:tile + TILES * (D - 1) + 1:TILES], qq[u][:, b, :],
                                     start=False, stop=True)
                    ins.then_inc(ev("lg_done"), 1)

                def turn_values(r):
                    if r == 0:
                        pe.wait_ge(ev("v_diag"), 16 * G * (s + 1))
                    if r == 1 and prep:
                        pe.wait_ge(ev("q2_ready"), t1 + 1)
                    need(pe, ev("vt_copied"), NVT * s + r - 1)
                    flat = vbt.rearrange("p g m -> p (g m)")
                    for i, tile in enumerate(VTS[r]):
                        ins = pe.transpose(bank[5 + r % 2][:, i * P:i * P + P], flat[:, tile:tile + TILES * (P - 1) + 1:TILES],
                                           ident[:, :])
                    ins.then_inc(ev("vt_done"), 1)

                for j in range(NG):
                    if a:
                        dots(j)
                        if j:
                            mixed(j - 1)
                    if j == 0 and prep:
                        need(pe, ev("q2_ready"), t1)
                        need(pe, ev("vt_copied"), NVT * s)
                        for b in range(2):
                            ins = mm(bank[6][:, b * N:b * N + N], wq_dup[:, b, :],
                                     hn_t[:, bass.ds(t1, 1), :].rearrange("p a b -> p (a b)"), start=True, stop=True)
                        ins.then_inc(ev("q_mm"), 1)
                        for b in range(2):
                            ins = mm(bank[5][:, b * N:b * N + N], wk_dup[:, b, :],
                                     hn_t[:, bass.ds(t1, 1), :].rearrange("p a b -> p (a b)"), start=True, stop=True)
                        ins.then_inc(ev("k_mm"), 1)
                    if j == 0 and b2:
                        pe.wait_ge(ev("ot_ready"), s - 1)
                        need(pe, ev("router_out"), s - 2)
                        mm(bank[7][:, 0:P], ot[:, 0:TXT], wp_pair[:, :], start=True, stop=False)
                        mm(bank[7][:, 0:P], ones_row[:, :], bp_row[:, :, :].rearrange("p a b -> p (a b)"), start=False, stop=True)
                        mm(bank[7][0:2 * TOK, P:P + D], ot5.rearrange("p a b -> p (a b)"), wp_both[:, :], start=True, stop=False)
                        mm(bank[7][0:2 * TOK, P:P + D], ones_row[:, 0:2 * TOK], bp_row[:, 0, :], start=False,
                           stop=True).then_inc(ev("pr_done"), 1)
                    if j == 1 and prep:
                        pe.wait_ge(ev("q_copied"), t1 + 1)
                        mm(bank[6][:, 0:N], wv_pair[:, :], hn_t[:, bass.ds(t1, 1), :].rearrange("p a b -> p (a b)"),
                           start=True, stop=True).then_inc(ev("v_mm"), 1)
                        pe.wait_ge(ev("k_copied"), t1 + 1)
                        pe.wait_ge(ev("mq_ready"), t1 + 1)
                        for b in range(2):
                            ins = mm(bank[5][:, b * D:b * D + D], mqx[p1][:, b].rearrange("p a b c -> p (a b c)"),
                                     mkx[p1].rearrange("p a b -> p (a b)"), start=True, stop=True)
                        ins.then_inc(ev("p_mm"), 1)
                    if j == 1 and b1:
                        pe.wait_ge(ev("mx_ready"), s)
                        need(pe, ev("h_added"), s - 1)
                        pe.transpose(bank[7][:, 0:P], mxv[:, 0:TXT], ident[:, :])
                        pe.transpose(bank[7][0:TOK, P:2 * P], mxv[:, TXT:N], ident[:, :]).then_inc(ev("t1_done"), 1)
                    if j == 2 and b1:
                        pe.wait_ge(ev("mn_ready"), s)
                        pe.transpose(bank[7][:, 0:TXT], mnx.rearrange("p a b -> p (a b)"), ident[:, :])
                        pe.transpose(bank[7][:, TXT:N], mnx5.rearrange("p a b -> p (a b)"),
                                     ident[0:TOK, 0:TOK]).then_inc(ev("t2_done"), 1)
                    if j == 2 and prep:
                        pe.wait_ge(ev("p_copied"), t1 + 1)
                        pe.wait_ge(ev("v_copied"), t1 + 1)
                        for b in range(2):
                            ins = mm(bank[6][D:P, b * N:b * N + N], pm[p1][:, b, :], qq[p1][:, b, :],
                                     start=True, stop=True)
                        ins.then_inc(ev("q2_mm"), 1)
                    if j == 3 and b2:
                        pe.wait_ge(ev("hn2_rows"), s - 1)
                        pe.wait_ge(ev("sub_done"), min(s, PAIRS) if isinstance(s, int) else s)
                        pe.transpose(bank[7][:, 0:TXT], hn2.rearrange("p a b -> p (a b)"), ident[:, :])
                        pe.transpose(bank[7][:, TXT:TXT + 2 * TOK], hn2k.rearrange("p a b -> p (a b)"),
                                     ident[0:2 * TOK, 0:2 * TOK]).then_inc(ev("t4a_done"), 1)
                    if j == 3 and a:
                        turn_values(0)
                        turn_values(1)
                    if j == 4 and b2:
                        pe.wait_ge(ev("hs2_ready"), s - 1)
                        mm(bank[7][:, 0:2 * EXPERTS], hs2[u][:, 0:TXT], wr_pair[:, :, :].rearrange("p a b -> p (a b)"),
                           start=True, stop=True)
                        mm(bank[7][0:2 * TOK, 2 * EXPERTS:3 * EXPERTS], tk10[u].rearrange("p a b -> p (a b)"),
                           wr_both[:, :], start=True, stop=True).then_inc(ev("t4b_done"), 1)
                    if j == 4 and a:
                        turn_values(2)
                        turn_values(3)
                    if j == 5 and a:
                        turn_values(4)
                if b1:
                    pe.wait_ge(ev("exp_done"), s)
                    need(pe, ev("ot_ready"), s - 1)
                    for tile in range(TILES):
                        mm(bank[4][:, 0:N], vbd[p1][:, tile, :], ll[p1][:, tile, :], start=tile == 0,
                           stop=tile == TILES - 1)
                    pe.wait_ge(ev("es_ready"), s)
                    mm(bank[4][:, N:2 * N], group_ones[:, :], es, start=True, stop=True).then_inc(ev("av_done"), 1)
                if a:
                    mixed(NG - 1)
            slots(pe, -1, 5, PAIRS - 1, PAIRS + 2, 2, attention)

            pe.wait_ge(ev("hn2_ready"), PAIRS)
            pe.wait_ge(ev("router_out"), PAIRS)
            pe.wait_ge(ev("weights_split"), 1)

            def experts(s, u):
                t1, p1 = s + 1, 1 - u

                def up(c):
                    if c == 0:
                        pe.wait_ge(ev("x_piece"), 4 * s + 4)
                    need(pe, ev("gelu_done"), CH * s + c - 2)
                    for k, x in enumerate((x12, x12, x13)):
                        ins = mm(bank[c % 3][:, 0:2 * N], w1_split[:, k, c // 2, (c % 2) * P:(c % 2) * P + P],
                                 x[u], start=k == 0, stop=k == 2)
                    ins.then_inc(ev("w1_done"), 1)

                def masks(e):
                    if e == 0:
                        pe.wait_ge(ev("mt_ready"), s + 1)
                    need(pe, ev("weighted"), EXPERTS * s + e - 1)
                    mm(bank[4 + 2 * (e % 2)][:, 0:2 * N], sel_e[:, e, :], mt[u].rearrange("p a b -> p (a b)"),
                       start=True, stop=True).then_inc(ev("mask_mm"), 1)

                def down(e):
                    if e < EXPERTS:
                        pe.wait_ge(ev("weighted"), EXPERTS * s + e + 1)
                    else:
                        pe.wait_ge(ev("gelu_done"), CH * s + CH)
                    if e == 0:
                        need(pe, ev("y_copied"), s)
                    for c in range(2):
                        for b in range(2):
                            ins = mm(bank[5][b * D:b * D + D, 0:N], w2_s[:, e, c, :], hg[e % HG][:, c, b * N:b * N + N],
                                     start=e == 0 and c == 0, stop=e == EXPERTS and c == 1)
                        for k in range(3 if e == c == 0 else 0):
                            for b in range(2):
                                mm(bank[5][b * D:b * D + D, 0:N], b2_split[:, k, :], mt[u][:, b, :], start=False, stop=False)
                    ins.then_inc(ev("w2_done"), 1)
                    if e == EXPERTS:
                        mm(bank[5][:, 2 * N:2 * N + 1], ident[:, :], ones_col[:, :], start=True, stop=True).then_inc(ev("y_mm"), 1)

                for e in range(EXPERTS + 3):
                    if within(s, 0, PAIRS):
                        if e <= EXPERTS:
                            up(2 * e)
                            up(2 * e + 1)
                        if e < EXPERTS:
                            masks(e)
                    if e == 0 and within(s - 1, 0, PAIRS):
                        pe.wait_ge(ev("y_copied"), s)
                        pe.wait_ge(ev("mt_ready"), min(s + 1, PAIRS) if isinstance(s, int) else s + 1)
                        pe.transpose(bank[7][:, 0:P], yt_sb[:, 0:TXT], ident[:, :])
                        mm(bank[7][0:2 * TOK, P:P + D], yk.rearrange("p a b -> p (a b)"), ident2[:, :],
                           start=True, stop=True).then_inc(ev("y_turned"), 1)
                    if e == 3 and within(t1, 0, PAIRS):
                        pe.wait_ge(ev("w_staged"), t1 + 1)
                        need(pe, ev("y_out"), t1 - 1)
                        pe.transpose(bank[7][:, 0:TXT], st_w[p1].rearrange("p a b -> p (a b)"), ident[:, :])
                        pe.transpose(bank[7][0:D, TXT:TXT + 2 * TOK], st_wk[p1].rearrange("p a b -> p (a b)"),
                                     ident[0:2 * TOK, 0:2 * TOK]).then_inc(ev("w_turned2"), 1)
                        need(pe, ev("x_piece"), 4 * t1)
                        for b in range(2):
                            ins = mm(bank[3][:, b * N:b * N + N], dup[:, b, :],
                                     hn_t[:, bass.ds(t1, 1), :].rearrange("p a b -> p (a b)"), start=True, stop=True)
                        ins.then_inc(ev("x_mm"), 1)
                    if within(s, 0, PAIRS) and e >= 2:
                        down(e - 2)
            slots(pe, -1, 3, PAIRS - 1, PAIRS + 1, 2, experts)


WLOADS = 2 * 11 + 1 + 2 * 4 + 8 + 1 + 4 + 3 + 1
NVT = -(-TILES // 4)
VTS = [range(r, min(r + 4, TILES)) for r in range(0, TILES, 4)]
ID_PARTS = ((0, 512), (512, 1024), (1024, 1024 + 448), (1024 + 448, LEAFC + OPC))


_OUTS = [((B, N, D), "float32")]
_PREFIXES = ("L0_tok_", "L0_txt_", "L0_attn_", "L0_ffn_")


def _short(name):
    for p in _PREFIXES[1:]:
        if name.startswith(p):
            return name[len(p):]
    return name.replace("L0_", "")


def kernel(**inputs):
    import numpy as _np
    import concourse.bacc as _bacc
    from concourse import mybir as _mybir
    from concourse.bass_utils import run_bass_kernel_spmd as _run

    nc = _bacc.Bacc("TRN2", target_bir_lowering=False, num_devices=1)
    arrays, aps = {}, {}
    for name, value in inputs.items():
        v = _np.ascontiguousarray(value)
        if v.ndim == 0:
            v = v.reshape(1)
        arrays[f"in_{name}_dram"] = v
        aps[_short(name)] = nc.dram_tensor(f"in_{name}_dram", v.shape, _mybir.dt.from_np(v.dtype),
                                           kind="ExternalInput").ap()
    out = nc.dram_tensor("out_0_dram", _OUTS[0][0], F32, kind="ExternalOutput").ap()
    build(nc, aps, out)
    r = _run(nc, [arrays], core_ids=[0])
    return r.results[0]["out_0_dram"]
```

```python
from contextlib import ExitStack

import concourse.bass as bass
from concourse import mybir

F32 = mybir.dt.float32
BF16 = mybir.dt.bfloat16
I32 = mybir.dt.int32
ACT = mybir.ActivationFunctionType
ALU = mybir.AluOpType
AX = mybir.AxisListType

P = 128
D = 64
B = 64
PAIRS = B // 2
TXT, TOK = 128, 5
N = TXT + TOK
NP = 136
H, HD = 8, 8
QB = HD
G = 2 * H
TILES = NP // 8
GROUPS = [range(j, min(j + 3, TILES)) for j in range(0, TILES, 3)]
NG = len(GROUPS)
PH, PW, SW, PX = 64, 25, 12, 84
STRUCTS, LEAVES, INNER = 2048, 8, 7
OPS, VOCAB = 64, 256
ST = STRUCTS // P
TS = ST // 2
LEAFC, OPC = LEAVES * P, INNER * P
EXPERTS, FF = 8, 256
CH = (EXPERTS + 1) * FF // P
EPS = 1e-5
MASKED = -1.0e30
HG = 4


def need(eng, sem, value):
    if isinstance(value, int) and value <= 0:
        return
    eng.wait_ge(sem, value)


def within(t, lo, hi):
    return not isinstance(t, int) or lo <= t < hi


def slots(eng, first, lo, hi, last, step, body):
    for t in range(first, lo):
        body(t, t % step)
    assert (hi - lo) % step == 0
    with eng.Fori(0, (hi - lo) // step) as i:
        for u in range(step):
            body(step * i + (lo + u), (lo + u) % step)
    for t in range(hi, last):
        body(t, t % step)


class Chain:

    def __init__(self, eng, sem):
        self.eng, self.sem, self.count = eng, sem, 0

    def step(self, ins):
        ins.then_inc(self.sem, 1)
        self.count += 1
        self.eng.wait_ge(self.sem, self.count)


def build(nc, a, out):
    ctx = ExitStack()
    with ctx:
        ctx.enter_context(nc.allow_non_contiguous_dma(reason="strided loads of weights and indices"))

        def sb(name, shape, dt=F32):
            return ctx.enter_context(nc.sbuf_tensor(name, shape, dt))

        def sem(name):
            return ctx.enter_context(nc.semaphore(name))

        bank = [ctx.enter_context(nc.psum_tensor(f"bank{i}", [P, 512], F32)) for i in range(8)]
        root_dram = nc.dram_tensor("root_table", [STRUCTS, D], F32, kind="Internal").ap()

        ident = sb("ident", [P, P])
        ident2 = sb("ident2", [P, D])
        group_of = sb("group_of", [P, G])
        head_of = sb("head_of", [P, H])
        lane_of = sb("lane_of", [P, 8])
        group_ones = sb("group_ones", [P, P])
        ones_row = sb("ones_row", [1, P])
        ones_col = sb("ones_col", [P, 1])
        ones16 = sb("ones16", [ST, P], BF16)
        iota_col = sb("iota_col", [P, 2])
        eps_col = sb("eps_col", [P, 1])
        minus_half = sb("minus_half", [P, 4])

        h_txt = sb("h_txt", [P, B, D])
        h_tok = sb("h_tok", [2 * TOK, PAIRS, D])
        hn_t = sb("hn_t", [P, PAIRS, N])

        wn = sb("wn", [D, 4, 2, D])
        wq_dup = sb("wq_dup", [P, 2, P])
        wk_dup = sb("wk_dup", [P, 2, P])
        wv_pair = sb("wv_pair", [P, P])
        wqk_pair = sb("wqk_pair", [P, 2, P])
        wqk_top = sb("wqk_top", [P, 2, D])
        wp_pair = sb("wp_pair", [P, P])
        wp_both = sb("wp_both", [P, D])
        wr_both = sb("wr_both", [P, EXPERTS])
        wr_pair = sb("wr_pair", [P, 2, EXPERTS])
        b_qkv = sb("b_qkv", [P, 3])
        b_qk_rows = sb("b_qk_rows", [P, P])
        b_top = sb("b_top", [P, D])
        bp_row = sb("bp_row", [1, 2, D])
        w1_split = sb("w1_split", [P, 3, EXPERTS + 1, FF], BF16)
        w2_s = sb("w2_s", [P, EXPERTS + 1, 2, D])
        b1_col = sb("b1_col", [P, EXPERTS + 1, 2])
        b2_rows = sb("b2_rows", [D, D])
        b2_split = sb("b2_split", [D, 3, D], BF16)
        b2s_col = sb("b2s_col", [P, 1])
        sel_e = sb("sel_e", [D, EXPERTS, P], BF16)
        conv_t = sb("conv_t", [3 * H, H])
        bn = sb("bn", [3 * H, 4])
        score_scale = sb("score_scale", [3 * H, 1])
        bn_inv = sb("bn_inv", [3 * H, 4])
        conv_a = sb("conv_a", [3 * H, H])
        pick_sq = sb("pick_sq", [3 * H, P])
        pick_lin = sb("pick_lin", [3 * H, D])
        conv_x = sb("conv_x", [3 * H, P])
        cb_row = sb("cb_row", [1, H])
        cb_x = sb("cb_x", [1, P])
        mix = sb("mix", [P, D])
        lin_a = sb("lin_a", [D, H])
        score_c = sb("score_c", [P, 2])
        bases = sb("bases", [P, PAIRS, 2, HD])
        router = sb("router", [P, B, EXPERTS])
        router_tok = sb("router_tok", [2 * TOK, PAIRS, EXPERTS])
        countdown = sb("countdown", [P, EXPERTS])

        ARENA = 32700
        QR_END, TREE_END = 7700, 14800
        arena = sb("arena", [P, ARENA])

        def carver(start=0, end=ARENA):
            at = [start]

            def carve(shape, dt=F32, parts=P):
                n = 1
                for s in shape:
                    n *= s
                words = n if dt != BF16 else (n + 1) // 2
                v = arena[0:parts, at[0]:at[0] + words]
                at[0] += words
                assert at[0] <= end, at[0]
                if dt != F32:
                    v = v.bitcast(dt)
                names = "abcde"[:len(shape)]
                if len(shape) > 1:
                    v = v.rearrange(f"p ({' '.join(names)}) -> p {' '.join(names)}",
                                    **dict(zip(names, shape)))
                return v
            carve.used = at
            return carve

        one = carver()
        ids_raw = one([LEAFC + OPC], I32, ST)
        ids_all = one([LEAFC + OPC], BF16, ST)
        leaf_hot = one([2, 2, LEAFC], BF16)
        op_hot = one([2, 4 * P], BF16, OPS)
        up_hot = one([8, 3 * P], BF16)
        comp = one([2, D])
        comp_sq = one([2, D])
        comp_d = one([2, 2, D])
        comp_st = one([4, 2])
        comp_t = one([2, P])
        gamma_bc = one([D])
        beta_bc = one([D])
        op_raw = one([D], F32, OPS)
        op_t = one([OPS], F32, D)
        w_op = one([D], F32, D)
        w_lr = one([D])
        w_mean = one([4])
        bc_row = one([D], F32, 1)
        tab = one([2, 2, 3, D], BF16)
        tab_op = one([3, D], BF16)
        tab_f = one([5, D])
        tab_r = one([5, D])
        lv_sq = [one([8, D]), one([4, D]), one([2, D])]
        lv_var = [one([8]), one([4]), one([2])]
        lv_std = [one([8]), one([4]), one([2])]
        lv_inv = [one([8]), one([4]), one([2])]
        lv_h = [one([8, D]), one([4, D]), one([2, D])]
        lv_g = [one([8, D]), one([4, D]), one([2, D])]
        kids1 = one([4, P])
        root_scratch = one([1])
        kids2 = one([2, P])
        one.used[0] = max(one.used[0], TREE_END)
        txt_idx = one([B], I32)
        xs = one([B, PX])
        wt = one([(PW + 1) // 2, D])
        btok = one([1])
        tok_t = one([PAIRS, TOK])
        tok_m = one([PAIRS, 2, TOK])
        ln_s = one([B])
        ln_m = one([B])
        ln_v = one([B])
        ln_d = one([B])
        ln_r = one([B])
        hn_txt = one([B, D])
        hn_tok = one([PAIRS, D], F32, 2 * TOK)
        ln_sq = xs.rearrange("p a b -> p (a b)")[:, 0:B * D].rearrange("p (a b) -> p a b", a=B)
        st_txt = [one([2, D]) for _ in range(2)]
        st_tok = [one([2, D], F32, 2 * TOK) for _ in range(2)]
        hs = [one([NP]) for _ in range(2)]
        qkn = [one([2, P]) for _ in range(2)]
        qkt = [one([2, P], F32, TOK) for _ in range(2)]
        gm = [one([2, H, HD]) for _ in range(2)]
        b2_r = one([D], F32, D)
        ids_v = hn_txt.rearrange("p a b -> p (a b)")[:, 0:2 * (LEAFC + OPC)].bitcast(BF16).rearrange(
            "p (k u c) -> p k u c", k=2, u=2)
        ids_one = [ids_v[0:ST, 0, u, :] for u in range(2)]
        ids_bc = [ids_v[:, 1, u, :] for u in range(2)]
        w1_f = one([EXPERTS + 1, FF])

        qr = carver()
        gall = qr([HD, 2, 2, PAIRS])
        top = qr([QB, 2, PAIRS])
        ym = qr([H, 3 * HD, HD])
        yt = qr([H * 3 * HD * (HD - 1)])
        qsd = qr([H])
        qri = qr([H])
        um = qr([H, HD, HD])
        sg = qr([H, HD])
        piv = qr([H])
        pinv = qr([H])
        ucol = qr([H, HD])
        mx = qr([HD, 2, H, HD])
        assert qr.used[0] <= QR_END
        w1_r = carver(QR_END, TREE_END)([EXPERTS + 1, FF])

        two = carver(QR_END, TREE_END)
        linb = [two([2, H, NP]) for _ in range(2)]
        qq = [two([2, N]) for _ in range(2)]
        kk = [two([2, NP]) for _ in range(2)]
        vv = [two([NP]) for _ in range(2)]
        pm = [two([2, D]) for _ in range(2)]
        mqx = [two([2, 2, H, HD]) for _ in range(2)]
        mkx = [two([H, HD]) for _ in range(2)]
        tk10 = [two([2, TOK]) for _ in range(2)]
        ot5 = two([2, TOK])
        mv = two([3, 2])
        two = carver(TREE_END)
        kbd = [two([2, G, NP]) for _ in range(2)]
        vbt = two([G, NP])
        vbd = [two([TILES, P]) for _ in range(2)]
        two = carver(0, QR_END)
        ll = [two([TILES, N]) for _ in range(2)]
        sq = [[two([3 * N]) for _ in range(2)] for _ in range(2)]
        mxv = two([N])
        mn = two([G])
        mn5 = two([G], F32, TOK)
        mnx = two([G, 8])
        mnx5 = two([G, 8], F32, TOK)
        es = two([N])
        rec = two([N])
        ot = two([N])
        gate = two([2])
        st6 = two([3, 6])
        ve = two([3])
        rs = two([3])
        hn2 = two([2, D])
        hn2k = two([2, D], F32, 2 * TOK)
        hs2 = [two([N]) for _ in range(2)]
        rt_logit = two([3, EXPERTS])
        rt_x = two([3, EXPERTS])
        rt_m = two([3])
        rt_w = two([3, EXPERTS])
        rt_first = two([3, EXPERTS])
        rt_left = two([3, EXPERTS])

        three = carver()
        rt_16 = three([B, EXPERTS], BF16)
        rt_16k = three([PAIRS, EXPERTS], BF16, 2 * TOK)
        wsp = three([B, 4, EXPERTS])
        wsp_tok = three([PAIRS, 4, EXPERTS], F32, 2 * TOK)
        st_w = [three([2, D]) for _ in range(2)]
        st_wk = [three([2, 4 * EXPERTS], F32, 2 * TOK) for _ in range(2)]
        mt = [three([2, N], BF16, D) for _ in range(2)]
        dup = three([2, P])
        x12 = [three([2 * N], BF16) for _ in range(2)]
        x13 = [three([2 * N], BF16) for _ in range(2)]
        x_r = three([2 * N])
        hg = [three([2, 2 * N]) for _ in range(HG)]
        yt_sb = three([N])
        yk = three([2, TOK])
        yo = [three([D]) for _ in range(3)]

        E = {}

        def ev(name):
            if name not in E:
                E[name] = sem(name)
            return E[name]

        LV = [bank[4][:, :].rearrange("p (n d) -> p n d", d=D),
              bank[6][:, 0:256].rearrange("p (n d) -> p n d", d=D),
              bank[7][:, 0:P].rearrange("p (n d) -> p n d", d=D)]

        def ln_slice(g):
            if g == 0:
                r, c, h, hn = slice(0, 2 * TOK), slice(0, PAIRS), h_tok[:, :, :], hn_tok
            else:
                r, c = slice(0, P), slice(16 * (g - 1), 16 * g)
                h, hn = h_txt[:, c, :], hn_txt[:, c, :]
            parts, n = r.stop, c.stop - c.start
            return dict(parts=parts, shape=[parts, n, D], h=h, hn=hn, sq=ln_sq[r, c, :],
                        **{k: v[r, c] for k, v in dict(s=ln_s, m=ln_m, v=ln_v, d=ln_d, r=ln_r).items()})

        def weights(dve, ch):
            nc.vector.tensor_reduce(lane_of[:, :], ident[:, :].rearrange("p (g k) -> p k g", g=G), AX.X, ALU.add)
            ch.step(nc.vector.tensor_reduce(group_of[:, :], ident[:, :].rearrange("p (g k) -> p g k", g=G), AX.X, ALU.add))
            nc.vector.tensor_tensor(head_of[:, :], group_of[:, 0:H], group_of[:, H:G], ALU.add)
            nc.vector.tensor_copy(group_ones[:, :].rearrange("p (g k) -> p g k", g=G),
                                  group_of[:, :].unsqueeze(2).to_broadcast([P, G, 8]))
            dve.wait_ge(ev("w_turned"), 1)
            turned = [bank[5][:, i * D:i * D + D] for i in range(4)]
            for b in range(2):
                half, cols = slice(b * D, b * D + D), slice(b * D, b * D + D)
                for c in range(2):
                    nc.vector.tensor_copy(wq_dup[half, b, c * D:c * D + D], turned[0][half])
                    nc.vector.tensor_copy(wk_dup[half, b, c * D:c * D + D], turned[1][half])
                    nc.vector.tensor_copy(wqk_pair[half, b, c * D:c * D + D], turned[c][half])
                nc.vector.tensor_copy(wv_pair[half, cols], turned[2][half])
                nc.vector.tensor_copy(wp_pair[half, cols], turned[3][half])
                nc.vector.tensor_copy(wqk_top[:, b, :], turned[b])
                nc.vector.tensor_copy(wr_pair[half, b, :], wr_both[half, :])
            nc.vector.tensor_copy(wp_both[:, :], turned[3])
            nc.vector.tensor_copy(conv_x[:, :].rearrange("c (b o k) -> c b o k", b=2, o=H),
                                  conv_t[:, :].unsqueeze(1).unsqueeze(3).to_broadcast([3 * H, 2, H, 8]))
            nc.vector.tensor_copy(cb_x[:, :].rearrange("c (b o k) -> c b o k", b=2, o=H),
                                  cb_row[:, :].unsqueeze(1).unsqueeze(3).to_broadcast([1, 2, H, 8]))
            ch.step(nc.vector.tensor_copy(b2_split[:, 0], b2_rows[:, :]))
            ch.step(nc.vector.tensor_tensor(b2_r, b2_rows[:, :], b2_split[:, 0], ALU.subtract))
            ch.step(nc.vector.tensor_copy(b2_split[:, 1], b2_r))
            nc.vector.tensor_tensor(b2_split[:, 2], b2_r, b2_split[:, 1], ALU.subtract)
            nc.vector.tensor_copy(sel_e[:, :, :], lane_of[0:D, :].unsqueeze(2).to_broadcast([D, EXPERTS, P]))
            dve.wait_ge(ev("bn_std"), 1)
            ch.step(nc.vector.reciprocal(bn_inv[:, 1:2], bn_inv[:, 0:1]))
            ch.step(nc.vector.tensor_tensor(bn_inv[:, 2:3], bn_inv[:, 1:2], bn[:, 0:1], ALU.mult))
            nc.vector.tensor_scalar(conv_a[:, :], conv_t[:, :], bn_inv[:, 2:3], score_scale[:, :], ALU.mult, ALU.mult)
            ch.step(nc.vector.tensor_tensor(bn_inv[:, 3:4], bn[:, 2:3], bn_inv[:, 2:3], ALU.mult))
            nc.vector.tensor_tensor(bn_inv[:, 3:4], bn[:, 1:2], bn_inv[:, 3:4], ALU.subtract).then_inc(ev("conv_ready"), 1)
            dve.wait_ge(ev("conv_mm"), 1)
            nc.vector.tensor_copy(lin_a[:, :], bank[6][0:D, 8:16])
            ch.step(nc.vector.tensor_copy(score_c[:, 0:1], bank[6][:, 16:17]))
            nc.vector.tensor_tensor(mix[:, :].rearrange("p (o k) -> p o k", o=H),
                                    bank[6][:, 0:H].unsqueeze(2).to_broadcast([P, H, 8]),
                                    lane_of[:, :].unsqueeze(1).to_broadcast([P, H, 8]), ALU.mult)
            nc.vector.scalar_tensor_tensor(score_c[:, 1:2], lane_of[:, 7:8], MASKED, score_c[:, 0:1], ALU.mult,
                                           ALU.add).then_inc(ev("weights_ready"), 1)

        def factorise(dve):
            cs = ev("qr_chain")
            n = [0]

            def step(ins):
                ins.then_inc(cs, 1)
                n[0] += 1
                dve.wait_ge(cs, n[0])
            nc.vector.memset(ym[:, :, 2 * HD:3 * HD, :], 0.0).then_inc(cs, 1)
            n[0] += 1
            dve.wait_ge(cs, 1)
            nc.vector.memset(ym.rearrange("p h r c -> p h (r c)")[:, :, 2 * HD * HD::HD + 1], 1.0)
            dve.wait_ge(ev("qr_mm"), 1)
            nc.vector.tensor_copy(ym[:, :, 0:HD, :], bank[0][:, :].rearrange("p (c h r) -> p h r c", c=HD, h=H))
            last = nc.vector.tensor_tensor(
                ym[:, :, HD:2 * HD, :], bank[1][:, :].rearrange("p (t h c) -> p h t c", t=QB, h=H),
                b_top[:, :].rearrange("p (h c) -> p h c", h=H).unsqueeze(2).to_broadcast([P, H, QB, HD]), ALU.add)
            for c in range(QB):
                last.then_inc(ev("pivot"), 1)
                dve.wait_ge(ev("pivot"), c + 1)
                dve.wait_ge(ev("pivot_root"), c + 1)
                step(nc.vector.reciprocal(qri, qsd))
                n_rows = 2 * HD + 1
                live = slice(c, c + n_rows)
                step(nc.vector.tensor_tensor(ym[:, :, live, c], ym[:, :, live, c],
                                             qri.unsqueeze(2).to_broadcast([P, H, n_rows]), ALU.mult))
                rest = HD - 1 - c
                if not rest:
                    break
                tmp = yt[:, 0:H * n_rows * rest].rearrange("p (h r k) -> p h r k", h=H, r=n_rows)
                shape = [P, H, n_rows, rest]
                step(nc.vector.tensor_tensor(tmp, ym[:, :, live, c].unsqueeze(3).to_broadcast(shape),
                                             ym[:, :, c + 1:HD, c].unsqueeze(2).to_broadcast(shape), ALU.mult))
                last = nc.vector.tensor_tensor(ym[:, :, live, c + 1:], ym[:, :, live, c + 1:], tmp, ALU.subtract)
            step(nc.vector.tensor_copy(um, ym[:, :, HD:2 * HD, :]))
            for c in range(QB):
                step(nc.vector.tensor_scalar(sg[:, :, c], um[:, :, c, c], 0.0, 0.5, ALU.is_ge, ALU.subtract))
                rest = HD - 1 - c
                if not rest:
                    break
                step(nc.vector.scalar_tensor_tensor(piv, sg[:, :, c], 2.0, um[:, :, c, c], ALU.mult, ALU.add))
                step(nc.vector.reciprocal(pinv, piv))
                step(nc.vector.tensor_tensor(ucol[:, :, 0:rest], um[:, :, c + 1:, c],
                                             pinv.unsqueeze(2).to_broadcast([P, H, rest]), ALU.mult))
                tmp = yt[:, 0:H * rest * rest].rearrange("p (h r k) -> p h r k", h=H, r=rest)
                shape = [P, H, rest, rest]
                step(nc.vector.tensor_tensor(tmp, ucol[:, :, 0:rest].unsqueeze(3).to_broadcast(shape),
                                             um[:, :, c, c + 1:].unsqueeze(2).to_broadcast(shape), ALU.mult))
                step(nc.vector.tensor_tensor(um[:, :, c + 1:, c + 1:], um[:, :, c + 1:, c + 1:], tmp, ALU.subtract))
            step(nc.vector.tensor_scalar(sg, sg, -2.0, None, ALU.mult))
            for c in range(2):
                ins = nc.vector.tensor_tensor(mx[:, :, c].rearrange("p i h j -> p h i j"), ym[:, :, 2 * HD:, :],
                                              sg.unsqueeze(2).to_broadcast([P, H, HD, HD]), ALU.mult)
            ins.then_inc(ev("mx_done"), 1)
            dve.wait_ge(ev("bases_mm"), 1)
            for q in range(2):
                v = bank[2 + q][:, :].rearrange("p (i x b t) -> p b t x i", i=4, x=2, b=2)
                for b in range(2):
                    half = slice(b * D, b * D + D)
                    nc.vector.tensor_copy(bases[half, :, :, 4 * q:4 * q + 4], v[half, b]).then_inc(ev("bases_ready"), 1)

        def copy_keys(dve, t, par):
            dve.wait_ge(ev("k_mm"), t + 1)
            need(dve, ev("k_diag"), 16 * G * (t - 1))
            need(dve, ev("lin_ready"), t - 1)
            nc.vector.tensor_scalar(kk[par][:, :, 0:N], bank[5][:, 0:2 * N].rearrange("p (a b) -> p a b", a=2),
                                    b_qkv[:, 1:2], None, ALU.add).then_inc(ev("k_copied"), 1)

        def attention_dve(dve, s, u):
            p1 = 1 - u
            a, b1, b2 = within(s, 0, PAIRS), within(s - 1, 0, PAIRS), within(s - 2, 0, PAIRS)
            b3 = within(s - 3, 0, PAIRS)
            prep = within(s + 1, 0, PAIRS)

            def scores(j):
                if not a:
                    return
                dve.wait_ge(ev("lg_done"), NG * s + j + 1)
                need(dve, ev("av_done"), s - 1)
                masked = N - (8 - 1) * TILES
                parts = [[i for i in GROUPS[j] if i < masked], [i for i in GROUPS[j] if i >= masked]]
                for c, tiles in enumerate(parts):
                    if tiles:
                        lo, k = tiles[0] - GROUPS[j].start, len(tiles)
                        ins = nc.vector.tensor_scalar(
                            ll[u][:, tiles[0]:tiles[0] + k, :],
                            bank[2 + j % 2][:, lo * N:(lo + k) * N].rearrange("p (a b) -> p a b", a=k),
                            score_c[:, c:c + 1], None, ALU.add)
                ins.then_inc(ev("scores_out"), 1)
            if b1:
                need(dve, ev("t1_done"), s - 1)
                dve.wait_ge(ev("scores_out"), NG * s)
                nc.vector.tensor_reduce(mxv, ll[p1].rearrange("p t n -> p n t"), AX.X, ALU.max).then_inc(ev("mx_ready"), 1)
            if prep and not (isinstance(s, int) and s == -1):
                copy_keys(dve, s + 1, p1)
            if b2:
                t = s - 2
                dve.wait_ge(ev("pr_done"), t + 1)
                hp = h_txt[:, bass.ds(2 * t, 2), :]
                nc.vector.tensor_tensor(hp, hp, bank[7][:, 0:P].rearrange("p (a b) -> p a b", a=2), ALU.add)
                ht = h_tok[:, bass.ds(t, 1), :]
                nc.vector.tensor_tensor(ht, ht, bank[7][0:2 * TOK, P:P + D].unsqueeze(1), ALU.add).then_inc(ev("h_added"), 1)
            if b2:
                t = s - 2
                dve.wait_ge(ev("h_added"), t + 1)
                nc.vector.tensor_copy(gate[:, 0:1], minus_half[:, 0:1])
                for b in range(2):
                    nc.vector.bn_stats(st6[:, b, :], h_txt[:, bass.ds(2 * t + b, 1), :].rearrange("p a b -> p (a b)"))
                nc.vector.bn_stats(st6[0:2 * TOK, 2, :], h_tok[:, bass.ds(t, 1), :].rearrange("p a b -> p (a b)")).then_inc(
                    ev("stats"), 1)
                dve.wait_ge(ev("stats"), t + 1)
                nc.vector.tensor_copy(gate[:, 1:2], minus_half[:, 1:2])
                for b in range(2):
                    nc.vector.bn_aggr(mv[:, b, :], st6[:, b, :])
                nc.vector.bn_aggr(mv[0:2 * TOK, 2, :], st6[0:2 * TOK, 2, :]).then_inc(ev("moments"), 1)
                dve.wait_ge(ev("moments"), t + 1)
                need(dve, ev("rs_ready"), t)
                nc.vector.tensor_scalar(ve, mv[:, :, 1], EPS, None, ALU.add).then_inc(ev("ve_ready"), 1)
            scores(0)
            if b2:
                t = s - 2
                dve.wait_ge(ev("rs_ready"), t + 1)
                need(dve, ev("t4a_done"), t)
                for b in range(2):
                    nc.vector.tensor_scalar(hn2[:, b, :], h_txt[:, bass.ds(2 * t + b, 1), :].rearrange("p a b -> p (a b)"),
                                            mv[:, b, 0:1], rs[:, b:b + 1], ALU.subtract, ALU.mult)
                for c in range(2):
                    ins = nc.vector.tensor_scalar(hn2k[:, c, :], h_tok[:, bass.ds(t, 1), :].rearrange("p a b -> p (a b)"),
                                                  mv[0:2 * TOK, 2, 0:1], rs[0:2 * TOK, 2:3], ALU.subtract, ALU.mult)
                ins.then_inc(ev("hn2_rows"), 1)
            if b1:
                dve.wait_ge(ev("t1_done"), s)
                nc.vector.tensor_reduce(mn, bank[7][:, 0:P].rearrange("p (g k) -> p g k", g=G), AX.X, ALU.max)
                nc.vector.tensor_reduce(mn5, bank[7][0:TOK, P:2 * P].rearrange("p (g k) -> p g k", g=G), AX.X,
                                        ALU.max).then_inc(ev("mn_done"), 1)
                dve.wait_ge(ev("mn_done"), s)
                nc.vector.tensor_copy(mnx, mn.unsqueeze(2).to_broadcast([P, G, 8]))
                nc.vector.tensor_copy(mnx5, mn5.unsqueeze(2).to_broadcast([TOK, G, 8])).then_inc(ev("mn_ready"), 1)
            if b3:
                route(dve, s - 3, 1)
            scores(1)
            if b1:
                dve.wait_ge(ev("t2_done"), s)
                nc.vector.tensor_tensor(ll[p1], ll[p1], bank[7][:, 0:N].unsqueeze(1).to_broadcast([P, TILES, N]),
                                        ALU.subtract).then_inc(ev("sub_done"), 1)
            if b3:
                route(dve, s - 3, 2)
            scores(2)
            if b2:
                t = s - 2
                dve.wait_ge(ev("t4a_done"), t + 1)
                need(dve, ev("hn2_ready"), t - 1)
                need(dve, ev("t4b_done"), t - 1)
                nc.vector.tensor_copy(hs2[u][:, 0:TXT], bank[7][:, 0:TXT])
                for b in range(2):
                    half, src = slice(b * D, b * D + D), slice(TXT + b * TOK, TXT + b * TOK + TOK)
                    nc.vector.tensor_copy(tk10[u][half, b, :], bank[7][half, src])
                    ins = nc.vector.tensor_copy(hs2[u][half, TXT:N], bank[7][half, src])
                ins.then_inc(ev("hs2_ready"), 1)
            if b3:
                route(dve, s - 3, 3)
            scores(3)
            if b3:
                route(dve, s - 3, 4)
            if b2:
                t = s - 2
                dve.wait_ge(ev("t4b_done"), t + 1)
                nc.vector.tensor_copy(rt_logit[:, 0:2], bank[7][:, 0:2 * EXPERTS].rearrange("p (a b) -> p a b", a=2))
                nc.vector.tensor_copy(rt_logit[0:2 * TOK, 2:3],
                                      bank[7][0:2 * TOK, 2 * EXPERTS:3 * EXPERTS].unsqueeze(1)).then_inc(ev("router_out"), 1)
                route(dve, t, 0)
            scores(4)
            if b1:
                dve.wait_ge(ev("exp_done"), s)
                need(dve, ev("av_done"), s - 1)
                nc.vector.tensor_reduce(es, ll[p1].rearrange("p t n -> p n t"), AX.X, ALU.add).then_inc(ev("es_ready"), 1)
            scores(5)
            if b1:
                dve.wait_ge(ev("av_done"), s)
                need(dve, ev("pr_done"), s - 1)
                nc.vector.reciprocal(rec, bank[4][:, N:2 * N]).then_inc(ev("rec_ready"), 1)
                dve.wait_ge(ev("rec_ready"), s)
                nc.vector.tensor_tensor(ot, bank[4][:, 0:N], rec, ALU.mult)
                for b in range(2):
                    half = slice(b * D, b * D + D)
                    ins = nc.vector.tensor_tensor(ot5[half, b, :], bank[4][half, TXT:N], rec[half, TXT:N], ALU.mult)
                ins.then_inc(ev("ot_ready"), 1)

        def route(dve, t, part):
            full = [P, 3, EXPERTS]
            m = rt_m.unsqueeze(2).to_broadcast(full)
            down = countdown[:, :].unsqueeze(1).to_broadcast(full)
            v = nc.vector

            def step(k, ins):
                ins.then_inc(ev("rt_step"), 1)
                dve.wait_ge(ev("rt_step"), RT_STEPS * t + k)
            if part == 0:
                dve.wait_ge(ev("router_out"), t + 1)
                step(1, v.tensor_reduce(rt_m, rt_logit, AX.X, ALU.max))
                v.tensor_tensor(rt_x, rt_logit, m, ALU.subtract).then_inc(ev("rt_shifted"), 1)
            if part == 1:
                dve.wait_ge(ev("rt_exp"), t + 1)
                step(2, v.tensor_reduce(rt_m, rt_x, AX.X, ALU.add))
                step(3, v.reciprocal(rt_m, rt_m))
                step(4, v.tensor_tensor(rt_x, rt_x, m, ALU.mult))
                step(5, v.tensor_reduce(rt_m, rt_x, AX.X, ALU.max))
                step(6, v.tensor_tensor(rt_w, rt_x, m, ALU.is_equal))
            if part == 2:
                step(7, v.tensor_tensor(rt_w, rt_w, down, ALU.mult))
                step(8, v.tensor_reduce(rt_m, rt_w, AX.X, ALU.max))
                step(9, v.tensor_tensor(rt_first, rt_w, m, ALU.is_equal))
                step(10, v.scalar_tensor_tensor(rt_left, rt_first, -2.0, rt_x, ALU.mult, ALU.add))
                step(11, v.tensor_reduce(rt_m, rt_left, AX.X, ALU.max))
            if part == 3:
                step(12, v.tensor_tensor(rt_w, rt_left, m, ALU.is_equal))
                step(13, v.tensor_tensor(rt_w, rt_w, down, ALU.mult))
                step(14, v.tensor_reduce(rt_m, rt_w, AX.X, ALU.max))
                step(15, v.tensor_tensor(rt_w, rt_w, m, ALU.is_equal))
                step(16, v.tensor_tensor(rt_w, rt_w, rt_first, ALU.add))
            if part == 4:
                step(17, v.tensor_tensor(rt_x, rt_x, rt_w, ALU.mult))
                step(18, v.tensor_reduce(rt_m, rt_x, AX.X, ALU.add))
                step(19, v.reciprocal(rt_m, rt_m))
                v.tensor_tensor(router[:, bass.ds(2 * t, 2), :], rt_x[:, 0:2], m[:, 0:2], ALU.mult)
                v.tensor_tensor(router_tok[:, bass.ds(t, 1), :], rt_x[0:2 * TOK, 2:3], m[0:2 * TOK, 2:3],
                                ALU.mult).then_inc(ev("routed"), 1)

        def split_weights(dve):
            dve.wait_ge(ev("hn2_ready"), PAIRS)
            dve.wait_ge(ev("routed"), PAIRS)
            ch = Chain(dve, ev("split_chain"))
            sets = ((router[:, :, :], wsp, rt_16), (router_tok[:, :, :], wsp_tok, rt_16k))
            for _, pieces, _ in sets:
                nc.vector.memset(pieces[:, :, 3, :], 0.0)
            for k in range(2):
                for r, _, h in sets:
                    ins = nc.vector.tensor_copy(h, r)
                ch.step(ins)
                for _, pieces, h in sets:
                    ins = nc.vector.tensor_copy(pieces[:, :, k, :], h)
                ch.step(ins)
                for r, pieces, _ in sets:
                    ins = nc.vector.tensor_tensor(r, r, pieces[:, :, k, :], ALU.subtract)
                ch.step(ins)
            for r, pieces, _ in sets:
                nc.vector.tensor_copy(pieces[:, :, 2, :], r)
            for v in (*mt, yk, dup):
                ins = nc.vector.memset(v, 0.0)
            ch.step(ins)
            for b in range(2):
                for c in range(2):
                    half = slice(b * D, b * D + D)
                    ins = nc.vector.tensor_copy(dup[half, b, c * D:c * D + D], ident[half, half])
            ins.then_inc(ev("weights_split"), 1)
            dve.wait_ge(ev("weights_split"), 1)

        def combine(dve, s, u):
            t1, p1 = s + 1, 1 - u
            if within(s - 1, 0, PAIRS):
                dve.wait_ge(ev("y_mm"), s)
                need(dve, ev("y_turned"), s - 1)
                nc.vector.tensor_scalar(yt_sb, bank[5][:, 0:N], b2s_col[:, :], None, ALU.add)
                for b in range(2):
                    half = slice(b * D, b * D + D)
                    ins = nc.vector.tensor_scalar(yk[half, b, :], bank[5][half, TXT:N], b2s_col[half, :], None, ALU.add)
                ins.then_inc(ev("y_copied"), 1)
            for e in range(EXPERTS):
                if within(s, 0, PAIRS):
                    dve.wait_ge(ev("mask_mm"), EXPERTS * s + e + 1)
                    dve.wait_ge(ev("gelu_done"), CH * s + 2 * e + 2)
                    nc.vector.tensor_tensor(hg[e % HG], hg[e % HG],
                                            bank[4 + 2 * (e % 2)][:, 0:2 * N].unsqueeze(1).to_broadcast([P, 2, 2 * N]),
                                            ALU.mult).then_inc(ev("weighted"), 1)
                if e == 1 and within(s - 1, 0, PAIRS):
                    dve.wait_ge(ev("y_turned"), s)
                    need(dve, ev("out_stored"), 64 * (s - 1))
                    nc.vector.tensor_copy(yo[2][0:2 * TOK], bank[7][0:2 * TOK, P:P + D])
                    for b in range(2):
                        ins = nc.vector.tensor_tensor(
                            yo[b], bank[7][:, b * D:b * D + D],
                            h_txt[:, bass.ds(2 * (s - 1) + b, 1), :].rearrange("p a d -> p (a d)"), ALU.add)
                    ins.then_inc(ev("y_added"), 1)
                    dve.wait_ge(ev("y_added"), s)
                    nc.vector.tensor_tensor(yo[2][0:2 * TOK], yo[2][0:2 * TOK],
                                            h_tok[:, bass.ds(s - 1, 1), :].rearrange("p a d -> p (a d)"),
                                            ALU.add).then_inc(ev("y_out"), 1)
                if e == 3 and within(t1, 0, PAIRS):
                    dve.wait_ge(ev("w_turned2"), t1 + 1)
                    need(dve, ev("mask_mm"), EXPERTS * (t1 - 1))
                    need(dve, ev("y_mm"), t1 - 1)
                    for b in range(2):
                        rows = slice(32 * b, 32 * b + 32)
                        nc.vector.tensor_copy(mt[p1][rows, b, 0:TXT], bank[7][rows, 0:TXT])
                        ins = nc.vector.tensor_copy(mt[p1][rows, b, TXT:N],
                                                    bank[7][rows, TXT + b * TOK:TXT + b * TOK + TOK])
                    ins.then_inc(ev("mt_ready"), 1)
                if e == 4 and within(t1, 0, PAIRS):
                    dve.wait_ge(ev("x_mm"), t1 + 1)
                    need(dve, ev("w1_done"), CH * (t1 - 1))
                    xd = bank[3][:, 0:2 * N]
                    nc.vector.tensor_copy(x12[p1], xd).then_inc(ev("x_piece"), 1)
                    dve.wait_ge(ev("x_piece"), 4 * t1 + 1)
                    nc.vector.tensor_copy(x13[p1][0:D], x12[p1][0:D])
                    nc.vector.tensor_tensor(x_r, xd, x12[p1], ALU.subtract).then_inc(ev("x_piece"), 1)
                    dve.wait_ge(ev("x_piece"), 4 * t1 + 2)
                if e == 5 and within(t1, 0, PAIRS):
                    nc.vector.tensor_copy(x12[p1][D:P], x_r[D:P]).then_inc(ev("x_piece"), 1)
                    dve.wait_ge(ev("x_piece"), 4 * t1 + 3)
                    nc.vector.tensor_tensor(x13[p1][D:P], x_r[D:P], x12[p1][D:P], ALU.subtract).then_inc(ev("x_piece"), 1)
                    dve.wait_ge(ev("x_piece"), 4 * t1 + 4)

        block = ctx.enter_context(nc.Block())

        @block.sync
        def _(sp):
            tl = ev("tree_loaded")
            loads = [
                (ids_raw[:, 0:LEAFC], a["leaf_ids"].rearrange("(t s) l -> t (s l)", t=ST)),
                (ids_raw[:, LEAFC:], a["op_ids"].rearrange("(t s) l -> t (s l)", t=ST)),
                (comp, a["comp_emb"].rearrange("(v p) d -> p v d", v=2)),
                (op_raw, a["op_emb"]),
                (w_op, a["W_bin"][0:D, :]),
                (w_lr, a["W_bin"][D:3 * D, :]),
                (bc_row, a["b_bin"].rearrange("(o d) -> o d", o=1)),
                (gamma_bc, a["gamma"].partition_broadcast(P)),
                (beta_bc, a["beta"].partition_broadcast(P)),
            ]
            for dst, src in loads:
                sp.dma_start(dst, src).then_inc(tl, 16)
            sp.dma_start(txt_idx, a["x_txt"].rearrange("b n -> n b")).then_inc(ev("token_ids_loaded"), 16)

            kl = ev("tok_loaded")
            x = a["x"].rearrange("b c h w -> (b c) h w")
            sp.dma_start(xs[0:PH], x[:, 0:PH, :].rearrange("b h w -> h b w")).then_inc(kl, 16)
            sp.dma_start(xs[PH:P, :, 0:PX - 1], x[:, 0:PH, 1:PX].rearrange("b h w -> h b w")).then_inc(kl, 16)
            w = a["tok_weight"].rearrange("(h w) d -> h w d", h=PH)
            sp.dma_start(wt[0:PH], w[:, 0:PW:2, :]).then_inc(kl, 16)
            sp.dma_start(wt[PH:P, 0:PW // 2, :], w[:, 1:PW:2, :]).then_inc(kl, 16)
            for b in range(2):
                sp.dma_start(btok[b * D:b * D + D], a["tok_bias"].rearrange("(d o) -> d o", o=1)).then_inc(kl, 16)

            wl = ev("weights_loaded")
            n = [0]

            def load(dst, src):
                sp.dma_start(dst, src).then_inc(wl, 16)
                n[0] += 1
            for b in range(2):
                load(wn[:, 0:3, b, :], a["w_qkv"].rearrange("(s c) d -> c s d", s=3))
                load(wn[:, 3, b, :], a["w_proj"])
                half = slice(b * D, b * D + D)
                for s in range(3):
                    load(b_qkv[half, s:s + 1], a["b_qkv"][s * D:s * D + D].rearrange("(d o) -> d o", o=1))
                load(b_top[half, :], a["b_qkv"][b * D:b * D + D].partition_broadcast(D))
                load(bp_row[:, b, :], a["b_proj"].rearrange("(o d) -> o d", o=1))
                load(wr_both[half, :], a["Wr"])
                load(w1_f[half, 0:EXPERTS, :], a["W1p"].rearrange("e d f -> d e f"))
                load(w1_f[half, EXPERTS, :], a["W1s"])
                load(b2s_col[half, :], a["b2s"].rearrange("(d o) -> d o", o=1))
            load(b_qk_rows[:, :], a["b_qkv"][0:P].partition_broadcast(P))
            for c in range(2):
                load(w2_s[:, 0:EXPERTS, c, :], a["W2p"][:, c * P:c * P + P, :].rearrange("e f d -> f e d"))
                load(w2_s[:, EXPERTS, c, :], a["W2s"][c * P:c * P + P, :])
                load(b1_col[:, 0:EXPERTS, c], a["b1p"][:, c * P:c * P + P].rearrange("e f -> f e"))
                load(b1_col[:, EXPERTS, c:c + 1], a["b1s"][c * P:c * P + P].rearrange("(f o) -> f o", o=1))
            for i in range(D // EXPERTS):
                load(b2_rows[i * EXPERTS:(i + 1) * EXPERTS, :], a["b2p"])
            load(conv_t[:, :], a["conv_w"].rearrange("o c -> c o"))
            for i, name in enumerate(["bn_gamma", "bn_beta", "bn_mean", "bn_var"]):
                load(bn[:, i:i + 1], a[name].rearrange("(c o) -> c o", o=1))
            for i, name in enumerate(["scale", "riem_scale", "grassman_scale"]):
                load(score_scale[i * H:i * H + H, :], a[name].partition_broadcast(H))
            load(cb_row[:, :], a["conv_b"].rearrange("(o c) -> o c", o=1))
            assert n[0] == WLOADS, n[0]

            def store_roots(s, _):
                if within(s - 2, 0, TS):
                    need(sp, ev("roots_ready"), s - 1)
                    sp.dma_start(root_dram.rearrange("(i u s) d -> i s u d", u=2, s=P)[s - 2], lv_g[2]).then_inc(
                        ev("roots_stored"), 16)
            slots(sp, 0, 2, TS, TS + 2, 1, store_roots)


            def diag(s, u):
                t, par = s + 1, 1 - u
                if within(t, 0, PAIRS):
                    sp.wait_ge(ev("k_copied"), t + 1)
                    if isinstance(t, int) and t < 2:
                        sp.wait_ge(ev("blocks_zero"), 2)
                    for g in range(G):
                        r = slice(8 * g, 8 * g + 8)
                        sp.dma_start(kbd[par][r, :, g, :], kk[par][r, :, :]).then_inc(ev("k_diag"), 16)
                    if isinstance(t, int) and t == 0:
                        sp.wait_ge(ev("v_copied"), 1)
                    else:
                        sp.wait_ge(ev("vt_done"), NVT * t)
                    for g in range(G):
                        r = slice(8 * g, 8 * g + 8)
                        sp.dma_start(vbt[r, g, :], vv[par][r, :]).then_inc(ev("v_diag"), 16)
            slots(sp, -1, 5, PAIRS - 1, PAIRS + 2, 2, diag)

            pairs_out = out.rearrange("(t b) n d -> t b n d", b=2)

            def store(t, u):
                sp.wait_ge(ev("y_out"), t + 1)
                for b in range(2):
                    sp.dma_start(pairs_out[t, b, TOK:N, :], yo[b]).then_inc(ev("out_stored"), 16)
                sp.dma_start(pairs_out[t, 0, 0:TOK, :], yo[2][0:TOK, :]).then_inc(ev("out_stored"), 16)
                sp.dma_start(pairs_out[t, 1, 0:TOK, :], yo[2][TOK:2 * TOK, :]).then_inc(ev("out_stored"), 16)
            slots(sp, 0, 2, PAIRS, PAIRS, 2, store)
            sp.wait_ge(ev("out_stored"), 64 * PAIRS)

        @block.gpsimd
        def _(pool):
            ch = Chain(pool, ev("pool_chain"))
            nc.gpsimd.memset(ones_row[:, :], 1.0)
            nc.gpsimd.memset(ones_col[:, :], 1.0)
            nc.gpsimd.memset(ones16[:, :], 1.0)
            nc.gpsimd.memset(eps_col[:, :], EPS)
            nc.gpsimd.memset(minus_half[:, :], -0.5)
            nc.gpsimd.memset(pick_sq[:, :], 0.0)
            nc.gpsimd.memset(pick_lin[:, :], 0.0)
            nc.gpsimd.memset(ident2[:, :], 0.0)
            nc.gpsimd.iota(iota_col[:, :], pattern=[[P, 2]], base=0, channel_multiplier=1,
                           allow_small_or_imprecise_dtypes=True)
            ch.step(nc.gpsimd.memset(ident[:, :], 0.0))

            def diagonal(v, pattern, base=0):
                return nc.gpsimd.affine_select(out=v, in_=v, compare_op=ALU.not_equal, fill=1.0, base=base,
                                               pattern=pattern, channel_multiplier=1)
            diagonal(ident[:, :], [[-1, P]]).then_inc(ev("ident_ready"), 1)
            diagonal(ident2[:, :], [[-1, D]])
            diagonal(pick_lin[:, :].rearrange("c (h d) -> c h d", h=H), [[-1, H], [0, HD]])
            diagonal(pick_sq[:, :].rearrange("c (g m) -> c g m", g=G), [[-1, G], [0, 8]], base=-H)
            ch.step(nc.gpsimd.memset(wq_dup[:, :, :], 0.0))
            diagonal(ident2[:, :], [[-1, D]], base=-D)
            nc.gpsimd.iota(countdown[:, :], pattern=[[-1, EXPERTS]], base=EXPERTS, channel_multiplier=0,
                           allow_small_or_imprecise_dtypes=True)
            for z in (wk_dup, wqk_pair, wr_pair):
                nc.gpsimd.memset(z[:, :, :], 0.0)
            nc.gpsimd.memset(wv_pair[:, :], 0.0)
            nc.gpsimd.memset(tok_m, 0.0)
            nc.gpsimd.memset(wp_pair[:, :], 0.0).then_inc(ev("zeros_ready"), 1)

            def affine(level, s):
                shape = [P, 8 >> level, D]
                first = isinstance(s, int) and s == 0
                pool.wait_ge(ev(f"normed{level}"), s + 1)
                if level < 2:
                    need(pool, ev(f"kids{level}"), s)
                else:
                    need(pool, ev("roots_stored"), 16 * s)
                nc.gpsimd.tensor_tensor(lv_g[level], lv_h[level], gamma_bc.unsqueeze(1).to_broadcast(shape),
                                        ALU.mult).then_inc(ev(f"gained{level}"), 1)
                pool.wait_ge(ev(f"gained{level}"), s + 1)
                nc.gpsimd.tensor_tensor(lv_g[level], lv_g[level], beta_bc.unsqueeze(1).to_broadcast(shape),
                                        ALU.add).then_inc(ev(f"leveled{level}" if level < 2 else "roots_raw" if first else "roots_ready"), 1)

            def tree(s, _):
                if within(s, 0, TS):
                    affine(0, s)
                if within(s - 1, 0, TS):
                    affine(1, s - 1)
                if within(s - 2, 0, TS):
                    affine(2, s - 2)
                    if isinstance(s, int) and s == 2:
                        pool.wait_ge(ev("roots_raw"), 1)
                        nc.gpsimd.memset(lv_g[2][0:2, 0, :], 0.0).then_inc(ev("roots_ready"), 1)
            pool.wait_ge(ev("tree_loaded"), 144)
            slots(pool, 0, 3, TS, TS + 2, 1, tree)

            pool.wait_ge(ev("roots_stored"), 16 * TS)
            pool.wait_ge(ev("token_ids_loaded"), 16)
            for b in range(B):
                nc.gpsimd.indirect_dma_start(
                    out=h_txt[:, b, :], out_offset=None, in_=root_dram,
                    in_offset=bass.IndirectOffsetOnAxis(ap=txt_idx[:, b:b + 1], axis=0)).then_inc(
                        ev(f"gathered{b // 16}"), 16)

            pool.wait_ge(ev("weights_loaded"), 16 * WLOADS)
            pool.wait_ge(ev("tok_ready"), 1)
            for g in range(4):
                pool.wait_ge(ev(f"gathered{g}"), 256)
            ch.step(nc.gpsimd.tensor_copy(w1_split[:, 0], w1_f))
            ch.step(nc.gpsimd.tensor_tensor(w1_r, w1_f, w1_split[:, 0], ALU.subtract))
            ch.step(nc.gpsimd.tensor_copy(w1_split[:, 1], w1_r))
            ch.step(nc.gpsimd.tensor_tensor(w1_split[:, 2], w1_r, w1_split[:, 1], ALU.subtract))
            nc.gpsimd.tensor_copy(w1_split[D:P, 2], w1_split[D:P, 0]).then_inc(ev("w1_pieces"), 1)
            pool.wait_ge(ev("w1_pieces"), 1)

            for v in (*linb, *kk, *vv, *tk10, *qq, *pm, ot5):
                nc.gpsimd.memset(v, 0.0)
            nc.gpsimd.memset(mv, 1.0).then_inc(ev("rows_zero"), 1)
            pool.wait_ge(ev("rows_zero"), 1)
            pool.wait_ge(ev("top_ready"), 1)
            nc.gpsimd.memset(vbt, 0.0)
            for par in (1, 0):
                nc.gpsimd.memset(kbd[par], 0.0).then_inc(ev("blocks_zero"), 1)
            pool.wait_ge(ev("bases_ready"), 4)

            def attention(s, u):
                t, par = s + 1, 1 - u
                if within(t, 0, PAIRS):
                    need(pool, ev("p_mm"), t - 1)
                    shape = [P, 2, H, HD]
                    for b in range(2):
                        nc.gpsimd.tensor_tensor(
                            mqx[par][:, b], bases[:, bass.ds(t, 1), 0, :].unsqueeze(2).to_broadcast(shape),
                            group_of[:, b * H:b * H + H].unsqueeze(1).unsqueeze(3).to_broadcast(shape), ALU.mult)
                    nc.gpsimd.tensor_tensor(mkx[par], bases[:, bass.ds(t, 1), 1, :].to_broadcast([P, H, HD]),
                                            head_of[:, :].unsqueeze(2).to_broadcast([P, H, HD]),
                                            ALU.mult).then_inc(ev("mq_ready"), 1)
                if within(s - 2, 0, PAIRS):
                    pool.wait_ge(ev("ve_ready"), s - 1)
                    nc.gpsimd.tensor_tensor(rs, ve, minus_half[:, 0:3], ALU.pow).then_inc(ev("rs_ready"), 1)
                if within(t, 0, PAIRS):
                    pool.wait_ge(ev("k_copied"), t + 1)
                    need(pool, ev("lg_done"), NG * (t - 1))
                    shape = [D, 2, H, NP]
                    nc.gpsimd.tensor_tensor(linb[par][0:D], kk[par][0:D].unsqueeze(2).to_broadcast(shape),
                                            lin_a[:, :].unsqueeze(1).unsqueeze(3).to_broadcast(shape),
                                            ALU.mult).then_inc(ev("lin_ready"), 1)
            slots(pool, -1, 5, PAIRS - 1, PAIRS + 2, 2, attention)

        @block.scalar
        def _(act):
            def copy_ids(s, u):
                act.wait_ge(ev("ids_bc"), 2 * s + u + 1)
                need(act, ev("hot"), 2 * s + u - 1)
                for i, (lo, hi) in enumerate(ID_PARTS):
                    ins = nc.scalar.activation(ids_bc[u][:, lo:hi], bank[i][:, 0:hi - lo], ACT.Identity)
                ins.then_inc(ev("ids_copied"), 1)

            act.wait_ge(ev("ident_ready"), 1)
            nc.scalar.activation(root_scratch, eps_col[:, :], ACT.Sqrt)
            copy_ids(0, 0)
            act.wait_ge(ev("comp_centred"), 1)
            nc.scalar.activation(comp_sq, comp, ACT.Square).then_inc(ev("comp_sq"), 1)
            act.wait_ge(ev("comp_var"), 1)
            nc.scalar.activation(comp_st[:, 2, :], comp_st[:, 1, :], ACT.Sqrt, bias=eps_col[:, :],
                                 scale=1.0 / D).then_inc(ev("comp_std"), 1)

            copy_ids(0, 1)

            def deviation(level, s):
                n = 8 >> level
                act.wait_ge(ev(f"level{level}"), s + 1)
                need(act, ev(f"var{level}"), s)
                nc.scalar.activation(lv_sq[level], LV[level], ACT.Square).then_inc(ev(f"sq{level}"), 1)

            def root(level, s):
                act.wait_ge(ev(f"var{level}"), s + 1)
                need(act, ev(f"inv{level}"), s)
                nc.scalar.activation(lv_std[level], lv_var[level], ACT.Sqrt, bias=eps_col[:, :],
                                     scale=1.0 / D).then_inc(ev(f"std{level}"), 1)

            def tree(s, _):
                if within(s + 1, 0, TS):
                    copy_ids(s + 1, 0)
                if within(s - 1, 0, TS):
                    act.wait_ge(ev("kids0"), s)
                    need(act, ev("level1"), s - 1)
                    nc.scalar.activation(kids1, bank[5][:, :].rearrange("p (a b) -> p a b", a=4),
                                         ACT.Identity).then_inc(ev("kids0_copied"), 1)
                if within(s + 1, 0, TS):
                    copy_ids(s + 1, 1)
                if within(s - 2, 0, TS):
                    act.wait_ge(ev("kids1"), s - 1)
                    need(act, ev("level2"), s - 2)
                    nc.scalar.activation(kids2, bank[5][:, 0:256].rearrange("p (a b) -> p a b", a=2),
                                         ACT.Identity).then_inc(ev("kids1_copied"), 1)
                for level in range(3):
                    if within(s - level, 0, TS):
                        deviation(level, s - level)
                        root(level, s - level)
            slots(act, 0, 3, TS - 1, TS + 2, 1, tree)

            act.wait_ge(ev("tok_mm"), 1)
            act.wait_ge(ev("tok_loaded"), 96)
            nc.scalar.activation(tok_t.rearrange("p a b -> p (a b)"), bank[0][:, 0:PAIRS * TOK], ACT.Gelu,
                                 bias=btok).then_inc(ev("tok_gelu"), 1)
            act.wait_ge(ev("weights_loaded"), 16 * WLOADS)
            nc.scalar.activation(bn_inv[:, 0:1], bn[:, 3:4], ACT.Sqrt, bias=eps_col[0:3 * H, :]).then_inc(ev("bn_std"), 1)
            def norm1(g):
                act.wait_ge(ev("ln_centred"), g + 1)
                w = ln_slice(g)
                nc.scalar.activation(w["sq"], w["hn"], ACT.Square).then_inc(ev("ln_sq"), 1)
                act.wait_ge(ev("ln_var"), g + 1)
                nc.scalar.activation(w["d"], w["v"], ACT.Sqrt, bias=eps_col[0:w["parts"], :],
                                     scale=1.0 / D).then_inc(ev("ln_std"), 1)

            def first(s, u):
                if within(s, 0, PAIRS):
                    need(act, ev("hs_mm"), s - 1)
                    nc.scalar.activation(st_txt[u], hn_txt[:, bass.ds(2 * s, 2), :], ACT.Identity)
                    nc.scalar.activation(st_tok[u], hn_tok[:, bass.ds(s, 1), :].to_broadcast([2 * TOK, 2, D]),
                                         ACT.Identity).then_inc(ev("staged"), 1)
                if within(s - 1, 0, PAIRS):
                    act.wait_ge(ev("hs_ready"), s)
                    nc.scalar.activation(hn_t[:, bass.ds(s - 1, 1), :], hs[1 - u][:, 0:N].unsqueeze(1),
                                         ACT.Identity).then_inc(ev("hn_t_ready"), 1)
            norm1(0)
            for g in range(4):
                norm1(g + 1)
                act.wait_ge(ev("hn_ready"), g + 2)
                slots(act, 8 * g, max(8 * g, 4), 8 * g + 8, PAIRS + 1 if g == 3 else 8 * g + 8, 2, first)

            for c in range(QB):
                act.wait_ge(ev("pivot"), c + 1)
                nc.scalar.activation(qsd, ym[:, :, c, c], ACT.Sqrt).then_inc(ev("pivot_root"), 1)

            def attention(s, u):
                t1, p1 = s + 1, 1 - u

                def squares(j, b):
                    act.wait_ge(ev("dg_done"), 2 * NG * s + 2 * j + b + 1)
                    need(act, ev("lg_done"), NG * s + j - 1)
                    n = len(GROUPS[j]) * N
                    nc.scalar.activation(sq[b][j % 2][:, 0:n], bank[b][:, 0:n], ACT.Square).then_inc(ev("sq_done"), 1)

                def turned(r):
                    act.wait_ge(ev("vt_done"), NVT * s + r + 1)
                    need(act, ev("av_done"), s - 1)
                    n = len(VTS[r])
                    nc.scalar.activation(vbd[u][:, VTS[r].start:VTS[r].stop, :],
                                         bank[5 + r % 2][:, 0:n * P].rearrange("p (a b) -> p a b", a=n),
                                         ACT.Identity).then_inc(ev("vt_copied"), 1)
                for j in range(NG):
                    if within(s, 0, PAIRS):
                        squares(j, 0)
                        squares(j, 1)
                    if within(t1, 0, PAIRS):
                        if j == 0:
                            act.wait_ge(ev("q_mm"), t1 + 1)
                            need(act, ev("lg_done"), NG * (t1 - 1))
                            nc.scalar.activation(qq[p1].rearrange("p a b -> p (a b)"), bank[6][:, 0:2 * N], ACT.Identity,
                                                 bias=b_qkv[:, 0:1]).then_inc(ev("q_copied"), 1)
                        if j == 1:
                            act.wait_ge(ev("v_mm"), t1 + 1)
                            need(act, ev("v_diag"), 16 * G * (t1 - 1))
                            nc.scalar.activation(vv[p1][:, 0:N], bank[6][:, 0:N], ACT.Identity,
                                                 bias=b_qkv[:, 2:3]).then_inc(ev("v_copied"), 1)
                            act.wait_ge(ev("p_mm"), t1 + 1)
                            need(act, ev("q2_mm"), t1 - 1)
                            nc.scalar.activation(pm[p1][D:P].rearrange("p a b -> p (a b)"), bank[5][D:P, 0:P],
                                                 ACT.Identity).then_inc(ev("p_copied"), 1)
                        if j == 2:
                            act.wait_ge(ev("q2_mm"), t1 + 1)
                            nc.scalar.activation(qq[p1][D:P].rearrange("p a b -> p (a b)"), bank[6][D:P, 0:2 * N],
                                                 ACT.Identity).then_inc(ev("q2_ready"), 1)
                    if j == 3 and within(s, 0, PAIRS):
                        turned(0)
                        turned(1)
                    if j == 4 and within(s - 1, 0, PAIRS):
                        act.wait_ge(ev("sub_done"), s)
                        nc.scalar.activation(ll[p1], ll[p1], ACT.Exp).then_inc(ev("exp_done"), 1)
                    if j == 4 and within(s, 0, PAIRS):
                        turned(2)
                        turned(3)
                    if j == 5 and within(s, 0, PAIRS):
                        turned(4)
                if within(s - 2, 0, PAIRS):
                    act.wait_ge(ev("hs2_ready"), s - 1)
                    nc.scalar.activation(hn_t[:, bass.ds(s - 2, 1), :], hs2[u].unsqueeze(1),
                                         ACT.Identity).then_inc(ev("hn2_ready"), 1)
                    act.wait_ge(ev("rt_shifted"), s - 1)
                    nc.scalar.activation(rt_x, rt_x, ACT.Exp).then_inc(ev("rt_exp"), 1)
            act.wait_ge(ev("rows_zero"), 1)
            act.wait_ge(ev("top_ready"), 1)
            slots(act, -1, 5, PAIRS - 1, PAIRS + 2, 2, attention)

            def experts(s, u):
                t1, p1 = s + 1, 1 - u
                for c in range(CH):
                    if within(s, 0, PAIRS):
                        act.wait_ge(ev("w1_done"), CH * s + c + 1)
                        if c % 2 == 0:
                            need(act, ev("w2_done"), (EXPERTS + 1) * s + c // 2 + 1 - HG)
                        nc.scalar.activation(hg[c // 2 % HG][:, c % 2], bank[c % 3][:, 0:2 * N], ACT.Gelu,
                                             bias=b1_col[:, c // 2, c % 2:c % 2 + 1]).then_inc(ev("gelu_done"), 1)
                    if c == 1 and within(t1, 0, PAIRS):
                        need(act, ev("w_turned2"), t1 - 1)
                        if isinstance(t1, int) and t1 == 0:
                            act.wait_ge(ev("weights_split"), 1)
                        nc.scalar.activation(st_w[p1], wsp[:, bass.ds(2 * t1, 2)].rearrange(
                            "p a b c -> p (a b c)").unsqueeze(1).to_broadcast([P, 2, D]), ACT.Identity)
                        nc.scalar.activation(st_wk[p1],
                                             wsp_tok[:, bass.ds(t1, 1)].rearrange("p a b c -> p a (b c)").to_broadcast(
                                                 [2 * TOK, 2, 4 * EXPERTS]), ACT.Identity).then_inc(ev("w_staged"), 1)
            slots(act, -1, 3, PAIRS - 1, PAIRS + 1, 2, experts)

        @block.vector
        def _(dve):
            ch = Chain(dve, ev("dve_chain"))
            dve.wait_ge(ev("tree_loaded"), 144)
            dve.wait_ge(ev("ident_ready"), 1)
            nc.vector.tensor_copy(ids_all[:, 0:LEAFC].rearrange("t (l s) -> t l s", l=LEAVES),
                                  ids_raw[:, 0:LEAFC].rearrange("t (s l) -> t l s", l=LEAVES))
            nc.vector.tensor_copy(ids_all[:, LEAFC:].rearrange("t (l s) -> t l s", l=INNER),
                                  ids_raw[:, LEAFC:].rearrange("t (s l) -> t l s", l=INNER))
            ch.step(nc.vector.memset(tab_op[OPS:P], 0.0))

            def pick_ids(s, u):
                need(dve, ev("ids_bc"), 2 * s + u - 1)
                nc.vector.tensor_scalar(ids_one[u], ids_all, ident[0:ST, bass.ds(2 * s + u, 1)], None,
                                        ALU.mult).then_inc(ev("ids_picked"), 1)

            def hots(s, u):
                dve.wait_ge(ev("ids_copied"), 2 * s + u + 1)
                need(dve, ev("level0" if u else "half0"), s)
                if u == 0:
                    need(dve, ev("level2"), s - 3)
                for v in range(2):
                    nc.vector.tensor_scalar(leaf_hot[:, u, v, :], ids_bc[u][:, 0:LEAFC], iota_col[:, v:v + 1], None,
                                            ALU.is_equal)
                nc.vector.tensor_scalar(op_hot[:, u, :], ids_bc[u][0:OPS, LEAFC:LEAFC + 4 * P], iota_col[0:OPS, 0:1],
                                        None, ALU.is_equal)
                nc.vector.tensor_scalar(up_hot[:, bass.ds(2 * (s % 4) + u, 1), :].rearrange("p a b -> p (a b)"),
                                        ids_bc[u][:, LEAFC + 4 * P:], iota_col[:, 0:1],
                                        None, ALU.is_equal).then_inc(ev("hot"), 1)

            pick_ids(0, 0)
            pick_ids(0, 1)
            nc.vector.tensor_reduce(w_mean[:, 0:1], w_lr, AX.X, ALU.add)
            nc.vector.tensor_reduce(w_mean[0:D, 1:2], w_op, AX.X, ALU.add)
            nc.vector.tensor_reduce(w_mean[0:1, 2:3], bc_row, AX.X, ALU.add)
            ch.step(nc.vector.tensor_reduce(comp_st[:, 0, :], comp, AX.X, ALU.add))
            nc.vector.tensor_scalar(w_mean[:, 0:1], w_mean[:, 0:1], 1.0 / D, None, ALU.mult)
            nc.vector.tensor_scalar(w_mean[0:D, 1:2], w_mean[0:D, 1:2], 1.0 / D, None, ALU.mult)
            nc.vector.tensor_scalar(w_mean[0:1, 2:3], w_mean[0:1, 2:3], 1.0 / D, None, ALU.mult)
            ch.step(nc.vector.tensor_scalar(comp_st[:, 0, :], comp_st[:, 0, :], 1.0 / D, None, ALU.mult))
            nc.vector.tensor_scalar(w_lr, w_lr, w_mean[:, 0:1], None, ALU.subtract)
            nc.vector.tensor_scalar(w_op, w_op, w_mean[0:D, 1:2], None, ALU.subtract)
            nc.vector.tensor_scalar(bc_row, bc_row, w_mean[0:1, 2:3], None, ALU.subtract)
            nc.vector.tensor_tensor(comp, comp, comp_st[:, 0, :].unsqueeze(2).to_broadcast([P, 2, D]),
                                    ALU.subtract).then_inc(ev("comp_centred"), 1)
            dve.wait_ge(ev("comp_sq"), 1)
            nc.vector.tensor_reduce(comp_st[:, 1, :], comp_sq, AX.X, ALU.add).then_inc(ev("comp_var"), 1)
            dve.wait_ge(ev("comp_std"), 1)
            ch.step(nc.vector.reciprocal(comp_st[:, 3, :], comp_st[:, 2, :]))
            ch.step(nc.vector.tensor_tensor(comp, comp, comp_st[:, 3, :].unsqueeze(2).to_broadcast([P, 2, D]), ALU.mult))
            ch.step(nc.vector.tensor_tensor(comp, comp, gamma_bc.unsqueeze(1).to_broadcast([P, 2, D]), ALU.mult))
            for c in range(2):
                ins = nc.vector.tensor_tensor(comp_d[:, :, c, :], comp, beta_bc.unsqueeze(1).to_broadcast([P, 2, D]),
                                              ALU.add)
            ins.then_inc(ev("comp_ready"), 1)
            dve.wait_ge(ev("comp_turned"), 1)
            nc.vector.tensor_copy(comp_t, bank[5][:, 0:256].rearrange("p (a b) -> p a b", a=2))
            nc.vector.tensor_copy(op_t, bank[5][0:D, 256:256 + OPS]).then_inc(ev("comp_copied"), 1)
            hots(0, 0)
            dve.wait_ge(ev("tables"), 1)
            for side in range(2):
                nc.vector.tensor_copy(tab_f[:, 2 * side:2 * side + 2, :],
                                      bank[4 + 2 * side][:, 0:P].rearrange("p (a b) -> p a b", a=2))
            ch.step(nc.vector.tensor_copy(tab_f[0:OPS, 4, :], bank[7][0:OPS, 0:D]))
            for piece in range(3):
                nc.vector.tensor_copy(tab[:, :, :, piece, :], tab_f[:, 0:4, :].rearrange("p (a v) d -> p a v d", a=2))
                ins = nc.vector.tensor_copy(tab_op[0:OPS, piece, :], tab_f[0:OPS, 4, :])
                if piece == 2:
                    ins.then_inc(ev("tables_split"), 1)
                    break
                ch.step(ins)
                nc.vector.tensor_copy(tab_r[:, 0:4, :].rearrange("p (a v) d -> p a v d", a=2), tab[:, :, :, piece, :])
                ch.step(nc.vector.tensor_copy(tab_r[0:OPS, 4, :], tab_op[0:OPS, piece, :]))
                nc.vector.tensor_tensor(tab_f[:, 0:4, :], tab_f[:, 0:4, :], tab_r[:, 0:4, :], ALU.subtract)
                ch.step(nc.vector.tensor_tensor(tab_f[0:OPS, 4, :], tab_f[0:OPS, 4, :], tab_r[0:OPS, 4, :], ALU.subtract))

            def variance(level, s):
                dve.wait_ge(ev(f"sq{level}"), s + 1)
                need(dve, ev(f"std{level}"), s)
                nc.vector.tensor_reduce(lv_var[level], lv_sq[level], AX.X, ALU.add).then_inc(ev(f"var{level}"), 1)

            def norm(level, s):
                shape = [P, 8 >> level, D]
                dve.wait_ge(ev(f"std{level}"), s + 1)
                nc.vector.reciprocal(lv_inv[level], lv_std[level]).then_inc(ev(f"inv{level}"), 1)
                dve.wait_ge(ev(f"inv{level}"), s + 1)
                need(dve, ev(f"gained{level}"), s)
                nc.vector.tensor_tensor(lv_h[level], LV[level], lv_inv[level].unsqueeze(2).to_broadcast(shape),
                                        ALU.mult).then_inc(ev(f"normed{level}"), 1)

            def tree(s, _):
                if within(s + 1, 0, TS):
                    hots(s + 1, 0)
                if within(s + 2, 0, TS):
                    pick_ids(s + 2, 0)
                    pick_ids(s + 2, 1)
                for level in range(3):
                    if within(s - level, 0, TS):
                        variance(level, s - level)
                        norm(level, s - level)
                if within(s + 1, 0, TS):
                    hots(s + 1, 1)
            hots(0, 1)
            pick_ids(1, 0)
            pick_ids(1, 1)
            slots(dve, 0, 3, TS - 2, TS + 2, 1, tree)

            dve.wait_ge(ev("tok_gelu"), 1)
            dve.wait_ge(ev("zeros_ready"), 1)
            nc.vector.tensor_copy(tok_m[0:D, :, 0, :], tok_t[0:D])
            nc.vector.tensor_copy(tok_m[D:P, :, 1, :], tok_t[D:P]).then_inc(ev("tok_split"), 1)
            for q in range(4):
                dve.wait_ge(ev("tok_rows"), q + 1)
                ins = nc.vector.tensor_copy(h_tok[:, 8 * q:8 * q + 8, :],
                                            bank[1 + q][0:2 * TOK, :].rearrange("p (a b) -> p a b", a=8))
            ins.then_inc(ev("tok_ready"), 1)
            dve.wait_ge(ev("tok_ready"), 1)

            weights(dve, ch)

            def norm1(g):
                w = ln_slice(g)
                if g:
                    dve.wait_ge(ev(f"gathered{g - 1}"), 256)
                ch.step(nc.vector.tensor_reduce(w["s"], w["h"], AX.X, ALU.add))
                ch.step(nc.vector.tensor_scalar(w["m"], w["s"], 1.0 / D, None, ALU.mult))
                nc.vector.tensor_tensor(w["hn"], w["h"], w["m"].unsqueeze(2).to_broadcast(w["shape"]),
                                        ALU.subtract).then_inc(ev("ln_centred"), 1)
                dve.wait_ge(ev("ln_sq"), g + 1)
                nc.vector.tensor_reduce(w["v"], w["sq"], AX.X, ALU.add).then_inc(ev("ln_var"), 1)
                dve.wait_ge(ev("ln_std"), g + 1)
                ch.step(nc.vector.reciprocal(w["r"], w["d"]))
                nc.vector.tensor_tensor(w["hn"], w["hn"], w["r"].unsqueeze(2).to_broadcast(w["shape"]),
                                        ALU.mult).then_inc(ev("hn_ready"), 1)

            def first(s, u):
                p1 = 1 - u
                if within(s, 0, PAIRS):
                    dve.wait_ge(ev("hs_mm"), s + 1)
                    need(dve, ev("qk_mm"), s - 1)
                    need(dve, ev("hn_t_ready"), s - 1)
                    nc.vector.tensor_copy(hs[u][:, 0:TXT], bank[u][:, 0:TXT])
                    for b in range(2):
                        ins = nc.vector.tensor_copy(hs[u][b * D:b * D + D, TXT:N],
                                                    bank[u][b * D:b * D + D, TXT + b * TOK:TXT + b * TOK + TOK])
                    ins.then_inc(ev("hs_ready"), 1)
                if within(s - 1, 0, PAIRS):
                    dve.wait_ge(ev("qk_mm"), s)
                    need(dve, ev("gram_mm"), s - 2)
                    nc.vector.tensor_tensor(qkn[p1], bank[2 + p1][:, 0:2 * P].rearrange("p (a b) -> p a b", a=2),
                                            b_qk_rows[:, :].unsqueeze(1).to_broadcast([P, 2, P]), ALU.add)
                    nc.vector.tensor_tensor(qkt[p1], bank[4 + p1][0:TOK, 0:2 * P].rearrange("p (a b) -> p a b", a=2),
                                            b_qk_rows[0:TOK, :].unsqueeze(1).to_broadcast([TOK, 2, P]),
                                            ALU.add).then_inc(ev("qk_ready"), 1)
                if within(s - 2, 0, PAIRS):
                    dve.wait_ge(ev("gram_mm"), s - 1)
                    shape = [P, 2, H, HD]
                    nc.vector.tensor_tensor(gm[u], bank[6 + u][:, 0:P].rearrange("p (a g b) -> p a g b", a=2, g=H),
                                            head_of[:, :].unsqueeze(1).unsqueeze(3).to_broadcast(shape),
                                            ALU.mult).then_inc(ev("gm_ready"), 1)
                    dve.wait_ge(ev("gm_ready"), s - 1)
                    for x in range(2):
                        half = slice(x * D, x * D + D)
                        ins = nc.vector.tensor_reduce(
                            gall[half, :, x, :, bass.ds(s - 2, 1)].rearrange("p a b c -> p b (a c)"),
                            gm[u][half].rearrange("p a g b -> p a b g"), AX.X, ALU.add)
                    ins.then_inc(ev("gall_ready"), 1)
            nc.vector.memset(gall, 0.0)
            nc.vector.memset(top, 0.0)
            norm1(0)
            for g in range(4):
                norm1(g + 1)
                slots(dve, 8 * g, max(8 * g, 4), 8 * g + 8, PAIRS + 2 if g == 3 else 8 * g + 8, 2, first)

            dve.wait_ge(ev("hn_t_ready"), PAIRS)
            for b in range(2):
                half = slice(b * D, b * D + D)
                nc.vector.tensor_copy(top[half, 0:TOK, b, :], hn_t[half, :, TXT:N].rearrange("p t n -> p n t"))
                ins = nc.vector.tensor_copy(top[half, TOK:QB, b, :], hn_t[half, :, 0:QB - TOK].rearrange("p t n -> p n t"))
            ins.then_inc(ev("top_ready"), 1)
            dve.wait_ge(ev("rows_zero"), 1)
            copy_keys(dve, 0, 0)
            factorise(dve)
            nc.vector.memset(rt_logit, 0.0).then_inc(ev("rt_zero"), 1)
            dve.wait_ge(ev("rt_zero"), 1)
            slots(dve, -1, 5, PAIRS - 1, PAIRS + 3, 2, lambda s, u: attention_dve(dve, s, u))
            split_weights(dve)
            slots(dve, -1, 3, PAIRS - 1, PAIRS + 1, 2, lambda s, u: combine(dve, s, u))

        @block.tensor
        def _(pe):
            mm = nc.tensor.matmul
            pe.wait_ge(ev("ident_ready"), 1)

            def spread(s, u):
                pe.wait_ge(ev("ids_picked"), 2 * s + u + 1)
                if not isinstance(s, int) or 2 * s + u > 0:
                    pe.wait_ge(ev("ids_copied"), 2 * s + u)
                for i, (lo, hi) in enumerate(ID_PARTS):
                    ins = mm(bank[i][:, 0:hi - lo], ones16[:, :], ids_one[u][:, lo:hi], start=True, stop=True)
                ins.then_inc(ev("ids_bc"), 1)

            spread(0, 0)
            spread(0, 1)
            pe.wait_ge(ev("comp_ready"), 1)
            for v in range(2):
                pe.transpose(bank[5][:, v * P:v * P + P], comp_d[:, v, :, :].rearrange("p c d -> p (c d)"), ident[:, :])
            pe.transpose(bank[5][0:D, 256:256 + OPS], op_raw, ident[0:OPS, 0:OPS]).then_inc(ev("comp_turned"), 1)
            pe.wait_ge(ev("comp_copied"), 1)
            for side in range(2):
                half = slice(side * D, side * D + D)
                for v in range(2):
                    mm(bank[4 + 2 * side][:, v * D:v * D + D], comp_t[half, v, :], w_lr[half, :], start=True, stop=True)
            mm(bank[7][0:OPS, 0:D], op_t, w_op, start=True, stop=False)
            mm(bank[7][0:OPS, 0:D], ones_row[:, 0:OPS], bc_row, start=False, stop=True).then_inc(ev("tables"), 1)
            pe.wait_ge(ev("tables_split"), 1)

            def op_terms(o, hot, rows):
                for piece in range(3):
                    mm(o, hot, tab_op[0:rows, piece, :], start=piece == 0, stop=False)

            def level0(s, u):
                pe.wait_ge(ev("hot"), 2 * s + u + 1)
                if u == 0:
                    need(pe, ev("normed0"), s)
                for k in range(4):
                    o = LV[0][:, 4 * u + k, :]
                    op_terms(o, op_hot[:, u, k * P:k * P + P], OPS)
                    for side in range(2):
                        for v in range(2):
                            for piece in range(3):
                                leaf = 2 * k + side
                                ins = mm(o, leaf_hot[:, u, v, leaf * P:leaf * P + P], tab[:, side, v, piece, :],
                                         start=False, stop=side == v == 1 and piece == 2)
                ins.then_inc(ev("level0" if u else "half0"), 1)

            def turn(level, s, dst):
                pe.wait_ge(ev(f"leveled{level}"), s + 1)
                if level == 0:
                    need(pe, ev("kids1_copied"), s - 1)
                else:
                    pe.wait_ge(ev("kids0_copied"), min(s + 2, TS) if isinstance(s, int) else s + 2)
                n = 4 >> level
                src = lv_g[level].rearrange("p (a b) d -> p a (b d)", b=2)
                for i in range(n):
                    ins = pe.transpose(dst[:, i * P:i * P + P], src[:, i, :], ident[:, :])
                ins.then_inc(ev(f"kids{level}"), 1)

            def upper(level, s, kids):
                pe.wait_ge(ev(f"kids{level - 1}_copied"), s + 1)
                need(pe, ev(f"normed{level}"), s)
                nodes = 4 >> level
                for u in range(2):
                    for k in range(nodes):
                        o = LV[level][:, nodes * u + k, :]
                        k3 = (0 if level == 1 else 2) + k
                        op_terms(o, up_hot[:, bass.ds(2 * (s % 4) + u, 1), k3 * P:k3 * P + P].rearrange(
                            "p a b -> p (a b)"), P)
                        ins = mm(o, kids[:, nodes * u + k, :], w_lr, start=False, stop=True)
                ins.then_inc(ev(f"level{level}"), 1)

            def tree(s, _):
                if within(s + 1, 0, TS):
                    spread(s + 1, 0)
                if within(s, 0, TS):
                    level0(s, 0)
                if within(s - 1, 0, TS):
                    turn(0, s - 1, bank[5][:, :])
                if within(s + 1, 0, TS):
                    spread(s + 1, 1)
                if within(s - 2, 0, TS):
                    turn(1, s - 2, bank[5][:, 0:256])
                if within(s, 0, TS):
                    level0(s, 1)
                if within(s - 1, 0, TS):
                    upper(1, s - 1, kids1)
                if within(s - 2, 0, TS):
                    upper(2, s - 2, kids2)
            slots(pe, 0, 3, TS - 1, TS + 2, 1, tree)

            pe.wait_ge(ev("tok_loaded"), 96)
            pe.wait_ge(ev("zeros_ready"), 1)
            steps = (PW + 1) // 2
            for b in range(2):
                for c in range(steps):
                    last = c == steps - 1
                    rows = slice(0, PH if last else P)
                    ins = mm(bank[0][b * D:b * D + D, 0:PAIRS * TOK], wt[rows, c, :],
                             xs[rows, b:B:2, 2 * c:2 * c + SW * (TOK - 1) + 1:SW], start=c == 0, stop=last)
            ins.then_inc(ev("tok_mm"), 1)
            pe.wait_ge(ev("tok_split"), 1)
            for t in range(PAIRS):
                ins = mm(bank[1 + t // 8][0:2 * TOK, (t % 8) * D:(t % 8) * D + D],
                         tok_m[:, t, :, :].rearrange("p a b -> p (a b)"), ident2[:, :], start=True, stop=True)
                if t % 8 == 7:
                    ins.then_inc(ev("tok_rows"), 1)

            pe.wait_ge(ev("weights_loaded"), 16 * WLOADS)
            for i in range(4):
                ins = pe.transpose(bank[5][:, i * D:i * D + D], wn[:, i, :, :].rearrange("p a b -> p (a b)"), ident[0:D, 0:D])
            ins.then_inc(ev("w_turned"), 1)
            pe.wait_ge(ev("conv_ready"), 1)
            mm(bank[6][:, 0:H], pick_sq[:, :], conv_a[:, :], start=True, stop=True)
            mm(bank[6][0:D, H:2 * H], pick_lin[:, :], conv_a[:, :], start=True, stop=True)
            mm(bank[6][:, 16:17], conv_x[:, :], bn_inv[:, 3:4], start=True, stop=False)
            mm(bank[6][:, 16:17], cb_x[:, :], ones_col[0:1, :], start=False, stop=True).then_inc(ev("conv_mm"), 1)
            pe.wait_ge(ev("weights_ready"), 1)

            def first(s, u):
                p1 = 1 - u
                if within(s, 0, PAIRS):
                    pe.wait_ge(ev("staged"), s + 1)
                    need(pe, ev("hs_ready"), s - 1)
                    pe.transpose(bank[u][:, 0:TXT], st_txt[u].rearrange("p a b -> p (a b)"), ident[:, :])
                    pe.transpose(bank[u][:, TXT:TXT + 2 * TOK], st_tok[u].rearrange("p a b -> p (a b)"),
                                 ident[0:2 * TOK, 0:2 * TOK]).then_inc(ev("hs_mm"), 1)
                if within(s - 1, 0, PAIRS):
                    pe.wait_ge(ev("hs_ready"), s)
                    need(pe, ev("qk_ready"), s - 2)
                    w = wqk_pair[:, :, :].rearrange("p a b -> p (a b)")
                    mm(bank[2 + p1][:, 0:2 * P], hs[p1][:, 0:TXT], w, start=True, stop=True)
                    mm(bank[4 + p1][0:TOK, 0:2 * P], hs[p1][:, TXT:N], w, start=True, stop=True).then_inc(ev("qk_mm"), 1)
                if within(s - 2, 0, PAIRS):
                    pe.wait_ge(ev("qk_ready"), s - 1)
                    need(pe, ev("gm_ready"), s - 3)
                    for b in range(2):
                        for src in (qkn, qkt):
                            for x in range(2):
                                half = slice(x * D, x * D + D)
                                ins = mm(bank[6 + u][half, b * D:b * D + D], src[u][:, b, half], src[u][:, b, half],
                                         start=src is qkn, stop=src is qkt)
                    ins.then_inc(ev("gram_mm"), 1)
            def keep_warm(n):
                for _ in range(n):
                    mm(bank[0][:, :], ident[:, :], w1_f[:, 0:2, :].rearrange("p a b -> p (a b)"), start=True, stop=True)
            for g in range(4):
                if g == 0:
                    pe.wait_ge(ev("hn_ready"), 1)
                keep_warm(10 if g else 6)
                slots(pe, 8 * g, max(8 * g, 4), 8 * g + 8, PAIRS + 2 if g == 3 else 8 * g + 8, 2, first)

            def queries_keys(s, t1):
                need(pe, ev("q2_ready"), t1)
                need(pe, ev("vt_copied"), NVT * s)
                for o, w, done in ((bank[6], wq_dup, "q_mm"), (bank[5], wk_dup, "k_mm")):
                    for b in range(2):
                        ins = mm(o[:, b * N:b * N + N], w[:, b, :],
                                 hn_t[:, bass.ds(t1, 1), :].rearrange("p a b -> p (a b)"), start=True, stop=True)
                    ins.then_inc(ev(done), 1)

            pe.wait_ge(ev("gall_ready"), PAIRS)
            pe.wait_ge(ev("hn_t_ready"), 1)
            queries_keys(-1, 0)
            pe.wait_ge(ev("top_ready"), 1)
            for c in range(HD):
                mm(bank[0][:, c * D:c * D + D], gall[:, c].rearrange("p a b c -> p (a b c)"), ident2[:, :],
                   start=True, stop=True)
            for r in range(QB):
                for x in range(2):
                    ins = mm(bank[1][x * D:x * D + D, r * D:r * D + D], top[:, r].rearrange("p a b -> p (a b)"),
                             wqk_top[:, x, :], start=True, stop=True)
            ins.then_inc(ev("qr_mm"), 1)
            pe.wait_ge(ev("mx_done"), 1)
            for i in range(HD):
                ins = pe.transpose(bank[2 + i // 4][:, (i % 4) * P:(i % 4) * P + P],
                                   mx[:, i].rearrange("p a b c -> p (a b c)"), ident[:, :])
            ins.then_inc(ev("bases_mm"), 1)
            pe.wait_ge(ev("bases_ready"), 4)

            def attention(s, u):
                t1, p1 = s + 1, 1 - u
                prep = within(t1, 0, PAIRS)
                a, b1, b2 = within(s, 0, PAIRS), within(s - 1, 0, PAIRS), within(s - 2, 0, PAIRS)

                def dots(j):
                    if j == 0:
                        pe.wait_ge(ev("k_diag"), 16 * G * (s + 1))
                        pe.wait_ge(ev("q2_ready"), s + 1)
                    for b in range(2):
                        need(pe, ev("sq_done"), 2 * NG * s + 2 * j + b - 1)
                        keys = kbd[u][:, b].rearrange("p g m -> p (g m)")
                        for i, tile in enumerate(GROUPS[j]):
                            ins = mm(bank[b][:, i * N:i * N + N], keys[:, tile:tile + TILES * (P - 1) + 1:TILES],
                                     qq[u][:, b, :], start=True, stop=True)
                        ins.then_inc(ev("dg_done"), 1)

                def mixed(j):
                    pe.wait_ge(ev("sq_done"), 2 * NG * s + 2 * j + 2)
                    need(pe, ev("scores_out"), NG * s + j - 1)
                    if j == 0:
                        pe.wait_ge(ev("lin_ready"), s + 1)
                    n = len(GROUPS[j]) * N
                    for b in range(2):
                        mm(bank[2 + j % 2][b * D:b * D + D, 0:n], mix[:, :], sq[b][j % 2][:, 0:n],
                           start=True, stop=False)
                    for i, tile in enumerate(GROUPS[j]):
                        cols = slice(i * N, i * N + N)
                        for b in range(2):
                            keys = linb[u][:, b].rearrange("p o m -> p (o m)")
                            ins = mm(bank[2 + j % 2][b * D:b * D + D, cols],
                                     keys[:, tile:tile + TILES * (D - 1) + 1:TILES], qq[u][:, b, :],
                                     start=False, stop=i == len(GROUPS[j]) - 1)
                    ins.then_inc(ev("lg_done"), 1)

                def turn_values(r):
                    if r == 0:
                        pe.wait_ge(ev("v_diag"), 16 * G * (s + 1))
                    if r == 1 and prep:
                        pe.wait_ge(ev("q2_ready"), t1 + 1)
                    need(pe, ev("vt_copied"), NVT * s + r - 1)
                    flat = vbt.rearrange("p g m -> p (g m)")
                    for i, tile in enumerate(VTS[r]):
                        ins = pe.transpose(bank[5 + r % 2][:, i * P:i * P + P], flat[:, tile:tile + TILES * (P - 1) + 1:TILES],
                                           ident[:, :])
                    ins.then_inc(ev("vt_done"), 1)

                for j in range(NG):
                    if a:
                        dots(j)
                        if j:
                            mixed(j - 1)
                    if j == 0 and prep and not (isinstance(s, int) and s == -1):
                        queries_keys(s, t1)
                    if j == 0 and b2:
                        pe.wait_ge(ev("ot_ready"), s - 1)
                        need(pe, ev("router_out"), s - 2)
                        mm(bank[7][:, 0:P], ot[:, 0:TXT], wp_pair[:, :], start=True, stop=False)
                        mm(bank[7][:, 0:P], ones_row[:, :], bp_row[:, :, :].rearrange("p a b -> p (a b)"), start=False, stop=True)
                        mm(bank[7][0:2 * TOK, P:P + D], ot5.rearrange("p a b -> p (a b)"), wp_both[:, :], start=True, stop=False)
                        mm(bank[7][0:2 * TOK, P:P + D], ones_row[:, 0:2 * TOK], bp_row[:, 0, :], start=False,
                           stop=True).then_inc(ev("pr_done"), 1)
                    if j == 1 and prep:
                        pe.wait_ge(ev("q_copied"), t1 + 1)
                        mm(bank[6][:, 0:N], wv_pair[:, :], hn_t[:, bass.ds(t1, 1), :].rearrange("p a b -> p (a b)"),
                           start=True, stop=True).then_inc(ev("v_mm"), 1)
                        pe.wait_ge(ev("k_copied"), t1 + 1)
                        pe.wait_ge(ev("mq_ready"), t1 + 1)
                        for b in range(2):
                            ins = mm(bank[5][:, b * D:b * D + D], mqx[p1][:, b].rearrange("p a b c -> p (a b c)"),
                                     mkx[p1].rearrange("p a b -> p (a b)"), start=True, stop=True)
                        ins.then_inc(ev("p_mm"), 1)
                    if j == 1 and b1:
                        pe.wait_ge(ev("mx_ready"), s)
                        need(pe, ev("h_added"), s - 1)
                        pe.transpose(bank[7][:, 0:P], mxv[:, 0:TXT], ident[:, :])
                        pe.transpose(bank[7][0:TOK, P:2 * P], mxv[:, TXT:N], ident[:, :]).then_inc(ev("t1_done"), 1)
                    if j == 2 and b1:
                        pe.wait_ge(ev("mn_ready"), s)
                        pe.transpose(bank[7][:, 0:TXT], mnx.rearrange("p a b -> p (a b)"), ident[:, :])
                        pe.transpose(bank[7][:, TXT:N], mnx5.rearrange("p a b -> p (a b)"),
                                     ident[0:TOK, 0:TOK]).then_inc(ev("t2_done"), 1)
                    if j == 2 and prep:
                        pe.wait_ge(ev("p_copied"), t1 + 1)
                        pe.wait_ge(ev("v_copied"), t1 + 1)
                        for b in range(2):
                            ins = mm(bank[6][D:P, b * N:b * N + N], pm[p1][:, b, :], qq[p1][:, b, :],
                                     start=True, stop=True)
                        ins.then_inc(ev("q2_mm"), 1)
                    if j == 3 and b2:
                        pe.wait_ge(ev("hn2_rows"), s - 1)
                        pe.wait_ge(ev("sub_done"), min(s, PAIRS) if isinstance(s, int) else s)
                        pe.transpose(bank[7][:, 0:TXT], hn2.rearrange("p a b -> p (a b)"), ident[:, :])
                        pe.transpose(bank[7][:, TXT:TXT + 2 * TOK], hn2k.rearrange("p a b -> p (a b)"),
                                     ident[0:2 * TOK, 0:2 * TOK]).then_inc(ev("t4a_done"), 1)
                    if j == 3 and a:
                        turn_values(0)
                        turn_values(1)
                    if j == 4 and b2:
                        pe.wait_ge(ev("hs2_ready"), s - 1)
                        mm(bank[7][:, 0:2 * EXPERTS], hs2[u][:, 0:TXT], wr_pair[:, :, :].rearrange("p a b -> p (a b)"),
                           start=True, stop=True)
                        mm(bank[7][0:2 * TOK, 2 * EXPERTS:3 * EXPERTS], tk10[u].rearrange("p a b -> p (a b)"),
                           wr_both[:, :], start=True, stop=True).then_inc(ev("t4b_done"), 1)
                    if j == 4 and a:
                        turn_values(2)
                        turn_values(3)
                    if j == 5 and a:
                        turn_values(4)
                if b1:
                    pe.wait_ge(ev("exp_done"), s)
                    need(pe, ev("ot_ready"), s - 1)
                    for tile in range(TILES):
                        mm(bank[4][:, 0:N], vbd[p1][:, tile, :], ll[p1][:, tile, :], start=tile == 0,
                           stop=tile == TILES - 1)
                    pe.wait_ge(ev("es_ready"), s)
                    mm(bank[4][:, N:2 * N], group_ones[:, :], es, start=True, stop=True).then_inc(ev("av_done"), 1)
                if a:
                    mixed(NG - 1)
            slots(pe, -1, 5, PAIRS - 1, PAIRS + 2, 2, attention)

            pe.wait_ge(ev("hn2_ready"), PAIRS)
            pe.wait_ge(ev("router_out"), PAIRS)
            pe.wait_ge(ev("weights_split"), 1)
            pe.wait_ge(ev("w1_pieces"), 1)

            def experts(s, u):
                t1, p1 = s + 1, 1 - u

                def up(c):
                    if c == 0:
                        pe.wait_ge(ev("x_piece"), 4 * s + 4)
                    need(pe, ev("gelu_done"), CH * s + c - 2)
                    for k, x in enumerate((x12, x12, x13)):
                        ins = mm(bank[c % 3][:, 0:2 * N], w1_split[:, k, c // 2, (c % 2) * P:(c % 2) * P + P],
                                 x[u], start=k == 0, stop=k == 2)
                    ins.then_inc(ev("w1_done"), 1)

                def masks(e):
                    if e == 0:
                        pe.wait_ge(ev("mt_ready"), s + 1)
                    need(pe, ev("weighted"), EXPERTS * s + e - 1)
                    mm(bank[4 + 2 * (e % 2)][:, 0:2 * N], sel_e[:, e, :], mt[u].rearrange("p a b -> p (a b)"),
                       start=True, stop=True).then_inc(ev("mask_mm"), 1)

                def down(e):
                    if e < EXPERTS:
                        pe.wait_ge(ev("weighted"), EXPERTS * s + e + 1)
                    else:
                        pe.wait_ge(ev("gelu_done"), CH * s + CH)
                    if e == 0:
                        need(pe, ev("y_copied"), s)
                    for c in range(2):
                        for b in range(2):
                            ins = mm(bank[5][b * D:b * D + D, 0:N], w2_s[:, e, c, :], hg[e % HG][:, c, b * N:b * N + N],
                                     start=e == 0 and c == 0, stop=e == EXPERTS and c == 1)
                        for k in range(3 if e == c == 0 else 0):
                            for b in range(2):
                                mm(bank[5][b * D:b * D + D, 0:N], b2_split[:, k, :], mt[u][:, b, :], start=False, stop=False)
                    ins.then_inc(ev("w2_done"), 1)
                    if e == EXPERTS:
                        mm(bank[5][:, 2 * N:2 * N + 1], ident[:, :], ones_col[:, :], start=True, stop=True).then_inc(ev("y_mm"), 1)

                for e in range(EXPERTS + 3):
                    if within(s, 0, PAIRS):
                        if e <= EXPERTS:
                            up(2 * e)
                            up(2 * e + 1)
                        if e < EXPERTS:
                            masks(e)
                    if e == 0 and within(s - 1, 0, PAIRS):
                        pe.wait_ge(ev("y_copied"), s)
                        pe.wait_ge(ev("mt_ready"), min(s + 1, PAIRS) if isinstance(s, int) else s + 1)
                        pe.transpose(bank[7][:, 0:P], yt_sb[:, 0:TXT], ident[:, :])
                        mm(bank[7][0:2 * TOK, P:P + D], yk.rearrange("p a b -> p (a b)"), ident2[:, :],
                           start=True, stop=True).then_inc(ev("y_turned"), 1)
                    if e == 3 and within(t1, 0, PAIRS):
                        pe.wait_ge(ev("w_staged"), t1 + 1)
                        need(pe, ev("y_out"), t1 - 1)
                        pe.transpose(bank[7][:, 0:TXT], st_w[p1].rearrange("p a b -> p (a b)"), ident[:, :])
                        pe.transpose(bank[7][0:D, TXT:TXT + 2 * TOK], st_wk[p1].rearrange("p a b -> p (a b)"),
                                     ident[0:2 * TOK, 0:2 * TOK]).then_inc(ev("w_turned2"), 1)
                        need(pe, ev("x_piece"), 4 * t1)
                        for b in range(2):
                            ins = mm(bank[3][:, b * N:b * N + N], dup[:, b, :],
                                     hn_t[:, bass.ds(t1, 1), :].rearrange("p a b -> p (a b)"), start=True, stop=True)
                        ins.then_inc(ev("x_mm"), 1)
                    if within(s, 0, PAIRS) and e >= 2:
                        down(e - 2)
            slots(pe, -1, 3, PAIRS - 1, PAIRS + 1, 2, experts)


RT_STEPS = 19
WLOADS = 2 * 11 + 1 + 2 * 4 + 8 + 1 + 4 + 3 + 1
NVT = -(-TILES // 4)
VTS = [range(r, min(r + 4, TILES)) for r in range(0, TILES, 4)]
ID_PARTS = ((0, 512), (512, 1024), (1024, 1024 + 448), (1024 + 448, LEAFC + OPC))


_OUTS = [((B, N, D), "float32")]
_PREFIXES = ("L0_tok_", "L0_txt_", "L0_attn_", "L0_ffn_")


def _short(name):
    for p in _PREFIXES[1:]:
        if name.startswith(p):
            return name[len(p):]
    return name.replace("L0_", "")


def kernel(**inputs):
    import numpy as _np
    import concourse.bacc as _bacc
    from concourse import mybir as _mybir
    from concourse.bass_utils import run_bass_kernel_spmd as _run

    nc = _bacc.Bacc("TRN2", target_bir_lowering=False, num_devices=1)
    arrays, aps = {}, {}
    for name, value in inputs.items():
        v = _np.ascontiguousarray(value)
        if v.ndim == 0:
            v = v.reshape(1)
        arrays[f"in_{name}_dram"] = v
        aps[_short(name)] = nc.dram_tensor(f"in_{name}_dram", v.shape, _mybir.dt.from_np(v.dtype),
                                           kind="ExternalInput").ap()
    out = nc.dram_tensor("out_0_dram", _OUTS[0][0], F32, kind="ExternalOutput").ap()
    build(nc, aps, out)
    r = _run(nc, [arrays], core_ids=[0])
    return r.results[0]["out_0_dram"]
```
